# Optimizing a Trainium2 kernel written in Bass

```python
import numpy as np
import jax
import jax.numpy as jnp

def _softmax(x, axis=-1):
    return jax.nn.softmax(x, axis=axis)

def _gelu(x):
    return jax.nn.gelu(x, approximate=True)

def _silu(x):
    return jax.nn.silu(x)

def _sigmoid(x):
    return jax.nn.sigmoid(x)

def _layernorm(x, axis=-1, eps=1e-05):
    m = jnp.mean(x, axis=axis, keepdims=True)
    v = jnp.var(x, axis=axis, keepdims=True)
    return (x - m) / jnp.sqrt(v + eps)

def _scatter_add(tgt, idx, src, axis=0):
    return tgt.at[idx].add(src)

def _segment_sum(src, seg, n):
    return jax.ops.segment_sum(src, seg, n)
kernel_name = 'mk_perceiver_d2_seqx_r4_950e23'

def setup_inputs(seed: int=0):
    np.random.seed(seed)
    _w = jnp.asarray

    def _rec_inputs():
        import jax
        import jax.numpy as jnp
        _rk = jax.random.key(seed)
        x = 7.22e-05 + 1 * jax.random.normal(jax.random.fold_in(_rk, 1), (8, 64, 512), jnp.float32)
        _lenS = 64 - jax.random.randint(jax.random.fold_in(_rk, 7), (8,), 0, max(1, 64 // 4) + 1, jnp.int32)
        _lenS2 = 1601 - jax.random.randint(jax.random.fold_in(_rk, 8), (8,), 0, max(1, 1601 // 4) + 1, jnp.int32)
        _ctx_512P = jax.random.normal(jax.random.fold_in(_rk, 11), (8, 16, 128), jnp.float32)
        _ctx_512c = jax.random.dirichlet(jax.random.fold_in(_rk, 511), 0.3 * jnp.ones((16,), jnp.float32), (8, 1601))
        _ctx_512t = jnp.einsum('bsk,bkd->bsd', _ctx_512c, _ctx_512P)
        _ctx_512t = _ctx_512t * jax.lax.rsqrt(jnp.mean(jnp.square(_ctx_512t)) + 1e-12) * 0.953939
        ctx_512 = -0.000514642 + 1.00011 * (_ctx_512t + 0.3 * jax.random.normal(jax.random.fold_in(_rk, 611), (8, 1601, 128), jnp.float32))
        return (x, ctx_512)
    x, ctx_512 = _rec_inputs()

    def _L0_xattn_setup():
        import jax, jax.numpy as jnp
        import numpy as np
        B, S, H, NH, L = (2, 512, 512, 16, 128)
        HD = H // NH
        key = jax.random.key(seed)
        k1, k2, k3, k4, k5 = jax.random.split(key, 5)
        scale = 0.02
        return {'q': jax.random.normal(k1, (B, S, H), dtype=jnp.float32), 'latent_kv': jax.random.normal(k2, (B, S, L), dtype=jnp.float32), 'Wq': jax.random.normal(k3, (H, H), dtype=jnp.float32) * scale, 'Wkv_expand': jax.random.normal(k4, (2 * H, L), dtype=jnp.float32) * scale, 'Wout': jax.random.normal(k5, (H, H), dtype=jnp.float32) * scale}
    _L0_xattn_all = _L0_xattn_setup()
    _L0_xattn_in = {k: v for k, v in _L0_xattn_all.items() if k in ('Wq', 'Wkv_expand', 'Wout')}
    del _L0_xattn_all

    def _L0_attn_setup():
        import jax, jax.numpy as jnp
        import numpy as np
        B, L, D, H = (2, 512, 512, 16)
        HD = D // H

        def rope(x, seq_len, theta=10000.0):
            d = x.shape[-1]
            freqs = 1.0 / theta ** (jnp.arange(0, d, 2, dtype=x.dtype) / d)
            t = jnp.arange(seq_len, dtype=x.dtype)
            f = jnp.outer(t, freqs)
            sin = jnp.repeat(jnp.sin(f), 2, axis=-1)
            cos = jnp.repeat(jnp.cos(f), 2, axis=-1)
            x1, x2 = (x[..., ::2], x[..., 1::2])
            x_rot = jnp.stack([-x2, x1], axis=-1).reshape(x.shape)
            return x * cos + x_rot * sin
        key = jax.random.key(seed)
        k1, k2, k3 = jax.random.split(key, 3)
        x = jax.random.normal(k1, (B, L, D), dtype=jnp.float32)
        w_qkv = jax.random.normal(k2, (D, 3 * D), dtype=jnp.float32) * (1.0 / np.sqrt(D))
        w_proj = jax.random.normal(k3, (D, D), dtype=jnp.float32) * (1.0 / np.sqrt(D))
        return {'x': x, 'w_qkv': w_qkv, 'w_proj': w_proj}
    _L0_attn_all = _L0_attn_setup()
    _L0_attn_in = {k: v for k, v in _L0_attn_all.items() if k in ('w_qkv', 'w_proj')}
    del _L0_attn_all

    def _L0_ffn_setup():
        import jax, jax.numpy as jnp
        import numpy as np
        H = 512
        I = 2048
        NE = 8
        S = 2
        N = NE - S
        K = N
        E = I // NE
        C = 2
        RESIDUAL = True
        B, L = (2, 512)

        def _swiglu(h, W, b):
            return jax.nn.silu(h @ W + b) * h
        key = jax.random.key(seed)
        ks = jax.random.split(key, 16)
        s = 0.02
        inp = {'x': jax.random.normal(ks[0], (B, L, H), dtype=jnp.float32), 'Wg': jax.random.normal(ks[1], (C, H, NE)) * s, 'bg': jnp.zeros((C, NE)), 'Wup': jax.random.normal(ks[2], (N, H, E)) * s, 'bup': jnp.zeros((N, E)), 'Wsw': jax.random.normal(ks[3], (N, E, E)) * s, 'bsw': jnp.zeros((N, E)), 'Wdn': jax.random.normal(ks[4], (N, E, H)) * s, 'bdn': jnp.zeros((N, H)), 'Wsu': jax.random.normal(ks[5], (H, S * E)) * s, 'bsu': jnp.zeros((S * E,)), 'Wsa': jax.random.normal(ks[6], (E, E)) * s, 'bsa': jnp.zeros((E,)), 'Wsd': jax.random.normal(ks[7], (S * E, H)) * s, 'bsd': jnp.zeros((H,))}
        return inp
    _L0_ffn_all = _L0_ffn_setup()
    _L0_ffn_in = {k: v for k, v in _L0_ffn_all.items() if k in ('Wg', 'bg', 'Wup', 'bup', 'Wsw', 'bsw', 'Wdn', 'bdn', 'Wsu', 'bsu', 'Wsa', 'bsa', 'Wsd', 'bsd')}
    del _L0_ffn_all

    def _L1_xattn_setup():
        import jax, jax.numpy as jnp
        import numpy as np
        B, S, L = (2, 256, 256)
        DIM_Q, H, K, D_C, D_CQ, R = (512, 16, 128, 128, 384, 64)

        def _rope_tables(length, dim):
            inv = 1.0 / 10000.0 ** (jnp.arange(0, dim, 2, dtype=jnp.float32) / dim)
            f = jnp.arange(length, dtype=jnp.float32)[:, None] * inv[None, :]
            sin = jnp.repeat(jnp.sin(f), 2, axis=-1)
            cos = jnp.repeat(jnp.cos(f), 2, axis=-1)
            return (sin, cos)

        def _rotate_half(x):
            half = x.shape[-1] // 2
            return jnp.concatenate([-x[..., half:], x[..., :half]], axis=-1)

        def _apply_rope(x, sin, cos):
            return x * cos + _rotate_half(x) * sin
        key = jax.random.key(seed)
        ks = jax.random.split(key, 8)
        return {'hidden_q': jax.random.normal(ks[0], (B, S, DIM_Q), jnp.float32), 'kv_c': jax.random.normal(ks[1], (B, L, D_C), jnp.float32), 'Wq': jax.random.normal(ks[2], (H * K, DIM_Q), jnp.float32) / np.sqrt(DIM_Q).astype(np.float32), 'w_kc_q': jax.random.normal(ks[3], (H, K, D_CQ), jnp.float32) / np.sqrt(K).astype(np.float32), 'w_kc_kv': jax.random.normal(ks[4], (H, K, D_C), jnp.float32) / np.sqrt(K).astype(np.float32), 'W_qr': jax.random.normal(ks[5], (H, D_CQ, R), jnp.float32) / np.float32(np.sqrt(D_CQ) * np.sqrt(R)), 'W_kr': jax.random.normal(ks[6], (H, D_C, R), jnp.float32) / np.sqrt(D_C).astype(np.float32), 'Wo': jax.random.normal(ks[7], (DIM_Q, H * K), jnp.float32) / np.sqrt(H * K).astype(np.float32)}
    _L1_xattn_all = _L1_xattn_setup()
    _L1_xattn_in = {k: v for k, v in _L1_xattn_all.items() if k in ('Wq', 'w_kc_q', 'w_kc_kv', 'W_qr', 'W_kr', 'Wo')}
    del _L1_xattn_all

    def _L1_attn_setup():
        import jax, jax.numpy as jnp
        import numpy as np
        B_, L, D_MODEL = (2, 1024, 512)
        H, P, N, G, K = (32, 64, 128, 1, 4)
        EPS = 1e-05
        INTER = H * P
        CONV_DIM = INTER + 2 * G * N
        PROJ = INTER + CONV_DIM + H

        def _silu(x):
            return x * jax.nn.sigmoid(x)

        def _mamba2_mixer(hidden_states, W_in, conv_w, conv_b, dt_bias, A_log, D_param, norm_w, W_out):
            b, l, _ = hidden_states.shape
            proj = jnp.einsum('bld,pd->blp', hidden_states, W_in)
            gate = proj[..., :INTER]
            hBC = proj[..., INTER:INTER + CONV_DIM]
            dt = proj[..., INTER + CONV_DIM:]
            xc = jnp.transpose(hBC, (0, 2, 1))
            conv = jax.lax.conv_general_dilated(xc, conv_w[:, None, :], window_strides=(1,), padding=[(K - 1, 0)], dimension_numbers=('NCH', 'OIH', 'NCH'), feature_group_count=CONV_DIM)
            hBC = _silu(jnp.transpose(conv + conv_b[None, :, None], (0, 2, 1)))
            xs = hBC[..., :INTER].reshape(b, l, H, P)
            Bm = hBC[..., INTER:INTER + G * N].reshape(b, l, G, N)
            Cm = hBC[..., INTER + G * N:].reshape(b, l, G, N)
            Bh = jnp.repeat(Bm, H // G, axis=2)
            Ch = jnp.repeat(Cm, H // G, axis=2)
            dt = jax.nn.softplus(dt + dt_bias)
            A = -jnp.exp(A_log)
            dA = jnp.exp(dt * A)

            def step(h, inp):
                dA_t, dt_t, x_t, B_t, C_t = inp
                u = (dt_t[:, :, None] * x_t)[..., None] * B_t[:, :, None, :]
                h = dA_t[:, :, None, None] * h + u
                y = jnp.einsum('bhpn,bhn->bhp', h, C_t)
                return (h, y)
            tm = lambda a: jnp.moveaxis(a, 1, 0)
            h0 = jnp.zeros((b, H, P, N), hidden_states.dtype)
            _, ys = jax.lax.scan(step, h0, (tm(dA), tm(dt), tm(xs), tm(Bh), tm(Ch)))
            y = jnp.moveaxis(ys, 0, 1) + D_param[None, None, :, None] * xs
            y = y.reshape(b, l, INTER)
            g = y * _silu(gate)
            g = g * jax.lax.rsqrt(jnp.mean(g * g, axis=-1, keepdims=True) + EPS) * norm_w
            return jnp.einsum('bli,di->bld', g, W_out)
        key = jax.random.key(seed)
        ks = jax.random.split(key, 5)
        hidden_states = jax.random.normal(ks[0], (B_, L, D_MODEL), jnp.float32)
        W_in = jax.random.normal(ks[1], (PROJ, D_MODEL), jnp.float32) * 0.02
        conv_w = jax.random.normal(ks[2], (CONV_DIM, K), jnp.float32) * 0.1
        conv_b = jnp.zeros((CONV_DIM,), jnp.float32)
        dt_bias = jnp.ones((H,), jnp.float32)
        A_log = jnp.log(jnp.arange(1, H + 1, dtype=jnp.float32))
        D_param = jnp.ones((H,), jnp.float32)
        norm_w = jnp.ones((INTER,), jnp.float32)
        W_out = jax.random.normal(ks[3], (D_MODEL, INTER), jnp.float32) * 0.02
        return dict(hidden_states=hidden_states, W_in=W_in, conv_w=conv_w, conv_b=conv_b, dt_bias=dt_bias, A_log=A_log, D_param=D_param, norm_w=norm_w, W_out=W_out)
    _L1_attn_all = _L1_attn_setup()
    _L1_attn_in = {k: v for k, v in _L1_attn_all.items() if k in ('W_in', 'conv_w', 'conv_b', 'dt_bias', 'A_log', 'D_param', 'norm_w', 'W_out')}
    del _L1_attn_all

    def _L1_ffn_setup():
        import jax, jax.numpy as jnp
        import numpy as np
        H = 512
        FFP = 256
        E = 8
        K = 2
        R = 16
        LORA_SCALE = 32.0 / 16.0
        key = jax.random.key(seed)
        ks = jax.random.split(key, 7)
        s = 0.02
        x = jax.random.normal(ks[0], (4, 512, H), dtype=jnp.float32)
        gate_w = jax.random.normal(ks[1], (H, E), dtype=jnp.float32)
        Wg = jax.random.normal(ks[2], (E, H, FFP), dtype=jnp.float32) * s
        Wu = jax.random.normal(ks[3], (E, H, FFP), dtype=jnp.float32) * s
        Wd = jax.random.normal(ks[4], (E, FFP, H), dtype=jnp.float32) * s
        A = jax.random.normal(ks[5], (E, H, R), dtype=jnp.float32) * s
        B = jax.random.normal(ks[6], (E, R, H), dtype=jnp.float32) * s
        return {'x': x, 'gate_w': gate_w, 'Wg': Wg, 'Wu': Wu, 'Wd': Wd, 'A': A, 'B': B}
    _L1_ffn_all = _L1_ffn_setup()
    _L1_ffn_in = {k: v for k, v in _L1_ffn_all.items() if k in ('gate_w', 'Wg', 'Wu', 'Wd', 'A', 'B')}
    del _L1_ffn_all
    return {'x': x, 'ctx_512': ctx_512, 'L0_xattn_Wq': _L0_xattn_in['Wq'], 'L0_xattn_Wkv_expand': _L0_xattn_in['Wkv_expand'], 'L0_xattn_Wout': _L0_xattn_in['Wout'], 'L0_attn_w_qkv': _L0_attn_in['w_qkv'], 'L0_attn_w_proj': _L0_attn_in['w_proj'], 'L0_ffn_Wg': _L0_ffn_in['Wg'], 'L0_ffn_bg': _L0_ffn_in['bg'], 'L0_ffn_Wup': _L0_ffn_in['Wup'], 'L0_ffn_bup': _L0_ffn_in['bup'], 'L0_ffn_Wsw': _L0_ffn_in['Wsw'], 'L0_ffn_bsw': _L0_ffn_in['bsw'], 'L0_ffn_Wdn': _L0_ffn_in['Wdn'], 'L0_ffn_bdn': _L0_ffn_in['bdn'], 'L0_ffn_Wsu': _L0_ffn_in['Wsu'], 'L0_ffn_bsu': _L0_ffn_in['bsu'], 'L0_ffn_Wsa': _L0_ffn_in['Wsa'], 'L0_ffn_bsa': _L0_ffn_in['bsa'], 'L0_ffn_Wsd': _L0_ffn_in['Wsd'], 'L0_ffn_bsd': _L0_ffn_in['bsd'], 'L1_xattn_Wq': _L1_xattn_in['Wq'], 'L1_xattn_w_kc_q': _L1_xattn_in['w_kc_q'], 'L1_xattn_w_kc_kv': _L1_xattn_in['w_kc_kv'], 'L1_xattn_W_qr': _L1_xattn_in['W_qr'], 'L1_xattn_W_kr': _L1_xattn_in['W_kr'], 'L1_xattn_Wo': _L1_xattn_in['Wo'], 'L1_attn_W_in': _L1_attn_in['W_in'], 'L1_attn_conv_w': _L1_attn_in['conv_w'], 'L1_attn_conv_b': _L1_attn_in['conv_b'], 'L1_attn_dt_bias': _L1_attn_in['dt_bias'], 'L1_attn_A_log': _L1_attn_in['A_log'], 'L1_attn_D_param': _L1_attn_in['D_param'], 'L1_attn_norm_w': _L1_attn_in['norm_w'], 'L1_attn_W_out': _L1_attn_in['W_out'], 'L1_ffn_gate_w': _L1_ffn_in['gate_w'], 'L1_ffn_Wg': _L1_ffn_in['Wg'], 'L1_ffn_Wu': _L1_ffn_in['Wu'], 'L1_ffn_Wd': _L1_ffn_in['Wd'], 'L1_ffn_A': _L1_ffn_in['A'], 'L1_ffn_B': _L1_ffn_in['B']}

def reference(x, ctx_512, L0_xattn_Wq, L0_xattn_Wkv_expand, L0_xattn_Wout, L0_attn_w_qkv, L0_attn_w_proj, L0_ffn_Wg, L0_ffn_bg, L0_ffn_Wup, L0_ffn_bup, L0_ffn_Wsw, L0_ffn_bsw, L0_ffn_Wdn, L0_ffn_bdn, L0_ffn_Wsu, L0_ffn_bsu, L0_ffn_Wsa, L0_ffn_bsa, L0_ffn_Wsd, L0_ffn_bsd, L1_xattn_Wq, L1_xattn_w_kc_q, L1_xattn_w_kc_kv, L1_xattn_W_qr, L1_xattn_W_kr, L1_xattn_Wo, L1_attn_W_in, L1_attn_conv_w, L1_attn_conv_b, L1_attn_dt_bias, L1_attn_A_log, L1_attn_D_param, L1_attn_norm_w, L1_attn_W_out, L1_ffn_gate_w, L1_ffn_Wg, L1_ffn_Wu, L1_ffn_Wd, L1_ffn_A, L1_ffn_B):
    import jax
    import jax.numpy as jnp

    def _L0_xattn_ref(q, latent_kv, Wq, Wkv_expand, Wout):
        import jax, jax.numpy as jnp
        import numpy as np
        B, S, H, NH, L = (2, 512, 512, 16, 128)
        HD = H // NH
        b, sq, _ = q.shape
        sk = latent_kv.shape[1]
        qp = q @ Wq.T
        kv = latent_kv @ Wkv_expand.T
        k, v = jnp.split(kv, 2, axis=-1)
        qh = qp.reshape(b, sq, NH, HD).transpose(0, 2, 1, 3)
        kh = k.reshape(b, sk, NH, HD).transpose(0, 2, 1, 3)
        vh = v.reshape(b, sk, NH, HD).transpose(0, 2, 1, 3)
        inv_sqrt_d = 1.0 / jnp.sqrt(jnp.float32(HD))
        scores = jnp.einsum('bhqd,bhkd->bhqk', qh, kh) * inv_sqrt_d
        causal = jnp.tril(jnp.ones((sq, sk), dtype=bool))
        scores = jnp.where(causal, scores, jnp.finfo(scores.dtype).min)
        attn = jax.nn.softmax(scores, axis=-1)
        out = jnp.einsum('bhqk,bhkd->bhqd', attn, vh)
        out = out.transpose(0, 2, 1, 3).reshape(b, sq, H)
        return out @ Wout.T

    def _L0_attn_ref(x, w_qkv, w_proj):
        import jax, jax.numpy as jnp
        import numpy as np
        B, L, D, H = (2, 512, 512, 16)
        HD = D // H

        def rope(x, seq_len, theta=10000.0):
            d = x.shape[-1]
            freqs = 1.0 / theta ** (jnp.arange(0, d, 2, dtype=x.dtype) / d)
            t = jnp.arange(seq_len, dtype=x.dtype)
            f = jnp.outer(t, freqs)
            sin = jnp.repeat(jnp.sin(f), 2, axis=-1)
            cos = jnp.repeat(jnp.cos(f), 2, axis=-1)
            x1, x2 = (x[..., ::2], x[..., 1::2])
            x_rot = jnp.stack([-x2, x1], axis=-1).reshape(x.shape)
            return x * cos + x_rot * sin
        Bc, Lc, Dc = x.shape
        scale = 1.0 / np.sqrt(HD)
        qkv = (x @ w_qkv).reshape(Bc, Lc, 3, H, HD)
        q, k, v = (qkv[:, :, 0], qkv[:, :, 1], qkv[:, :, 2])
        q = rope(jnp.transpose(q, (0, 2, 1, 3)), Lc)
        k = rope(jnp.transpose(k, (0, 2, 1, 3)), Lc)
        v = jnp.transpose(v, (0, 2, 1, 3))
        att = jnp.einsum('bhqd,bhkd->bhqk', q, k) * scale
        att = jax.nn.softmax(att, axis=-1)
        out = jnp.einsum('bhqk,bhkd->bhqd', att, v)
        out = jnp.transpose(out, (0, 2, 1, 3)).reshape(Bc, Lc, Dc)
        return out @ w_proj

    def _L0_ffn_ref(x, Wg, bg, Wup, bup, Wsw, bsw, Wdn, bdn, Wsu, bsu, Wsa, bsa, Wsd, bsd):
        import jax, jax.numpy as jnp
        import numpy as np
        H = 512
        I = 2048
        NE = 8
        S = 2
        N = NE - S
        K = N
        E = I // NE
        C = 2
        RESIDUAL = True
        B, L = (2, 512)

        def _swiglu(h, W, b):
            return jax.nn.silu(h @ W + b) * h
        bsz, seq, _ = x.shape
        xt = x.reshape(-1, H)
        res = xt
        for j in range(C):
            gate = xt @ Wg[j] + bg[j]
            _, ids = jax.lax.top_k(gate, K)
            in_top = jax.nn.one_hot(ids, NE, dtype=gate.dtype).sum(-2) > 0
            w = jax.nn.softmax(jnp.where(in_top, gate, -jnp.inf), axis=-1)
            h = jnp.einsum('th,nhe->nte', xt, Wup) + bup[:, None, :]
            h = jax.nn.silu(jnp.einsum('nte,nef->ntf', h, Wsw) + bsw[:, None, :]) * h
            eo = jnp.einsum('nte,neh->nth', h, Wdn) + bdn[:, None, :]
            out = jnp.einsum('nth,tn->th', eo, w[:, :N])
            sh = (xt @ Wsu + bsu).reshape(-1, S, E)
            sh = _swiglu(sh, Wsa, bsa)
            out = out + sh.reshape(-1, S * E) @ Wsd + bsd
            xt = res + out if RESIDUAL else out
        return xt.reshape(bsz, seq, H)

    def _L1_xattn_ref(hidden_q, kv_c, Wq, w_kc_q, w_kc_kv, W_qr, W_kr, Wo):
        import jax, jax.numpy as jnp
        import numpy as np
        B, S, L = (2, 256, 256)
        DIM_Q, H, K, D_C, D_CQ, R = (512, 16, 128, 128, 384, 64)

        def _rope_tables(length, dim):
            inv = 1.0 / 10000.0 ** (jnp.arange(0, dim, 2, dtype=jnp.float32) / dim)
            f = jnp.arange(length, dtype=jnp.float32)[:, None] * inv[None, :]
            sin = jnp.repeat(jnp.sin(f), 2, axis=-1)
            cos = jnp.repeat(jnp.cos(f), 2, axis=-1)
            return (sin, cos)

        def _rotate_half(x):
            half = x.shape[-1] // 2
            return jnp.concatenate([-x[..., half:], x[..., :half]], axis=-1)

        def _apply_rope(x, sin, cos):
            return x * cos + _rotate_half(x) * sin
        Bv, Sv, _ = hidden_q.shape
        _, Lv, _ = kv_c.shape
        q_hk = (hidden_q @ Wq.T).reshape(Bv, Sv, H, K)
        q_big = jnp.einsum('bshk,hkq->bshq', q_hk, w_kc_q)
        sin_q, cos_q = _rope_tables(Sv, D_CQ)
        q_big = _apply_rope(q_big, sin_q[None, :, None, :], cos_q[None, :, None, :])
        sin_k, cos_k = _rope_tables(Lv, D_C)
        kv_r = _apply_rope(kv_c, sin_k[None], cos_k[None])
        q_r = jnp.einsum('bshq,hqr->bhsr', q_big, W_qr)
        k_r = jnp.einsum('bld,hdr->bhlr', kv_r, W_kr)
        scores = jnp.einsum('bhsr,bhlr->bhsl', q_r, k_r)
        attn = jax.nn.softmax(scores, axis=-1)
        ctx_c = jnp.einsum('bhsl,bld->bhsd', attn, kv_r)
        ctx_lat = jnp.einsum('bhsd,hkd->bhsk', ctx_c, w_kc_kv)
        ctx = ctx_lat.transpose(0, 2, 1, 3).reshape(Bv, Sv, H * K)
        return ctx @ Wo.T

    def _L1_attn_ref(hidden_states, W_in, conv_w, conv_b, dt_bias, A_log, D_param, norm_w, W_out):
        import jax, jax.numpy as jnp
        import numpy as np
        B_, L, D_MODEL = (2, 1024, 512)
        H, P, N, G, K = (32, 64, 128, 1, 4)
        EPS = 1e-05
        INTER = H * P
        CONV_DIM = INTER + 2 * G * N
        PROJ = INTER + CONV_DIM + H

        def _silu(x):
            return x * jax.nn.sigmoid(x)

        def _mamba2_mixer(hidden_states, W_in, conv_w, conv_b, dt_bias, A_log, D_param, norm_w, W_out):
            b, l, _ = hidden_states.shape
            proj = jnp.einsum('bld,pd->blp', hidden_states, W_in)
            gate = proj[..., :INTER]
            hBC = proj[..., INTER:INTER + CONV_DIM]
            dt = proj[..., INTER + CONV_DIM:]
            xc = jnp.transpose(hBC, (0, 2, 1))
            conv = jax.lax.conv_general_dilated(xc, conv_w[:, None, :], window_strides=(1,), padding=[(K - 1, 0)], dimension_numbers=('NCH', 'OIH', 'NCH'), feature_group_count=CONV_DIM)
            hBC = _silu(jnp.transpose(conv + conv_b[None, :, None], (0, 2, 1)))
            xs = hBC[..., :INTER].reshape(b, l, H, P)
            Bm = hBC[..., INTER:INTER + G * N].reshape(b, l, G, N)
            Cm = hBC[..., INTER + G * N:].reshape(b, l, G, N)
            Bh = jnp.repeat(Bm, H // G, axis=2)
            Ch = jnp.repeat(Cm, H // G, axis=2)
            dt = jax.nn.softplus(dt + dt_bias)
            A = -jnp.exp(A_log)
            dA = jnp.exp(dt * A)

            def step(h, inp):
                dA_t, dt_t, x_t, B_t, C_t = inp
                u = (dt_t[:, :, None] * x_t)[..., None] * B_t[:, :, None, :]
                h = dA_t[:, :, None, None] * h + u
                y = jnp.einsum('bhpn,bhn->bhp', h, C_t)
                return (h, y)
            tm = lambda a: jnp.moveaxis(a, 1, 0)
            h0 = jnp.zeros((b, H, P, N), hidden_states.dtype)
            _, ys = jax.lax.scan(step, h0, (tm(dA), tm(dt), tm(xs), tm(Bh), tm(Ch)))
            y = jnp.moveaxis(ys, 0, 1) + D_param[None, None, :, None] * xs
            y = y.reshape(b, l, INTER)
            g = y * _silu(gate)
            g = g * jax.lax.rsqrt(jnp.mean(g * g, axis=-1, keepdims=True) + EPS) * norm_w
            return jnp.einsum('bli,di->bld', g, W_out)
        return _mamba2_mixer(hidden_states, W_in, conv_w, conv_b, dt_bias, A_log, D_param, norm_w, W_out)

    def _L1_ffn_ref(x, gate_w, Wg, Wu, Wd, A, B):
        import jax, jax.numpy as jnp
        import numpy as np
        H = 512
        FFP = 256
        E = 8
        K = 2
        R = 16
        LORA_SCALE = 32.0 / 16.0
        b, s, h = x.shape
        xf = x.reshape(-1, h).astype(jnp.float32)
        logits = xf @ gate_w
        probs = jax.nn.softmax(logits, axis=-1)
        vals, idx = jax.lax.top_k(probs, K)
        w = vals / jnp.clip(vals.sum(axis=-1, keepdims=True), 1e-09)
        We = jnp.sum(jax.nn.one_hot(idx, E, dtype=w.dtype) * w[..., None], axis=1)
        out = jnp.zeros_like(xf)
        for e in range(E):
            mid = jax.nn.silu(xf @ Wg[e]) * (xf @ Wu[e])
            oe = mid @ Wd[e] + xf @ A[e] @ B[e] * LORA_SCALE
            out = out + We[:, e:e + 1] * oe
        return out.reshape(b, s, h)
    x = x + _L0_xattn_ref(_layernorm(x, axis=-1), ctx_512, L0_xattn_Wq, L0_xattn_Wkv_expand, L0_xattn_Wout)
    x = x + _L0_attn_ref(_layernorm(x, axis=-1), L0_attn_w_qkv, L0_attn_w_proj)
    x = x + _L0_ffn_ref(_layernorm(x, axis=-1), L0_ffn_Wg, L0_ffn_bg, L0_ffn_Wup, L0_ffn_bup, L0_ffn_Wsw, L0_ffn_bsw, L0_ffn_Wdn, L0_ffn_bdn, L0_ffn_Wsu, L0_ffn_bsu, L0_ffn_Wsa, L0_ffn_bsa, L0_ffn_Wsd, L0_ffn_bsd)
    x = x + _L1_xattn_ref(_layernorm(x, axis=-1), ctx_512, L1_xattn_Wq, L1_xattn_w_kc_q, L1_xattn_w_kc_kv, L1_xattn_W_qr, L1_xattn_W_kr, L1_xattn_Wo)
    x = x + _L1_attn_ref(_layernorm(x, axis=-1), L1_attn_W_in, L1_attn_conv_w, L1_attn_conv_b, L1_attn_dt_bias, L1_attn_A_log, L1_attn_D_param, L1_attn_norm_w, L1_attn_W_out)
    x = x + _L1_ffn_ref(_layernorm(x, axis=-1), L1_ffn_gate_w, L1_ffn_Wg, L1_ffn_Wu, L1_ffn_Wd, L1_ffn_A, L1_ffn_B)
    return x

_drawn_inputs = setup_inputs


def setup_inputs(seed=0):
    import zlib

    import numpy as np

    out = dict(_drawn_inputs(seed))
    spreads = {'L0_ffn_bg': (0.0, 0.1),
     'L0_ffn_bup': (0.0, 0.1),
     'L0_ffn_bsw': (0.0, 0.1),
     'L0_ffn_bdn': (0.0, 0.1),
     'L0_ffn_bsu': (0.0, 0.1),
     'L0_ffn_bsa': (0.0, 0.1),
     'L0_ffn_bsd': (0.0, 0.1),
     'L1_attn_conv_b': (0.0, 0.1),
     'L1_attn_dt_bias': (1.0, 0.2),
     'L1_attn_D_param': (1.0, 0.2),
     'L1_attn_norm_w': (1.0, 0.2)}
    factors = {}
    for name, (base, spread) in spreads.items():
        noise = np.random.default_rng([zlib.crc32(name.encode()), seed]).standard_normal(out[name].shape)
        drawn = base * np.exp(spread * noise) if base else spread * noise
        out[name] = jnp.asarray(drawn.astype(out[name].dtype))
    for name, factor in factors.items():
        out[name] = (out[name] * factor).astype(out[name].dtype)
    return out
```

```python
from contextlib import ExitStack

import numpy as np

import concourse.bass as bass
from concourse import mybir

F32 = mybir.dt.float32
F32R = mybir.dt.float32r
BF16 = mybir.dt.bfloat16
ALU = mybir.AluOpType
ACT = mybir.ActivationFunctionType
AX_X = mybir.AxisListType.X

P = 128
B, S, H = 8, 64, 512
T = B * S
FT = H // P
G = T // P
CTX, CD = 1601, 128
NH, HD = 16, 32
HPT = P // HD
NE = 8
GATED = 6
FF = 256
XH, XQ, XR = 16, 384, 64
QT = XQ // P
KT = 13
LASTK = CTX - (KT - 1) * P
MH, MP, MN = 32, 64, 128
INNER = MH * MP
IT = INNER // P
CONV_K = 4
LORA = 16
MASKED = -1e30
CHUNK = 8 * P


def stream_plan():
    up, down, half = CHUNK, CHUNK, CHUNK // 2
    plan = [("A", (6 * P, 6 * P), 2), ("A", (CHUNK, CHUNK), 1),
            ("B", (CHUNK, half), 4), ("B", (CHUNK, CHUNK), 1)]
    for _ in range(2):
        plan += [("C", (up, half), 1), ("C", (up, down, half) * 2, 3), ("C", (up, down, half, down), 1)]
    plan += [("D1", (CHUNK, 6 * P), XH),
             ("D3", (P,), 1), ("D3", (5 * P, 5 * P), 7), ("D3", (5 * P, 4 * P), 1),
             ("E", (CHUNK,), 1), ("E", (CHUNK, CHUNK), IT // 2), ("E", (CHUNK, CHUNK), 4),
             ("F", (half, CHUNK, CHUNK, half), 1), ("F", (CHUNK,) * 6, 3), ("F", (CHUNK,) * 4, 1)]
    return plan


def plan_starts():
    starts, n = {}, 0
    for stage, widths, reps in stream_plan():
        starts.setdefault(stage, n)
        n += len(widths) * reps
    starts["end"] = n
    return starts


def offsets(fields):
    at, found = 0, {}
    for name, width in fields:
        found[name] = (at, width)
        at += width
    return found, at


CONSTANTS, CONSTANT_COLS = offsets([
    ("ident", P), ("mean", P), ("rope", P), ("causal", P), ("batch", P), ("upto", P), ("after", P),
    ("cos_b", S), ("sin_b", S), ("cos_q", QT * S), ("sin_q", QT * S),
    ("lower", NE * NE), ("select", NE * P), ("select_lora", P)])
SMALLS, SMALL_COLS = offsets([
    ("c_gate", 2 * FT * NE), ("c_gate_bias", 2 * NE), ("c_up_bias", NE * 2), ("c_sw_bias", NE * 2),
    ("c_down_bias", H), ("f_gate", FT * NE), ("dt_w", FT * MH), ("dt_bias", MH), ("a_log", MH),
    ("conv_w", (IT + 2) * CONV_K), ("conv_b", IT + 2), ("skip", IT), ("norm_w", IT)])


def shape_constants():
    c = np.zeros((P, CONSTANT_COLS), np.float32)

    def put(name, a):
        first, width = CONSTANTS[name]
        c[:a.shape[0], first:first + width] = a.reshape(a.shape[0], width)

    i = np.arange(P)
    same = i[:, None] // S == i[None, :] // S
    put("ident", np.eye(P, dtype=np.float32))
    put("mean", np.full((P, P), 1.0 / H, np.float32))
    rope = np.zeros((P, P), np.float32)
    rope[i[1::2], i[0::2]] = -1.0
    rope[i[0::2], i[1::2]] = 1.0
    put("rope", rope)
    put("causal", np.where(same & (i[None, :] <= i[:, None]), 0.0, MASKED).astype(np.float32))
    put("batch", np.where(same, 0.0, MASKED).astype(np.float32))
    put("upto", (same & (i[:, None] <= i[None, :])).astype(np.float32))
    put("after", (same & (i[:, None] > i[None, :])).astype(np.float32))

    def angles(n, dim):
        exponent = (np.arange(0, dim, 2, dtype=np.float32) / np.float32(dim)).astype(np.float64)
        inv = np.float32(1.0) / (10000.0 ** exponent).astype(np.float32)
        f = np.arange(n, dtype=np.float32)[:, None] * inv[None, :]
        return np.repeat(f, 2, axis=1)

    fb = np.tile(angles(S, HD).T, (HPT, 1))
    put("cos_b", np.cos(fb))
    put("sin_b", np.sin(fb))
    fq = angles(S, XQ).T
    sign_q = np.where(np.arange(XQ) < XQ // 2, -1.0, 1.0).astype(np.float32)[:, None]
    tiles = lambda a: a.reshape(QT, P, S).transpose(1, 0, 2)
    put("cos_q", tiles(np.cos(fq)))
    put("sin_q", tiles(np.sin(fq) * sign_q))
    e = np.arange(NE)
    put("lower", np.broadcast_to((e[None, :] < e[:, None]).astype(np.float32).reshape(1, -1), (P, NE * NE)))
    put("select", np.repeat(np.eye(NE, dtype=np.float32), P, axis=1))
    put("select_lora", np.where(i[None, :] // LORA == e[:, None], 2.0, 0.0).astype(np.float32))
    fk = angles(KT * P, CD)
    sign_k = np.where(np.arange(CD) < CD // 2, -1.0, 1.0).astype(np.float32)[None, :]
    by_tile = lambda a: np.ascontiguousarray(a.reshape(KT, P, CD).transpose(1, 0, 2))
    return c, np.stack([by_tile(np.cos(fk)), by_tile(np.sin(fk) * sign_k)]).astype(np.float32)


def lay_out(i):
    def tile(w, k, m):
        return w[k * P:(k + 1) * P, m * P:(m + 1) * P]

    def rows(a):
        return np.concatenate([a, np.zeros((P - a.shape[0], a.shape[1]), a.dtype)]) if a.shape[0] < P else a

    chunks = []

    def chunk(*tiles):
        chunks.append(np.concatenate(tiles, axis=1))

    wq, wkv, wo = i["L0_xattn_Wq"].T, i["L0_xattn_Wkv_expand"].T, i["L0_xattn_Wout"].T
    for f in range(FT):
        chunk(*[tile(wq, k, f) for k in range(FT)], tile(wkv, 0, f), tile(wkv, 0, FT + f))

    def projection(w):
        for m in range(0, FT, 2):
            chunk(*[tile(w, k, n) for n in (m, m + 1) for k in range(FT)])

    projection(wo)
    w = i["L0_attn_w_qkv"]
    for f in range(FT):
        chunk(*[tile(w, k, o + f) for o in (0, FT) for k in range(FT)])
        chunk(*[tile(w, k, 2 * FT + f) for k in range(FT)])
    projection(i["L0_attn_w_proj"])

    def up_c(e):
        w, o = (i["L0_ffn_Wup"][e], 0) if e < GATED else (i["L0_ffn_Wsu"], 2 * (e - GATED))
        chunk(*[tile(w, k, o + m) for m in range(2) for k in range(FT)])

    def sw_c(e):
        w = i["L0_ffn_Wsw"][e] if e < GATED else i["L0_ffn_Wsa"]
        chunk(*[tile(w, k, m) for m in range(2) for k in range(2)])

    def down_c(e):
        w = i["L0_ffn_Wdn"][e] if e < GATED else i["L0_ffn_Wsd"][(e - GATED) * FF:(e - GATED + 1) * FF]
        chunk(*[tile(w, k, m) for m in range(FT) for k in range(2)])

    for _ in range(2):
        up_c(0)
        sw_c(0)
        for e in range(1, NE):
            up_c(e)
            down_c(e - 1)
            sw_c(e)
        down_c(NE - 1)

    wq = i["L1_xattn_Wq"].T
    turn = (np.arange(XQ) + XQ // 2) % XQ
    for h in range(XH):
        kc = i["L1_xattn_w_kc_q"][h]
        chunk(*[tile(wq, k, h) for k in range(FT)], kc, rows(i["L1_xattn_W_kr"][h].T))
        chunk(kc[:, turn], rows(i["L1_xattn_W_qr"][h].T))
    wo = i["L1_xattn_Wo"].T
    lat = lambda h: i["L1_xattn_w_kc_kv"][h].T
    out = lambda h: [tile(wo, h, m) for m in range(FT)]
    chunk(lat(0))
    for h in range(1, XH):
        chunk(lat(h), *out(h - 1))
    chunk(*out(XH - 1))

    w = i["L1_attn_W_in"].T
    four = lambda m: [tile(w, k, m) for k in range(FT)]
    chunk(*four(2 * IT), *four(2 * IT + 1))
    for m in range(0, IT, 2):
        chunk(*four(IT + m), *four(IT + m + 1))
        chunk(*four(m), *four(m + 1))
    wo = i["L1_attn_W_out"].T
    for k in range(0, IT, 2):
        chunk(*[tile(wo, n, m) for n in (k, k + 1) for m in range(FT)])

    lora_a = i["L1_ffn_A"].transpose(1, 0, 2).reshape(H, NE * LORA)
    lora_b = i["L1_ffn_B"].reshape(NE * LORA, H)
    chunk(*[tile(lora_a, k, 0) for k in range(FT)])
    wide = lambda w: chunk(*[tile(w, k, m) for m in range(2) for k in range(FT)])
    deep = lambda w: chunk(*[tile(w, k, m) for m in range(FT) for k in range(2)])
    wide(i["L1_ffn_Wg"][0])
    wide(i["L1_ffn_Wu"][0])
    chunk(lora_b)
    for e in range(1, NE):
        wide(i["L1_ffn_Wg"][e])
        wide(i["L1_ffn_Wu"][e])
        deep(i["L1_ffn_Wd"][e - 1])
    deep(i["L1_ffn_Wd"][NE - 1])

    widths = [w for _, body, reps in stream_plan() for _ in range(reps) for w in body]
    assert [c.shape for c in chunks] == [(P, w) for w in widths]
    stream = np.concatenate([np.ascontiguousarray(c).reshape(-1) for c in chunks])

    small = np.zeros((P, SMALL_COLS), np.float32)

    def put(name, a):
        first, width = SMALLS[name]
        small[:a.shape[0], first:first + width] = a.reshape(a.shape[0], width)

    every = lambda a: np.broadcast_to(a.reshape(1, -1), (P, a.size))
    put("c_gate", i["L0_ffn_Wg"].reshape(2, FT, P, NE).transpose(2, 0, 1, 3))
    put("c_gate_bias", every(i["L0_ffn_bg"]))
    up_bias = np.concatenate([i["L0_ffn_bup"], i["L0_ffn_bsu"].reshape(2, FF)])
    sw_bias = np.concatenate([i["L0_ffn_bsw"], i["L0_ffn_bsa"][None], i["L0_ffn_bsa"][None]])
    put("c_up_bias", up_bias.reshape(NE, 2, P).transpose(2, 0, 1))
    put("c_sw_bias", sw_bias.reshape(NE, 2, P).transpose(2, 0, 1))
    put("c_down_bias", np.concatenate([i["L0_ffn_bdn"], i["L0_ffn_bsd"][None], np.zeros((1, H), np.float32)]))
    put("f_gate", i["L1_ffn_gate_w"].reshape(FT, P, NE).transpose(1, 0, 2))
    put("dt_w", np.ascontiguousarray(w[:, 2 * INNER + 2 * MN:]).reshape(FT, P, MH).transpose(1, 0, 2))
    put("dt_bias", every(i["L1_attn_dt_bias"]))
    put("a_log", every(i["L1_attn_A_log"]))
    put("conv_w", i["L1_attn_conv_w"].reshape(IT + 2, P, CONV_K).transpose(1, 0, 2))
    put("conv_b", i["L1_attn_conv_b"].reshape(IT + 2, P).T)
    put("skip", np.repeat(i["L1_attn_D_param"], MP).reshape(IT, P).T)
    put("norm_w", i["L1_attn_norm_w"].reshape(IT, P).T)

    constants, rope_k = shape_constants()
    ctx = i["ctx_512"]
    tiles = np.concatenate([ctx, np.zeros((B, KT * P - CTX, CD), np.float32)], axis=1)
    return {
        "x": np.ascontiguousarray(i["x"].reshape(T, FT, P).transpose(2, 1, 0)),
        "ctx_first": np.ascontiguousarray(ctx[:, :S].reshape(T, CD).T),
        "ctx": np.ascontiguousarray(tiles.reshape(B, KT, P, CD).transpose(0, 2, 1, 3)),
        "weights": stream, "small": small, "constants": constants, "rope_k": rope_k,
    }


def perceiver_stack(nc, x_in, ctx_first, ctx_in, weights, small_in, constants_in, rope_k_in, x_out):
    starts = plan_starts()
    last_stage = LAST_STAGE

    with ExitStack() as held:
        def sb(name, shape, dt=F32, scope=None):
            return (scope or held).enter_context(nc.sbuf_tensor(name, shape, dt))

        def sem(name):
            return held.enter_context(nc.semaphore(name))

        x = sb("x", [P, FT, T])
        landing = sb("landing", [P, 2, CHUNK])
        wpair = sb("wpair", [P, 2, 2, CHUNK], F32R)
        const = sb("const", [P, CONSTANT_COLS])
        small = sb("small", [P, SMALL_COLS])
        eps = sb("eps", [P, 1])
        zero_b = sb("zero_b", [P, T], BF16)
        big = sb("big", [P, B * XH * S])
        psum = held.enter_context(nc.psum_tensor("psum", [P, 8, 512], F32))

        def bank(k):
            return psum[:, k, :]

        def by_batch(ap):
            return ap.rearrange("p (b s) -> p b s", s=S)

        def over_batches(ap):
            return ap.unsqueeze(1).broadcast_to([P, B, S])

        def constant(name, rows=P):
            first, width = CONSTANTS[name]
            return const[0:rows, first:first + width]

        def small_at(name, rows=P):
            first, width = SMALLS[name]
            return small[0:rows, first:first + width]

        ln_scope = ExitStack()
        xn = sb("xn", [P, 2, FT, T], F32R, ln_scope)
        xc = sb("xc", [P, FT, T], F32, ln_scope)
        sq = sb("sq", [P, FT, T], F32, ln_scope)
        rstd = sb("rstd", [P, T], F32, ln_scope)

        with ExitStack() as scope:
            first_pair = sb("first_pair", [P, 2, T], F32R, scope)
            first_raw = sb("first_raw", [P, T], F32, scope)
            ident_b = sb("ident_b", [P, P], BF16, scope)
            mask_b = sb("mask_b", [P, 2, G, P], BF16, scope)
            q_raw = sb("q_raw", [P, T], F32, scope)
            k_raw = sb("k_raw", [P, T], F32, scope)
            q_t = sb("q_t", [P, T], F32, scope)
            k_t = sb("k_t", [P, T], F32, scope)
            turned = sb("turned", [P, 2, T], F32, scope)
            v_tok = sb("v_tok", [P, G, P], F32, scope)
            prob = sb("prob", [P, HPT, G, P], F32, scope)
            prob_t = sb("prob_t", [P, 2, G, P], F32, scope)
            neg_max = sb("neg_max", [P, HPT, G], F32, scope)
            row_sum = sb("row_sum", [P, HPT, G], F32, scope)
            row_inv = sb("row_inv", [P, HPT, G], F32, scope)
            heads_out = sb("heads_out", [P, 2, FT, T], F32R, scope)
        with ExitStack() as scope:
            wide_w = sb("wide_w", [P, NE, T], F32, scope)
            gate_s = sb("gate_s", [P, 8, G, NE], F32, scope)
            pairs_s = sb("pairs_s", [P, 2, G, NE, NE], F32, scope)
            gate_col = sb("gate_col", [P, 4, G, 1], F32, scope)
            w_rows = sb("w_rows", [NE, T], F32, scope)
            hid = sb("hid", [P, 2, T], F32, scope)
            hid_pair = sb("hid_pair", [P, 2, 2, T], F32R, scope)
            act_o = sb("act_o", [P, 2, T], F32, scope)
            mid = sb("mid", [P, 2, T], F32, scope)
            mid_pair = sb("mid_pair", [P, 2, 2, T], F32R, scope)
            lora_h = sb("lora_h", [P, T], F32, scope)
            lora_w = sb("lora_w", [P, T], F32, scope)
            lora_pair = sb("lora_pair", [P, 2, T], F32R, scope)
        with ExitStack() as scope:
            hk_pair = sb("hk_pair", [P, 2, T], F32R, scope)
            by_cos = sb("by_cos", [P, QT, T], F32, scope)
            by_sin = sb("by_sin", [P, 2, T], F32, scope)
            turned_pair = sb("turned_pair", [P, 2, QT, T], F32R, scope)
            absorb_pair = sb("absorb_pair", [P, 2, QT * P], F32R, scope)
        with ExitStack() as scope:
            conv_in = sb("conv_in", [P, 2, B, S + CONV_K - 1], F32, scope)
            conv_acc = sb("conv_acc", [P, 2, T], F32, scope)
            bc_t = sb("bc_t", [P, 2, T], F32, scope)
            dt_s = sb("dt_s", [P, 5, G * MH], F32, scope)
            exp_a = sb("exp_a", [P, MH], F32, scope)
            g_mask = sb("g_mask", [P, G, P], F32, scope)
            xs_t = sb("xs_t", [P, 2, 2, T], F32, scope)
            silu_g = sb("silu_g", [P, 2, 2, T], F32, scope)
            decay_in = sb("decay_in", [P, G, 4, P], F32, scope)
            decay = sb("decay", [P, 2, 4, P], F32, scope)
            mix = sb("mix", [P, G, 4, P], F32, scope)
            xdt = sb("xdt", [P, G, 4, MP], F32, scope)
            y_sum = sb("y_sum", [P, 2, T], F32, scope)
            y_gated = sb("y_gated", [P, 2, T], F32, scope)
            y_sq = sb("y_sq", [P, 2, T], F32, scope)
            sq_sum = sb("sq_sum", [P, T], F32, scope)
            gated_pair = sb("gated_pair", [P, 4, 2, T], F32R, scope)
        with ExitStack() as scope:
            ctx_pair = sb("ctx_pair", [P, 2, 2, T], F32R, scope)
            lat_pair = sb("lat_pair", [P, 2, 2, T], F32R, scope)
        ln_scope.close()
        with ExitStack() as scope:
            kv_t = sb("kv_t", [P, 2, 2, CTX + 1], F32R, scope)
            expo = sb("expo", [P, 2, 2, CTX + 1], F32, scope)
            expo_t = sb("expo_t", [P, 3, 2, 512], F32R, scope)
            q_pair = sb("q_pair", [P, 2, 2, 256], F32R, scope)
            out_c = sb("out_c", [P, 256], F32, scope)
            diag = sb("diag", [P, 2, 2, P], F32, scope)
            part_max = sb("part_max", [P, 2, 2], F32, scope)
            neg_m = sb("neg_m", [P, 2], F32, scope)
            part_sum = sb("part_sum", [P, 2, 3], F32, scope)
            sums = sb("sums", [P, 2, 2], F32, scope)
            kv_pair = sb("kv_pair", [P, 2, 2, KT, CD], F32R, scope)
            rope_k = sb("rope_k", [P, 2, KT, CD], F32, scope)
            kv = sb("kv", [P, KT, CD], F32, scope)
            kv_turn = sb("kv_turn", [P, KT, CD], F32, scope)

        inputs_in = sem("inputs_in")
        smalls_in = sem("smalls_in")
        chunk_in = [sem("chunk_in_0"), sem("chunk_in_1")]
        chunk_high = sem("chunk_high")
        chunk_split = sem("chunk_split")
        pool_started = sem("pool_started")
        chunk_used = sem("chunk_used")
        setup = sem("setup")
        x_ready = sem("x_ready")
        ln_mean, ln_centred, ln_squared, ln_var = sem("ln_mean"), sem("ln_centred"), sem("ln_squared"), sem("ln_var")
        ln_log, ln_rstd, ln_normal = sem("ln_log"), sem("ln_rstd"), sem("ln_normal")
        ln_high, ln_low = sem("ln_high"), sem("ln_low")
        stored = sem("stored")

        projected = sem("projected")
        q_in, k_in, v_in = sem("q_in"), sem("k_in"), sem("v_in")
        qk_turned, rope_steps = sem("qk_turned"), sem("rope_steps")
        scores, maxed, expd = sem("scores"), sem("maxed"), sem("expd")
        row_inverted, normal = sem("row_inverted"), sem("normal")
        prob_turned, prob_in = sem("prob_turned"), sem("prob_in")
        attended, heads_high, heads_low = sem("attended"), sem("heads_high"), sem("heads_low")
        heads_read = sem("heads_read")
        out_done = sem("out_done")
        gated, gate_exp = sem("gated"), sem("gate_exp")
        gate_step = sem("gate_step")
        rows_turned, rows_in = sem("rows_turned"), sem("rows_in")
        spread, spread_in = sem("spread"), sem("spread_in")
        first, second = sem("first"), sem("second")
        hid_in, hid_high, hid_low = sem("hid_in"), sem("hid_high"), sem("hid_low")
        silu_done, mid_step = sem("silu_done"), sem("mid_step")
        mid_high, mid_low = sem("mid_high"), sem("mid_low")
        lora_done, lora_in = sem("lora_done"), sem("lora_in")
        mixed_out = sem("mixed_out")
        second_in = sem("second_in")

        hk_done, hk_high, hk_low = sem("hk_done"), sem("hk_high"), sem("hk_low")
        absorbed, absorb_high, absorb_low = sem("absorbed"), sem("absorb_high"), sem("absorb_low")
        q_big, q_turned = sem("q_big"), sem("q_turned")
        turn_step = sem("turn_step")
        rope_high, rope_low = sem("rope_high"), sem("rope_low")
        q_lat, q_lat_in = sem("q_lat"), sem("q_lat_in")
        tables_in, ctx_loaded = sem("tables_in"), sem("ctx_loaded")
        kv_step = sem("kv_step")
        values_high, values_split = sem("values_high"), sem("values_split")
        keys_t, keys_high, keys_low = sem("keys_t"), sem("keys_high"), sem("keys_low")
        qu_high, qu_low = sem("qu_high"), sem("qu_low")
        scored = sem("scored")
        max_part, max_done = sem("max_part"), sem("max_done")
        exp_done = sem("exp_done")
        summed, inverted, diagonal = sem("summed"), sem("inverted"), sem("diagonal")
        exp_t, exp_t_high, exp_t_low = sem("exp_t"), sem("exp_t_high"), sem("exp_t_low")
        context_sum, context_in = sem("context_sum"), sem("context_in")
        scale_out, context_done = sem("scale_out"), sem("context_done")
        ctx_high, ctx_low = sem("ctx_high"), sem("ctx_low")
        lat_done, lat_high, lat_low = sem("lat_done"), sem("lat_high"), sem("lat_low")
        d_out = sem("d_out")
        bc_done, conv_pad = sem("bc_done"), sem("conv_pad")
        conv_step, conv_silu = sem("conv_step"), sem("conv_silu")
        dt_done, dt_step, dt_exp, a_exp = sem("dt_done"), sem("dt_step"), sem("dt_exp"), sem("a_exp")
        g_done, g_masked = sem("g_done"), sem("g_masked")
        xs_done, gate_done, xs_copied, gate_silu = sem("xs_done"), sem("gate_done"), sem("xs_copied"), sem("gate_silu")
        decay_ready, decay_sum, decay_exp, mixed = sem("decay_ready"), sem("decay_sum"), sem("decay_exp"), sem("mixed")
        xs_turned, xdt_ready = sem("xs_turned"), sem("xdt_ready")
        y_done, y_step, y_squared = sem("y_done"), sem("y_step"), sem("y_squared")
        norm_sum, norm_log, norm_inv = sem("norm_sum"), sem("norm_log"), sem("norm_inv")
        gh_high, gh_low = sem("gh_high"), sem("gh_low")
        e_out, e_scaled = sem("e_out"), sem("e_scaled")

        block = held.enter_context(nc.Block())

        def chunk_regions():
            n = at = 0
            for stage, widths, reps in stream_plan():
                yield stage, n, at, widths, reps
                n += len(widths) * reps
                at += sum(widths) * P * reps

        def run_region(eng, region, step):
            _, n0, at0, widths, reps = region
            ats = [at0 + P * sum(widths[:j]) for j in range(len(widths))]
            if reps == 1:
                for j, w in enumerate(widths):
                    step(n0 + j, (n0 + j) // 2, ats[j], (n0 + j) % 2, w)
                return
            first = 0
            if n0 == 0:
                for j, w in enumerate(widths):
                    step(j, 0, ats[j], j % 2, w)
                first = 1
            with eng.Fori(first, reps) as i:
                for j, w in enumerate(widths):
                    step(n0 + j + i * len(widths), (n0 + j) // 2 + i * (len(widths) // 2),
                         ats[j] + i * (sum(widths) * P), (n0 + j) % 2, w)

        def unslotted(n):
            return isinstance(n, int) and n < 2

        REGIONS = [r for r in chunk_regions() if STAGES.index(r[0][0]) <= STAGES.index(last_stage)]

        def weight(slot, part, t, rows=P):
            return wpair[0:rows, slot, part, t * P:(t + 1) * P]

        @block.sync
        def _(sp):
            sp.dma_start(x[:, :, :], x_in).then_inc(inputs_in, 16)
            sp.dma_start(const[:, :], constants_in).then_inc(smalls_in, 16)
            sp.dma_start(small[:, :], small_in).then_inc(smalls_in, 16)
            sp.dma_start(first_raw[:, :], ctx_first).then_inc(inputs_in, 16)

            def load(n, _, at, slot, width):
                if not unslotted(n):
                    sp.wait_ge(chunk_split, n - 1)
                sp.dma_start(landing[:, slot, 0:width],
                             weights[bass.ds(at, P * width)].rearrange("(p n) -> p n", p=P)
                             ).then_inc(chunk_in[slot], 16)

            for region in REGIONS:
                if region[0] == "D1":
                    sp.wait_ge(x_ready, 4 * 3)
                    sp.dma_start(rope_k[:, :, :, :], rope_k_in.rearrange("a p k d -> p a k d")).then_inc(tables_in, 16)
                    sp.dma_start(kv[:, :, :], ctx_in[0]).then_inc(ctx_loaded, 16)
                run_region(sp, region, load)
                if region[0] == "D1":
                    with sp.Fori(1, B) as b:
                        sp.wait_ge(keys_t, 4 * b)
                        sp.wait_ge(values_split, b)
                        sp.dma_start(kv[:, :, :], ctx_in[bass.ds(b, 1)].rearrange("a p k d -> (a p) k d")
                                     ).then_inc(ctx_loaded, 16)

            sp.wait_ge(x_ready, 4 * (STAGES.index(last_stage) + 1))
            sp.dma_start(x_out, x[:, :, :]).then_inc(stored, 16)
            sp.wait_ge(stored, 16)

        @block.gpsimd
        def _(pool):
            def split(n, use, _, slot, width):
                pool.wait_ge(chunk_in[slot], 16 * use + 16)
                if not unslotted(n):
                    pool.wait_ge(chunk_used, n - 1)
                pool.sem_inc(pool_started, 1)
                pool.tensor_scalar(wpair[:, slot, 0, 0:width], landing[:, slot, 0:width], 1.0, 1.0,
                                   ALU.mult, ALU.mult).then_inc(chunk_high, 1)
                pool.wait_ge(chunk_high, n + 1)
                pool.tensor_tensor(wpair[:, slot, 1, 0:width], landing[:, slot, 0:width],
                                   wpair[:, slot, 0, 0:width].bitcast(F32), ALU.subtract
                                   ).then_inc(chunk_split, 1)

            def context_steps(b, buffer, reused):
                half = CD // 2
                cos, sin = rope_k[:, 0, :, :], rope_k[:, 1, :, :]
                pool.wait_ge(ctx_loaded, 16 * b + 16)
                pool.tensor_tensor(kv_turn[:, :, 0:half], kv[:, :, half:CD], sin[:, :, 0:half], ALU.mult)
                pool.tensor_tensor(kv_turn[:, :, half:CD], kv[:, :, 0:half], sin[:, :, half:CD],
                                   ALU.mult).then_inc(kv_step, 1)
                yield
                pool.wait_ge(kv_step, 3 * b + 1)
                pool.tensor_tensor(kv[:, :, :], kv[:, :, :], cos, ALU.mult).then_inc(kv_step, 1)
                yield
                pool.wait_ge(kv_step, 3 * b + 2)
                pool.tensor_tensor(kv[:, :, :], kv[:, :, :], kv_turn[:, :, :], ALU.add).then_inc(kv_step, 1)
                yield
                pool.wait_ge(kv_step, 3 * b + 3)
                if reused:
                    pool.wait_ge(context_sum, 4 * b - 4)
                pool.sem_inc(pool_started, 1)
                pool.tensor_scalar(kv_pair[:, buffer, 0, :, :], kv[:, :, :], 1.0, 1.0, ALU.mult, ALU.mult
                                   ).then_inc(values_high, 1)
                yield
                pool.wait_ge(values_high, b + 1)
                pool.tensor_tensor(kv_pair[:, buffer, 1, :, :], kv[:, :, :],
                                   kv_pair[:, buffer, 0, :, :].bitcast(F32), ALU.subtract
                                   ).then_inc(values_split, 1)
                yield

            def whole(steps):
                for _ in steps:
                    pass

            for region in REGIONS:
                if region[0] != "D1":
                    run_region(pool, region, split)
                    continue
                _, n0, at0, widths, _ = region
                pool.wait_ge(tables_in, 16)
                steps = context_steps(0, 0, False)
                for part in range(5):
                    run_region(pool, ("D1", n0 + 6 * part, at0 + 3 * part * sum(widths) * P, widths, 3), split)
                    next(steps)
                run_region(pool, ("D1", n0 + 30, at0 + 15 * sum(widths) * P, widths, 1), split)
                whole(context_steps(1, 1, False))
                with pool.Fori(1, B // 2) as i:
                    for j in range(2):
                        whole(context_steps(2 * i + j, j, True))

        CB, DB, EB, FB = starts["C"], starts["D1"], starts["E"], starts["F"]
        D3B = starts["D3"]
        A_OUT, B_OUT, E_OUT = FT, starts["B"] + 2 * FT, EB + 1 + IT
        SPREADS = (GATED, GATED, NE + 1)
        SPREAD_0 = (0, GATED, 2 * GATED)
        GATE_STEPS = (12, 12, 16)
        GATE_0 = (0, 12, 24)
        ROW_CHUNKS = ((0, 400), (400, 400), (800, 400), (1200, 401))

        def c_chunks(p, e):
            base = CB + 3 * NE * p
            return (base, base + 1) if isinstance(e, int) and e == 0 else (base + 3 * e - 1, base + 3 * e + 1)

        def f_chunks(e):
            return (FB + 1, FB + 2) if isinstance(e, int) and e == 0 else (FB + 3 * e + 1, FB + 3 * e + 2)

        def runs(stage):
            return STAGES.index(stage) <= STAGES.index(last_stage)

        @block.tensor
        def _(pe):
            def product(out, w, act, start=False, stop=False):
                pe.matmul(out, w(0), act(0), start=start, stop=False)
                pe.matmul(out, w(0), act(1), start=False, stop=False)
                return pe.matmul(out, w(1), act(0), start=False, stop=stop)

            def tokens(pair, k):
                return lambda part: pair[:, part, k, :]

            def tile_of(slot, t):
                return lambda part: weight(slot, part, t)

            def chunk_ready(n):
                pe.wait_ge(chunk_split, n + 1)

            def open_sums():
                for m in range(FT):
                    pe.matmul(bank(4 + m), zero_b[:, 0:P], zero_b[:, :], start=True, stop=False)

            def layer_norm(k):
                if k:
                    pe.wait_ge(x_ready, 4 * k)
                else:
                    pe.wait_ge(inputs_in, 32)
                    pe.wait_ge(smalls_in, 32)
                for f in range(FT):
                    mm = pe.matmul(bank(6), constant("mean"), x[:, f, :], start=f == 0, stop=f == FT - 1)
                mm.then_inc(ln_mean, 1)
                for f in range(FT):
                    pe.wait_ge(ln_squared, 4 * k + f + 1)
                    mm = pe.matmul(bank(7), constant("mean"), sq[:, f, :], start=f == 0, stop=f == FT - 1)
                mm.then_inc(ln_var, 1)
                pe.wait_ge(ln_low, 4 * k + 4)

            def wide(slot, first_tile, act, out, kts=FT, close=True):
                for k in range(kts):
                    mm = product(out, tile_of(slot, first_tile + k), tokens(act, k),
                                 start=k == 0, stop=close and k == kts - 1)
                return mm

            def attention_tile(u, mask, rope):
                if rope:
                    for side, (raw, arrived) in enumerate(((q_raw, q_in), (k_raw, k_in))):
                        pe.wait_ge(arrived, u + 1)
                        pe.matmul(bank(3 + side), constant("rope"), raw[:, :], start=True, stop=True
                                  ).then_inc(qk_turned, 1)
                    pe.wait_ge(rope_steps, 6 * (u - FT) + 6)
                else:
                    pe.wait_ge(q_in, u + 1)
                    pe.wait_ge(k_in, u + 1)
                for h in range(HPT):
                    rows = slice(h * HD, (h + 1) * HD)
                    pe.matmul(bank(3 + h), ident_b[:, :], mask_b[:, mask, :, :].rearrange("p g k -> p (g k)"),
                              start=True, stop=False)
                    for g in range(G):
                        mm = pe.matmul(bank(3 + h)[:, g * P:(g + 1) * P], q_t[rows, g * P:(g + 1) * P],
                                       k_t[rows, g * P:(g + 1) * P], start=False, stop=g == G - 1)
                    mm.then_inc(scores, 1)

                def transposes(h):
                    pe.wait_ge(normal, HPT * u + h + 1)
                    for g in range(G):
                        mm = pe.transpose(bank(h % 2)[:, g * P:(g + 1) * P], prob[:, h, g, :], constant("ident"))
                    mm.then_inc(prob_turned, 1)

                def values(h):
                    pe.wait_ge(prob_in, HPT * u + h + 1)
                    if h == 0:
                        pe.wait_ge(v_in, u + 1)
                        pe.wait_ge(heads_read, u + 1)
                    for g in range(G):
                        mm = pe.matmul(bank(7)[h * HD:(h + 1) * HD, g * P:(g + 1) * P],
                                       v_tok[:, g, h * HD:(h + 1) * HD], prob_t[:, h % 2, g, :],
                                       start=True, stop=True)
                    if h == HPT - 1:
                        mm.then_inc(attended, 1)

                transposes(0)
                transposes(1)
                values(0)
                transposes(2)
                values(1)
                transposes(3)
                values(2)
                values(3)

            def value_tile(slot, first_tile, act, kts):
                for g in range(G):
                    for k in range(kts):
                        group = lambda part, k=k: act(part, k)[:, g * P:(g + 1) * P]
                        mm = product(bank(2)[:, g * P:(g + 1) * P], group, tile_of(slot, first_tile + k),
                                     start=k == 0, stop=k == kts - 1)
                return mm

            def out_projection(n0, tiles):
                pe.wait_ge(heads_low, tiles)
                for c in range(2):
                    chunk_ready(n0 + c)
                    slot = (n0 + c) % 2
                    wide(slot, 0, heads_out, bank(2 * c)).then_inc(out_done, 1)
                    wide(slot, FT, heads_out, bank(2 * c + 1)).then_inc(chunk_used, 1)

            layer_norm(0)
            pe.wait_ge(setup, 7)
            with pe.Fori(0, FT // 2) as i:
                for j in range(2):
                    u = 2 * i + j
                    chunk_ready(u)
                    wide(j, 0, xn, bank(0)).then_inc(projected, 1)
                    product(bank(1), tile_of(j, FT), lambda part: first_pair[:, part, :], start=True, stop=True
                            ).then_inc(projected, 1)
                    value_tile(j, FT + 1, lambda part, k: first_pair[:, part, :], 1).then_inc(chunk_used, 1)
                    attention_tile(u, 0, False)
            out_projection(A_OUT, FT)

            if runs("B"):
                layer_norm(1)
                n0, slot = starts["B"], starts["B"] % 2
                with pe.Fori(0, FT) as f:
                    chunk_ready(n0 + 2 * f)
                    wide(slot, 0, xn, bank(0)).then_inc(projected, 1)
                    wide(slot, FT, xn, bank(1)).then_inc(chunk_used, 1)
                    chunk_ready(n0 + 2 * f + 1)
                    value_tile(1 - slot, 0, lambda part, k: xn[:, part, k, :], FT).then_inc(chunk_used, 1)
                    attention_tile(FT + f, 1, True)
                out_projection(B_OUT, 2 * FT)

            def gate_logits(src, w):
                for g in range(G):
                    for k in range(FT):
                        mm = pe.matmul(bank(4)[:, g * NE:(g + 1) * NE], src[:, k, g * P:(g + 1) * P],
                                       w[:, k, :], start=k == 0, stop=k == FT - 1)
                mm.then_inc(gated, 1)

            def turn_rows(p):
                pe.wait_ge(gate_step, GATE_0[p] + GATE_STEPS[p])
                for g in range(G):
                    mm = pe.transpose(bank(5)[0:NE, g * P:(g + 1) * P], gate_s[:, 5, g, :], constant("ident"))
                mm.then_inc(rows_turned, 1)
                pe.wait_ge(rows_in, p + 1)

            def spread_rows(p, first_spread, experts):
                for e in range(experts):
                    if e >= 2:
                        pe.wait_ge(spread_in, first_spread + e - 1)
                    pe.matmul(bank(5 + e % 2), constant("select", NE)[:, e * P:(e + 1) * P], w_rows[:, :],
                              start=True, stop=True).then_inc(spread, 1)
                pe.wait_ge(spread_in, first_spread + experts)

            def two_tiles(n, slot, act, first_bank, signal, kts=FT):
                chunk_ready(n)
                wide(slot, 0, act, bank(first_bank), kts).then_inc(signal, 1)
                wide(slot, kts, act, bank(first_bank + 1), kts).then_inc(chunk_used, 1)

            def down(n, slot, expert, last=False):
                chunk_ready(n)
                pe.wait_ge(mid_low, 2 * expert + 2)
                for m in range(FT):
                    for k in range(2):
                        mm = product(bank(4 + m), tile_of(slot, 2 * m + k),
                                     lambda part, k=k: mid_pair[:, part, k, :], stop=last and k == 1)
                    if last and m < FT - 1:
                        mm.then_inc(mixed_out, 1)
                mm.then_inc(chunk_used, 1)

            def second_products(p, e, n, slot):
                pe.wait_ge(hid_low, 2 * (NE * p + e) + 2)
                two_tiles(n, slot, hid_pair, 2, second, 2)

            if runs("C"):
                layer_norm(2)
            for p in range(2 if runs("C") else 0):
                cb = CB + 3 * NE * p
                if p:
                    pe.wait_ge(second_in, 3 * FT)
                first_c, width_c = SMALLS["c_gate"]
                w = small[:, first_c + p * FT * NE:first_c + (p + 1) * FT * NE].rearrange("p (k e) -> p k e", e=NE)
                gate_logits(sq if p else xc, w)
                two_tiles(cb, cb % 2, xn, 0, first)
                second_products(p, 0, cb + 1, (cb + 1) % 2)
                turn_rows(p)
                spread_rows(p, SPREAD_0[p], GATED)
                for m in range(FT):
                    pe.matmul(bank(4 + m), small_at("c_down_bias", NE)[:, m * P:(m + 1) * P], w_rows[:, :],
                              start=True, stop=False)

                def expert_c(e, n, slot):
                    two_tiles(n, slot, xn, 0, first)
                    down(n + 1, 1 - slot, NE * p + e - 1)
                    second_products(p, e, n + 2, slot)

                with pe.Fori(0, 3) as i:
                    for j in range(2):
                        expert_c(2 * i + j + 1, cb + 2 + 6 * i + 3 * j, (cb + 3 * j) % 2)
                expert_c(NE - 1, cb + 20, cb % 2)
                down(cb + 23, (cb + 23) % 2, NE * p + NE - 1, True)

            if runs("D"):
                layer_norm(3)

                def absorbed_queries(h):
                    pe.wait_ge(absorb_low, h + 1)
                    pe.wait_ge(rope_low, QT * h + QT)
                    pe.wait_ge(q_lat_in, h + 1)
                    for k in range(QT):
                        mm = product(bank(7), lambda part, k=k: absorb_pair[:, part, k * P:(k + 1) * P],
                                     tokens(turned_pair, k), start=k == 0, stop=k == QT - 1)
                    mm.then_inc(q_lat, 1)

                def query_head(h, slot, before):
                    n = DB + 2 * h
                    chunk_ready(n)
                    if before:
                        pe.wait_ge(absorb_low, h)
                    wide(slot, 0, xn, bank(0)).then_inc(hk_done, 1)
                    if before:
                        absorbed_queries(h - 1)
                    chunk_ready(n + 1)
                    pe.wait_ge(hk_low, h + 1)
                    for k in range(QT):
                        mm = product(bank(0)[:, k * P:(k + 1) * P],
                                     lambda part, k=k: weight(1 - slot, part, QT + k, XR),
                                     lambda part: weight(slot, part, FT + QT, XR), start=True, stop=True)
                    mm.then_inc(absorbed, 1)
                    for side in range(2):
                        for k in range(QT):
                            mm = product(bank(1 + QT * side + k),
                                         tile_of(slot, FT + k) if side == 0 else tile_of(1 - slot, k),
                                         lambda part: hk_pair[:, part, :], start=True, stop=True)
                            mm.then_inc(chunk_used if k == QT - 1 else (q_big, q_turned)[side], 1)

                slot = DB % 2
                query_head(0, slot, False)
                with pe.Fori(1, XH) as h:
                    query_head(h, slot, True)
                absorbed_queries(XH - 1)

                def turn_keys(b, part, unit=None):
                    if part == 0:
                        pe.wait_ge(kv_step, 3 * b + 3)
                        if unit is not None:
                            pe.wait_ge(context_done, unit + 1)
                    pe.wait_ge(keys_low, 4 * b + part + 1)
                    for k in range(4 * part, min(4 * part + 4, KT)):
                        rows = P if k < KT - 1 else LASTK
                        at = (k - 4 * part) * P
                        mm = pe.transpose(bank(7)[:, at:at + rows], kv[0:rows, k, :],
                                          constant("ident", rows)[:, 0:rows])
                    mm.then_inc(keys_t, 1)

                def score_row(i, k, r):
                    unit, buffer, keys = 8 * i + k, k % 2, (k // 4) % 2
                    if r == 0:
                        pe.wait_ge(qu_low, unit + 1)
                        if k % 4 == 0:
                            pe.wait_ge(keys_low, 4 * (2 * i + k // 4) + 5)
                    for c in range(4):
                        pe.wait_ge(exp_done, 6 * unit + 3 * r + (1, 1, 2, 3)[c])
                        product(bank(c)[:, 0:402],
                                lambda part: q_pair[:, buffer, part, r * P:(r + 1) * P],
                                lambda part, c=c: kv_t[:, keys, part, 400 * c:400 * c + 402],
                                start=True, stop=True).then_inc(scored, 1)

                def turn_exp(i, k, q):
                    if q == 0:
                        pe.wait_ge(exp_done, 6 * (8 * i + k) + 9)
                    for t in range(2 * q, min(2 * q + 2, KT)):
                        rows = P if t < KT - 1 else LASTK
                        for r in range(2):
                            at = (t % 2) * 256 + r * P
                            mm = pe.transpose(bank(4 + q % 2)[0:rows, at:at + P],
                                              expo[:, k % 2, r, t * P:t * P + rows], constant("ident"))
                    mm.then_inc(exp_t, 1)

                def add_values(i, k, q):
                    unit, buffer = 8 * i + k, (k // 4) % 2
                    if q == 0:
                        pe.wait_ge(context_in, unit + 1)
                        if k % 4 == 0:
                            pe.wait_ge(values_split, 2 * i + k // 4 + 1)
                    pe.wait_ge(exp_t_low, 7 * unit + q + 1)
                    for t in range(2 * q, min(2 * q + 2, KT)):
                        rows = P if t < KT - 1 else LASTK
                        cols = slice((t % 2) * 256, (t % 2) * 256 + 256)
                        mm = product(bank(6)[:, 0:256],
                                     lambda part, t=t, rows=rows: kv_pair[0:rows, buffer, part, t, :],
                                     lambda part, rows=rows, cols=cols: expo_t[0:rows, q % 3, part, cols],
                                     start=t == 0, stop=t == KT - 1)
                    if q == 6:
                        mm.then_inc(context_sum, 1)

                def spread_scale(i, k, turned_b):
                    unit = 8 * i + k
                    pe.wait_ge(diagonal, 2 * unit + 2)
                    pe.wait_ge(context_done, unit + 1)
                    if turned_b is not None:
                        pe.wait_ge(keys_low, 4 * turned_b + 5)
                    pe.matmul(bank(7)[:, 0:256], constant("mean"),
                              diag[:, k % 2, :, :].rearrange("p r q -> p (r q)"), start=True, stop=True
                              ).then_inc(scale_out, 1)

                def units(i, last):
                    for k in range(8):
                        ahead = k < 7 or not last
                        nxt = (i, k + 1) if k < 7 else (i + 1, 0)
                        turned_b = {2: 2 * i + 1, 6: None if last else 2 * i + 2}.get(k)
                        keys = ((lambda part: turn_keys(turned_b, part, 8 * i + k)) if turned_b is not None
                                else (lambda part: None))
                        if ahead:
                            score_row(*nxt, 0)
                        keys(0)
                        turn_exp(i, k, 0)
                        turn_exp(i, k, 1)
                        keys(1)
                        add_values(i, k, 0)
                        turn_exp(i, k, 2)
                        add_values(i, k, 1)
                        keys(2)
                        turn_exp(i, k, 3)
                        add_values(i, k, 2)
                        if ahead:
                            score_row(*nxt, 1)
                        keys(3)
                        for q in range(4, 7):
                            turn_exp(i, k, q)
                            add_values(i, k, q - 1)
                        add_values(i, k, 6)
                        spread_scale(i, k, turned_b)

                pe.wait_ge(q_lat_in, XH + 1)
                for part in range(4):
                    turn_keys(0, part)
                for r in range(2):
                    score_row(0, 0, r)
                with pe.Fori(0, B // 2 - 1) as i:
                    units(i, False)
                units(B // 2 - 1, True)

                def value_latents(h, slot, buffer):
                    chunk_ready(D3B + h)
                    pe.wait_ge(ctx_low, h + 1)
                    return product(bank(buffer), tile_of(slot, 0), lambda part: ctx_pair[:, buffer, part, :],
                                   start=True, stop=True)

                def latent_outputs(h, n, slot, first_tile, buffer, last=False):
                    chunk_ready(n)
                    pe.wait_ge(lat_low, h + 1)
                    for m in range(FT):
                        mm = product(bank(4 + m), tile_of(slot, first_tile + m),
                                     lambda part: lat_pair[:, buffer, part, :], stop=last)
                        if last and m < FT - 1:
                            mm.then_inc(d_out, 1)
                    mm.then_inc(chunk_used, 1)

                value_latents(0, D3B % 2, 0).then_inc(chunk_used, 1)
                pe.wait_ge(context_done, 4 * B + 1)
                open_sums()

                def latent_head(h, j):
                    slot = (D3B + j) % 2
                    value_latents(h, slot, j % 2).then_inc(lat_done, 1)
                    latent_outputs(h - 1, D3B + h, slot, 1, 1 - j % 2)

                with pe.Fori(0, 7) as i:
                    for j in (1, 2):
                        latent_head(2 * i + j, j)
                latent_head(XH - 1, XH - 1)
                latent_outputs(XH - 1, D3B + XH, (D3B + XH) % 2, 0, (XH - 1) % 2, True)

            if runs("E"):
                layer_norm(4)
                chunk_ready(EB)
                wide(EB % 2, 0, xn, bank(0)).then_inc(bc_done, 1)
                wide(EB % 2, FT, xn, bank(1)).then_inc(chunk_used, 1)
                dt_w = small_at("dt_w").rearrange("p (k h) -> p k h", h=MH)
                for g in range(G):
                    for k in range(FT):
                        mm = pe.matmul(bank(2)[:, g * MH:(g + 1) * MH], xc[:, k, g * P:(g + 1) * P], dt_w[:, k, :],
                                       start=k == 0, stop=k == FT - 1)
                mm.then_inc(dt_done, 1)
                pe.wait_ge(conv_silu, 2)
                for g in range(G):
                    cols = slice(g * P, (g + 1) * P)
                    mm = pe.matmul(bank(3)[:, cols], bc_t[:, 0, cols], bc_t[:, 1, cols], start=True, stop=True)
                mm.then_inc(g_done, 1)
                pe.wait_ge(dt_step, 1)
                pe.wait_ge(g_masked, 1)

                def mamba_outputs(i):
                    pe.wait_ge(mixed, 4 * i + 4)
                    for m in range(2):
                        pe.wait_ge(xdt_ready, 2 * i + 2)
                        for hh in range(2):
                            for g in range(G):
                                mm = pe.matmul(bank(4 + m)[hh * MP:(hh + 1) * MP, g * P:(g + 1) * P],
                                               xdt[:, g, 2 * m + hh, :], mix[:, g, 2 * m + hh, :],
                                               start=True, stop=True)
                        mm.then_inc(y_done, 1)

                def mamba_tiles(i, buffer, before):
                    n = EB + 1 + 2 * i
                    slot = (EB + 1) % 2
                    pe.wait_ge(xs_copied, 2 * i + 2)
                    two_tiles(n, slot, xn, 0, xs_done)
                    if before:
                        mamba_outputs(i - 1)
                    for g in range(G):
                        pe.wait_ge(decay_ready, 4 * i + g + 1)
                        if g >= 2:
                            pe.wait_ge(decay_exp, 4 * i + g - 1)
                        pe.matmul(bank(6 + g % 2), constant("after"),
                                  decay_in[:, g, :, :].rearrange("p h t -> p (h t)"), start=True, stop=True
                                  ).then_inc(decay_sum, 1)
                    if before:
                        pe.wait_ge(gate_silu, 2 * i)
                    two_tiles(n + 1, 1 - slot, xn, 2, gate_done)
                    pe.wait_ge(conv_silu, 2 * i + 4)
                    if before:
                        pe.wait_ge(y_step, 8 * i - 6)
                    for m in range(2):
                        for g in range(G):
                            cols = slice(g * P, (g + 1) * P)
                            mm = pe.transpose(bank(4 + m)[:, cols], xs_t[:, buffer, m, cols], constant("ident"))
                    mm.then_inc(xs_turned, 1)

                for i in range(2):
                    mamba_tiles(i, i, i > 0)
                with pe.Fori(1, IT // 4) as i:
                    for j in range(2):
                        mamba_tiles(2 * i + j, j, True)
                mamba_outputs(IT // 2 - 1)
                pe.wait_ge(y_step, 4 * IT)
                pe.matmul(bank(3), constant("mean"), sq_sum[:, :], start=True, stop=True).then_inc(norm_sum, 1)
                open_sums()

                def output_chunk(c, j, last=False):
                    n = E_OUT + c
                    chunk_ready(n)
                    pe.wait_ge(gh_low, 2 * c + 2)
                    for kk in range(2):
                        for m in range(FT):
                            mm = product(bank(4 + m), tile_of((E_OUT + j) % 2, FT * kk + m),
                                         lambda part, kk=kk: gated_pair[:, 2 * (j % 2) + kk, part, :],
                                         stop=last and kk == 1)
                            if last and kk == 1 and m < FT - 1:
                                mm.then_inc(e_out, 1)
                    mm.then_inc(chunk_used, 1)

                with pe.Fori(0, 3) as i:
                    for j in range(2):
                        output_chunk(2 * i + j, j)
                output_chunk(6, 0)
                output_chunk(7, 1, True)

            if runs("F"):
                layer_norm(5)
                gate_logits(xc, small_at("f_gate").rearrange("p (k e) -> p k e", e=NE))
                chunk_ready(FB)
                wide(FB % 2, 0, xn, bank(7)).then_inc(chunk_used, 1)
                two_tiles(FB + 1, (FB + 1) % 2, xn, 0, first)
                two_tiles(FB + 2, FB % 2, xn, 2, second)
                turn_rows(2)
                pe.matmul(bank(4), constant("select_lora", NE), w_rows[:, :], start=True, stop=True
                          ).then_inc(lora_done, 1)
                spread_rows(2, SPREAD_0[2], NE)
                chunk_ready(FB + 3)
                pe.wait_ge(lora_in, 4)
                for m in range(FT):
                    mm = product(bank(4 + m), tile_of((FB + 3) % 2, m), lambda part: lora_pair[:, part, :],
                                 start=True)
                mm.then_inc(chunk_used, 1)

                def expert_f(e, n, slot):
                    pe.wait_ge(silu_done, 2 * (2 * NE + e))
                    two_tiles(n, slot, xn, 0, first)
                    pe.wait_ge(mid_step, 4 * (2 * NE + e))
                    two_tiles(n + 1, 1 - slot, xn, 2, second)
                    down(n + 2, slot, 2 * NE + e - 1)

                with pe.Fori(0, 3) as i:
                    for j in range(2):
                        expert_f(2 * i + j + 1, FB + 4 + 6 * i + 3 * j, (FB + 3 * j) % 2)
                expert_f(NE - 1, FB + 22, FB % 2)
                down(FB + 25, (FB + 25) % 2, 3 * NE - 1, True)

        @block.scalar
        def _(act):
            def layer_norm(k):
                for f in range(FT):
                    act.wait_ge(ln_centred, 4 * k + f + 1)
                    act.activation(sq[:, f, :], xc[:, f, :], ACT.Square).then_inc(ln_squared, 1)
                act.wait_ge(ln_var, k + 1)
                act.activation(rstd[:, :], bank(7), ACT.Ln, bias=eps[:, 0:1]).then_inc(ln_log, 1)
                act.wait_ge(ln_log, k + 1)
                act.activation(rstd[:, :], rstd[:, :], ACT.Exp, scale=-0.5).then_inc(ln_rstd, 1)
                for f in range(FT):
                    act.wait_ge(ln_normal, 4 * k + f + 1)
                    act.copy(xn[:, 0, f, :], xc[:, f, :]).then_inc(ln_high, 1)

            def attention_tile(u, f, q_at, v_at, rope):
                act.wait_ge(projected, q_at)
                act.mul((q_raw if rope else q_t)[:, :], bank(0), HD ** -0.5).then_inc(q_in, 1)
                act.wait_ge(chunk_used, v_at)
                act.copy(v_tok[:, :, :].rearrange("p g d -> p (g d)"), bank(2)).then_inc(v_in, 1)

                def exps(h):
                    act.wait_ge(maxed, HPT * u + h + 1)
                    for g in range(G):
                        act.activation(prob[:, h, g, :], bank(3 + h)[:, g * P:(g + 1) * P], ACT.Exp,
                                       bias=neg_max[:, h, g:g + 1], accum_out=row_sum[:, h, g:g + 1]
                                       ).then_inc(expd, 1)

                def turned_in(h):
                    act.wait_ge(prob_turned, HPT * u + h + 1)
                    act.copy(prob_t[:, h % 2, :, :].rearrange("p g k -> p (g k)"), bank(h % 2)).then_inc(prob_in, 1)

                exps(0)
                exps(1)
                exps(2)
                turned_in(0)
                exps(3)
                turned_in(1)
                turned_in(2)
                turned_in(3)
                act.wait_ge(attended, u + 1)
                act.copy(heads_out[:, 0, bass.ds(f, 1), :].rearrange("p a t -> p (a t)"), bank(7)
                         ).then_inc(heads_high, 1)

            act.wait_ge(setup, 7)
            layer_norm(0)
            with act.Fori(0, FT) as u:
                attention_tile(u, u, 2 * u + 1, u + 1, False)
            if runs("B"):
                layer_norm(1)
                with act.Fori(0, FT) as f:
                    attention_tile(FT + f, f, 2 * FT + f + 1, starts["B"] + 2 * f + 2, True)

            def spread_copies(first_spread, count, first_bank, targets):
                for e in range(count):
                    act.wait_ge(spread, first_spread + e + 1)
                    act.copy(targets(e), bank(first_bank(e))).then_inc(spread_in, 1)

            def gate_exps(p, steps):
                act.wait_ge(gate_step, GATE_0[p] + steps)
                act.activation(gate_s[:, 2, :, :], gate_s[:, 1, :, :], ACT.Exp).then_inc(gate_exp, 1)

            def expert_c(p, e):
                expert = NE * p + e
                up, sw = c_chunks(p, e)
                if not (isinstance(expert, int) and expert == 0):
                    act.wait_ge(mid_step, 4 * expert)
                for m in range(2):
                    act.wait_ge(first, expert + 1) if m == 0 else act.wait_ge(chunk_used, up + 1)
                    act.activation(hid[:, m, :], bank(m), ACT.Identity,
                                   bias=small_at("c_up_bias")[:, bass.ds(2 * e + m, 1)]).then_inc(hid_in, 1)
                for m in range(2):
                    act.wait_ge(second, expert + 1) if m == 0 else act.wait_ge(chunk_used, sw + 1)
                    act.activation(act_o[:, m, :], bank(2 + m), ACT.Silu,
                                   bias=small_at("c_sw_bias")[:, bass.ds(2 * e + m, 1)]).then_inc(silu_done, 1)

            if runs("C"):
                layer_norm(2)
                for p in range(2):
                    gate_exps(p, 3)
                    expert_c(p, 0)
                    spread_copies(SPREAD_0[p], GATED, lambda e: 5 + e % 2, lambda e: wide_w[:, e, :])
                    with act.Fori(1, NE) as e:
                        expert_c(p, e)

            if runs("D"):
                layer_norm(3)

                def latent_queries_in(h):
                    act.wait_ge(q_lat, h + 1)
                    act.copy(big[:, :].rearrange("p (b c) -> p b c", b=B)[:, :, bass.ds(h * S, S)],
                             by_batch(bank(7))).then_inc(q_lat_in, 1)

                def query_head(h, before):
                    act.wait_ge(hk_done, h + 1)
                    act.copy(hk_pair[:, 0, :], bank(0)).then_inc(hk_high, 1)
                    if before:
                        latent_queries_in(h - 1)
                    act.wait_ge(absorbed, h + 1)
                    act.copy(absorb_pair[:, 0, :], bank(0)[:, 0:QT * P]).then_inc(absorb_high, 1)
                    for k in range(QT):
                        act.wait_ge(turn_step, 3 * QT * h + 3 * k + 3)
                        act.copy(turned_pair[:, 0, k, :], by_cos[:, k, :]).then_inc(rope_high, 1)

                act.sem_inc(q_lat_in, 1)
                query_head(0, False)
                with act.Fori(1, XH) as h:
                    query_head(h, True)
                latent_queries_in(XH - 1)

                def keys_in(b, buffer, part):
                    act.wait_ge(keys_t, 4 * b + part + 1)
                    at, width = 512 * part, min(512, CTX - 512 * part)
                    act.copy(kv_t[:, buffer, 0, at:at + width], bank(7)[:, 0:width]).then_inc(keys_high, 1)
                    if part == 3:
                        act.copy(kv_t[:, buffer, 0, CTX:CTX + 1], bank(7)[:, width - 1:width]).then_inc(keys_high, 1)

                def unit_queries(i, k):
                    act.copy(q_pair[:, k % 2, 0, :], big[:, bass.ds(256 * (8 * i + k), 256)]).then_inc(qu_high, 1)

                def exps(i, k, r):
                    act.wait_ge(max_done, 2 * (8 * i + k) + r + 1)
                    buffer = k % 2
                    act.activation(expo[:, buffer, r, 0:800].rearrange("p (c n) -> p c n", c=2),
                                   psum[:, 0:2, 0:400], ACT.Exp, bias=neg_m[:, r:r + 1],
                                   accum_out=part_sum[:, r, 0:1]).then_inc(exp_done, 1)
                    for c in (2, 3):
                        at, width = ROW_CHUNKS[c]
                        act.activation(expo[:, buffer, r, at:at + width], bank(c)[:, 0:width], ACT.Exp,
                                       bias=neg_m[:, r:r + 1], accum_out=part_sum[:, r, c - 1:c]).then_inc(exp_done, 1)

                def exp_t_in(i, k, q):
                    act.wait_ge(exp_t, 7 * (8 * i + k) + q + 1)
                    rows, width = (P, 512) if q < 6 else (LASTK, 256)
                    act.copy(expo_t[0:rows, q % 3, 0, 0:width], bank(4 + q % 2)[0:rows, 0:width]
                             ).then_inc(exp_t_high, 1)

                def units(i, last):
                    for k in range(8):
                        ahead = k < 7 or not last
                        nxt = (i, k + 1) if k < 7 else (i + 1, 0)
                        turned_b = {2: (2 * i + 1, 1), 6: None if last else (2 * i + 2, 0)}.get(k)
                        keys = (lambda part: keys_in(*turned_b, part)) if turned_b else (lambda part: None)
                        keys(0)
                        exp_t_in(i, k, 0)
                        exp_t_in(i, k, 1)
                        keys(1)
                        if ahead:
                            exps(*nxt, 0)
                        exp_t_in(i, k, 2)
                        keys(2)
                        exp_t_in(i, k, 3)
                        keys(3)
                        exp_t_in(i, k, 4)
                        exp_t_in(i, k, 5)
                        if ahead:
                            exps(*nxt, 1)
                        exp_t_in(i, k, 6)
                        if k < 6:
                            unit_queries(i, k + 2)
                        elif not last:
                            unit_queries(i + 1, k - 6)
                        act.wait_ge(context_sum, 8 * i + k + 1)
                        act.wait_ge(context_done, 8 * i + k + 1)
                        act.copy(out_c[:, :], bank(6)[:, 0:256]).then_inc(context_in, 1)

                act.sem_inc(exp_done, 3)
                act.sem_inc(context_in, 1)
                act.wait_ge(q_lat_in, XH + 1)
                for k in range(2):
                    unit_queries(0, k)
                for part in range(4):
                    keys_in(0, 0, part)
                for r in range(2):
                    exps(0, 0, r)
                with act.Fori(0, B // 2 - 1) as i:
                    units(i, False)
                units(B // 2 - 1, True)

                def head_context(h, buffer):
                    act.copy(by_batch(ctx_pair[:, buffer, 0, :]),
                             big[:, :].rearrange("p (b c) -> p b c", b=B)[:, :, bass.ds(h * S, S)]
                             ).then_inc(ctx_high, 1)

                def latents_in(h, buffer):
                    if isinstance(h, int) and h == 0:
                        act.wait_ge(chunk_used, D3B + 1)
                    else:
                        act.wait_ge(lat_done, h)
                    act.copy(lat_pair[:, buffer, 0, :], bank(buffer)).then_inc(lat_high, 1)

                act.wait_ge(context_done, 4 * B + 1)
                head_context(0, 0)
                head_context(1, 1)
                latents_in(0, 0)
                head_context(2, 0)
                latents_in(1, 1)
                head_context(3, 1)
                with act.Fori(1, XH // 2 - 1) as i:
                    for j in range(2):
                        latents_in(2 * i + j, j)
                        head_context(2 * i + j + 2, j)
                for j in range(2):
                    latents_in(XH - 2 + j, j)

            if runs("E"):
                layer_norm(4)
                act.activation(exp_a[:, :], small_at("a_log"), ACT.Exp).then_inc(a_exp, 1)
                act.wait_ge(conv_pad, 1)

                def conv_input(m, earlier):
                    if earlier is not None:
                        act.wait_ge(conv_step, earlier)
                    act.copy(conv_in[:, m, :, CONV_K - 1:], by_batch(bank(m))).then_inc(xs_copied, 1)

                act.wait_ge(bc_done, 1)
                conv_input(0, None)
                act.wait_ge(chunk_used, EB + 1)
                conv_input(1, None)
                act.wait_ge(dt_step, 3)
                act.activation(dt_s[:, 3, :], dt_s[:, 2, :], ACT.Exp).then_inc(dt_exp, 1)
                act.wait_ge(dt_exp, 1)
                act.activation(dt_s[:, 4, :], dt_s[:, 3, :], ACT.Ln, bias=1.0).then_inc(dt_exp, 1)
                for m in range(2):
                    act.wait_ge(conv_step, 4 * m + 4)
                    act.activation(bc_t[:, m, :], conv_acc[:, m, :], ACT.Silu).then_inc(conv_silu, 1)

                def squares(i):
                    for m in range(2):
                        act.wait_ge(y_step, 8 * i + 3 + m)
                        act.activation(y_sq[:, m, :], y_gated[:, m, :], ACT.Square).then_inc(y_squared, 1)

                def mamba_tiles(i, buffer):
                    n = EB + 1 + 2 * i
                    for m in range(2):
                        act.wait_ge(xs_done, i + 1) if m == 0 else act.wait_ge(chunk_used, n + 1)
                        conv_input(m, 8 * i + 4 * m + 4)
                    for g in range(G):
                        act.wait_ge(decay_sum, 4 * i + g + 1)
                        if not (isinstance(i, int) and 4 * i + g < 2):
                            act.wait_ge(mixed, 4 * i + g - 1)
                        act.activation(decay[:, g % 2, :, :].rearrange("p h t -> p (h t)"), bank(6 + g % 2),
                                       ACT.Exp).then_inc(decay_exp, 1)
                    if not (isinstance(i, int) and i < 2):
                        act.wait_ge(y_step, 8 * i - 12)
                    for m in range(2):
                        act.wait_ge(conv_step, 8 * i + 4 * m + 12)
                        act.activation(xs_t[:, buffer, m, :], conv_acc[:, m, :], ACT.Silu).then_inc(conv_silu, 1)
                    for m in range(2):
                        act.wait_ge(gate_done, i + 1) if m == 0 else act.wait_ge(chunk_used, n + 2)
                        act.activation(silu_g[:, buffer, m, :], bank(2 + m), ACT.Silu).then_inc(gate_silu, 1)
                    if not (isinstance(i, int) and i == 0):
                        squares(i - 1)

                for i in range(2):
                    mamba_tiles(i, i)
                with act.Fori(1, IT // 4) as i:
                    for j in range(2):
                        mamba_tiles(2 * i + j, j)
                squares(IT // 2 - 1)

                def gated_high(c, j):
                    for kk in range(2):
                        act.copy(gated_pair[:, 2 * (j % 2) + kk, 0, :], big[:, bass.ds(T * (2 * c + kk), T)]
                                 ).then_inc(gh_high, 1)

                act.wait_ge(y_step, 4 * IT)
                gated_high(0, 0)
                gated_high(1, 1)
                act.wait_ge(norm_sum, 1)
                act.activation(rstd[:, :], bank(3), ACT.Ln, bias=eps[:, 0:1], scale=H / INNER).then_inc(norm_log, 1)
                act.wait_ge(norm_log, 1)
                act.activation(rstd[:, :], rstd[:, :], ACT.Exp, scale=-0.5).then_inc(norm_inv, 1)
                with act.Fori(1, 4) as i:
                    for j in range(2):
                        act.wait_ge(chunk_used, E_OUT + 2 * i + j - 1)
                        gated_high(2 * i + j, j)

            if runs("F"):
                layer_norm(5)
                gate_exps(2, 3)
                act.wait_ge(chunk_used, FB + 1)
                act.copy(lora_h[:, :], bank(7)).then_inc(lora_in, 1)

                def expert_f(e):
                    expert = 2 * NE + e
                    act.wait_ge(mid_step, 4 * expert)
                    for m in range(2):
                        act.wait_ge(first, expert + 1) if m == 0 else act.wait_ge(chunk_used, f_chunks(e)[0] + 1)
                        act.activation(act_o[:, m, :], bank(m), ACT.Silu).then_inc(silu_done, 1)

                expert_f(0)
                spread_copies(SPREAD_0[2], NE, lambda e: 5 + e % 2, lambda e: wide_w[:, e, :])
                with act.Fori(1, NE) as e:
                    expert_f(e)

        @block.vector
        def _(dve):
            def low(out, value, high):
                return dve.tensor_tensor(out, value, high.bitcast(F32), ALU.subtract)

            def layer_norm(k):
                dve.wait_ge(ln_mean, k + 1)
                for f in range(FT):
                    dve.tensor_tensor(xc[:, f, :], x[:, f, :], bank(6), ALU.subtract).then_inc(ln_centred, 1)
                dve.wait_ge(ln_rstd, k + 1)
                for f in range(FT):
                    dve.tensor_tensor(xc[:, f, :], xc[:, f, :], rstd[:, :], ALU.mult).then_inc(ln_normal, 1)
                for f in range(FT):
                    dve.wait_ge(ln_high, 4 * k + f + 1)
                    low(xn[:, 1, f, :], xc[:, f, :], xn[:, 0, f, :]).then_inc(ln_low, 1)

            def add_tile(m, k):
                dve.tensor_tensor(x[:, m, :], x[:, m, :], bank(k), ALU.add).then_inc(x_ready, 1)

            def add_projection(stage, n0):
                for c in range(2):
                    dve.wait_ge(out_done, 2 * stage + c + 1)
                    add_tile(2 * c, 2 * c)
                    dve.wait_ge(chunk_used, n0 + c + 1)
                    add_tile(2 * c + 1, 2 * c + 1)

            dve.memset(zero_b[:, :], 0.0).then_inc(setup, 1)
            dve.memset(eps[:, :], 1e-5).then_inc(setup, 1)
            dve.wait_ge(smalls_in, 32)
            dve.tensor_copy(ident_b[:, :], constant("ident")).then_inc(setup, 1)
            for n, name in enumerate(("causal", "batch")):
                dve.tensor_copy(mask_b[:, n, :, :], constant(name).unsqueeze(1).broadcast_to([P, G, P])).then_inc(setup, 1)
            dve.wait_ge(inputs_in, 32)
            dve.tensor_copy(first_pair[:, 0, :], first_raw[:, :]).then_inc(setup, 1)
            dve.wait_ge(setup, 6)
            low(first_pair[:, 1, :], first_raw[:, :], first_pair[:, 0, :]).then_inc(setup, 1)

            def rope(u, side, raw, arrived, out):
                at = 6 * (u - FT) + 3 * side
                dve.wait_ge(qk_turned, 2 * (u - FT) + side + 1)
                dve.tensor_tensor(by_batch(turned[:, side, :]), by_batch(bank(3 + side)),
                                  over_batches(constant("sin_b")), ALU.mult).then_inc(rope_steps, 1)
                dve.wait_ge(arrived, u + 1)
                dve.tensor_tensor(by_batch(out[:, :]), by_batch(raw[:, :]), over_batches(constant("cos_b")),
                                  ALU.mult).then_inc(rope_steps, 1)
                dve.wait_ge(rope_steps, at + 2)
                dve.tensor_tensor(out[:, :], out[:, :], turned[:, side, :], ALU.add).then_inc(rope_steps, 1)

            def attention_tile(u, f, k_at, with_rope):
                dve.wait_ge(*k_at)
                dve.tensor_copy((k_raw if with_rope else k_t)[:, :], bank(1)).then_inc(k_in, 1)
                if with_rope:
                    rope(u, 0, q_raw, q_in, q_t)
                    rope(u, 1, k_raw, k_in, k_t)

                def row_max(h):
                    dve.wait_ge(scores, HPT * u + h + 1)
                    dve.tensor_reduce(neg_max[:, h, :], bank(3 + h).rearrange("p (g k) -> p g k", g=G), AX_X,
                                      ALU.max, negate=True).then_inc(maxed, 1)

                def normalise(h):
                    dve.wait_ge(expd, G * (HPT * u + h) + G)
                    dve.reciprocal(row_inv[:, h, :], row_sum[:, h, :]).then_inc(row_inverted, 1)
                    dve.wait_ge(row_inverted, HPT * u + h + 1)
                    dve.tensor_tensor(prob[:, h, :, :], prob[:, h, :, :],
                                      row_inv[:, h, :].unsqueeze(2).broadcast_to([P, G, P]), ALU.mult
                                      ).then_inc(normal, 1)

                row_max(0)
                row_max(1)
                row_max(2)
                normalise(0)
                row_max(3)
                normalise(1)
                normalise(2)
                normalise(3)
                dve.wait_ge(heads_high, u + 1)
                tile = bass.ds(f, 1)
                dve.tensor_tensor(heads_out[:, 1, tile, :].rearrange("p a t -> p (a t)"), bank(7),
                                  heads_out[:, 0, tile, :].rearrange("p a t -> p (a t)").bitcast(F32),
                                  ALU.subtract).then_inc(heads_low, 1)
                dve.wait_ge(heads_low, u + 1)
                dve.sem_inc(heads_read, 1)

            dve.sem_inc(heads_read, 1)
            layer_norm(0)
            with dve.Fori(0, FT) as u:
                attention_tile(u, u, (projected, 2 * u + 2), False)
            add_projection(0, A_OUT)
            if runs("B"):
                layer_norm(1)
                with dve.Fori(0, FT) as f:
                    attention_tile(FT + f, f, (chunk_used, starts["B"] + 2 * f + 1), True)
                add_projection(1, B_OUT)

            class Steps:
                at = 0

                def __call__(self, ins):
                    ins.then_inc(gate_step, 1)
                    self.at += 1
                    dve.wait_ge(gate_step, self.at)

            step = Steps()

            def bcast(ap):
                return ap.broadcast_to([P, G, NE])

            def take_top(values, count, weights_in):
                theirs = values.unsqueeze(2).broadcast_to([P, G, NE, NE])
                own = values.unsqueeze(3).broadcast_to([P, G, NE, NE])
                lower = constant("lower").rearrange("p (e j) -> p e j", e=NE)
                step(dve.tensor_tensor(pairs_s[:, 0, :, :, :], theirs, own, ALU.is_gt))
                step(dve.tensor_tensor(pairs_s[:, 1, :, :, :], theirs, own, ALU.is_equal))
                step(dve.tensor_tensor(pairs_s[:, 1, :, :, :], pairs_s[:, 1, :, :, :],
                                       lower.unsqueeze(1).broadcast_to([P, G, NE, NE]), ALU.mult))
                step(dve.tensor_tensor(pairs_s[:, 0, :, :, :], pairs_s[:, 0, :, :, :], pairs_s[:, 1, :, :, :], ALU.add))
                step(dve.tensor_reduce(gate_s[:, 3, :, :], pairs_s[:, 0, :, :, :], AX_X, ALU.add))
                step(dve.scalar_tensor_tensor(out=gate_s[:, 4, :, :], in0=gate_s[:, 3, :, :], scalar=count - 0.5,
                                              in1=weights_in, op0=ALU.is_lt, op1=ALU.mult))

            def gate_c(p):
                first_b, _ = SMALLS["c_gate_bias"]
                bias = small[:, first_b + NE * p:first_b + NE * (p + 1)]
                dve.wait_ge(gated, p + 1)
                step(dve.tensor_tensor(gate_s[:, 0, :, :], bank(4)[:, 0:G * NE].rearrange("p (g e) -> p g e", e=NE),
                                       bias.unsqueeze(1).broadcast_to([P, G, NE]), ALU.add))
                step(dve.tensor_reduce(gate_col[:, 0, :, :], gate_s[:, 0, :, :], AX_X, ALU.max))
                step(dve.tensor_tensor(gate_s[:, 1, :, :], gate_s[:, 0, :, :], bcast(gate_col[:, 0, :, :]), ALU.subtract))
                dve.wait_ge(gate_exp, p + 1)
                take_top(gate_s[:, 0, :, :], GATED, gate_s[:, 2, :, :])
                step(dve.tensor_reduce(gate_col[:, 1, :, :], gate_s[:, 4, :, :], AX_X, ALU.add))
                step(dve.reciprocal(gate_col[:, 2, :, :], gate_col[:, 1, :, :]))
                step(dve.tensor_tensor(gate_s[:, 5, :, 0:GATED], gate_s[:, 4, :, 0:GATED],
                                       gate_col[:, 2, :, :].broadcast_to([P, G, GATED]), ALU.mult))

            def gate_f():
                dve.wait_ge(gated, 3)
                step(dve.tensor_copy(gate_s[:, 0, :, :], bank(4)[:, 0:G * NE].rearrange("p (g e) -> p g e", e=NE)))
                step(dve.tensor_reduce(gate_col[:, 0, :, :], gate_s[:, 0, :, :], AX_X, ALU.max))
                step(dve.tensor_tensor(gate_s[:, 1, :, :], gate_s[:, 0, :, :], bcast(gate_col[:, 0, :, :]), ALU.subtract))
                dve.wait_ge(gate_exp, 3)
                step(dve.tensor_reduce(gate_col[:, 1, :, :], gate_s[:, 2, :, :], AX_X, ALU.add))
                step(dve.reciprocal(gate_col[:, 2, :, :], gate_col[:, 1, :, :]))
                step(dve.tensor_tensor(gate_s[:, 6, :, :], gate_s[:, 2, :, :], bcast(gate_col[:, 2, :, :]), ALU.mult))
                take_top(gate_s[:, 6, :, :], 2, gate_s[:, 6, :, :])
                step(dve.tensor_reduce(gate_col[:, 1, :, :], gate_s[:, 4, :, :], AX_X, ALU.add))
                step(dve.tensor_scalar(gate_col[:, 2, :, :], gate_col[:, 1, :, :], 1e-9, None, ALU.max))
                step(dve.reciprocal(gate_col[:, 3, :, :], gate_col[:, 2, :, :]))
                step(dve.tensor_tensor(gate_s[:, 5, :, :], gate_s[:, 4, :, :], bcast(gate_col[:, 3, :, :]), ALU.mult))

            def rows_copy(p):
                dve.wait_ge(rows_turned, p + 1)
                dve.tensor_copy(w_rows[:, :], bank(5)[0:NE, :]).then_inc(rows_in, 1)

            def hidden(expert):
                for m in range(2):
                    dve.wait_ge(hid_in, 2 * expert + m + 1)
                    dve.tensor_copy(hid_pair[:, 0, m, :], hid[:, m, :]).then_inc(hid_high, 1)
                for m in range(2):
                    dve.wait_ge(hid_high, 2 * expert + m + 1)
                    low(hid_pair[:, 1, m, :], hid[:, m, :], hid_pair[:, 0, m, :]).then_inc(hid_low, 1)

            def middle(expert, e, other, down_before=None):
                wide_e = wide_w[:, bass.ds(e, 1), :].rearrange("p a t -> p (a t)")
                if not (isinstance(expert, int) and expert == 0):
                    dve.wait_ge(mid_low, 2 * expert)
                for m in range(2):
                    dve.wait_ge(silu_done, 2 * expert + m + 1)
                    dve.tensor_tensor(mid[:, m, :], act_o[:, m, :], other(m), ALU.mult).then_inc(mid_step, 1)
                for m in range(2):
                    dve.wait_ge(mid_step, 4 * expert + m + 1)
                    dve.tensor_tensor(mid[:, m, :], mid[:, m, :], wide_e, ALU.mult).then_inc(mid_step, 1)
                if down_before is not None:
                    dve.wait_ge(chunk_used, down_before + 1)
                for m in range(2):
                    dve.wait_ge(mid_step, 4 * expert + m + 3)
                    dve.tensor_copy(mid_pair[:, 0, m, :], mid[:, m, :]).then_inc(mid_high, 1)
                for m in range(2):
                    dve.wait_ge(mid_high, 2 * expert + m + 1)
                    low(mid_pair[:, 1, m, :], mid[:, m, :], mid_pair[:, 0, m, :]).then_inc(mid_low, 1)

            def sum_ready(p, m, last_chunk):
                dve.wait_ge(mixed_out, 3 * p + m + 1) if m < FT - 1 else dve.wait_ge(chunk_used, last_chunk + 1)

            if runs("C"):
                layer_norm(2)
                dve.memset(gate_s[:, 5, :, GATED:NE], 1.0)
                dve.memset(wide_w[:, GATED:NE, :], 1.0)
                for p in range(2):
                    gate_c(p)
                    hidden(NE * p)
                    rows_copy(p)
                    dve.wait_ge(spread_in, SPREAD_0[p] + GATED)
                    middle(NE * p, 0, lambda m: hid[:, m, :])
                    with dve.Fori(1, NE) as e:
                        hidden(NE * p + e)
                        middle(NE * p + e, e, lambda m: hid[:, m, :])
                    last_chunk = CB + 3 * NE * (p + 1) - 1
                    for m in range(FT):
                        sum_ready(p, m, last_chunk)
                        dve.tensor_tensor(sq[:, m, :], xc[:, m, :], bank(4 + m), ALU.add).then_inc(second_in, 1)
                    for m in range(FT):
                        dve.wait_ge(second_in, 3 * FT * p + m + 1)
                        if p == 0:
                            dve.tensor_copy(xn[:, 0, m, :], sq[:, m, :]).then_inc(second_in, 1)
                        else:
                            dve.tensor_tensor(x[:, m, :], x[:, m, :], sq[:, m, :], ALU.add).then_inc(x_ready, 1)
                    for m in range(FT if p == 0 else 0):
                        dve.wait_ge(second_in, FT + m + 1)
                        low(xn[:, 1, m, :], sq[:, m, :], xn[:, 0, m, :]).then_inc(second_in, 1)

            if runs("D"):
                layer_norm(3)
                cos_q = constant("cos_q").rearrange("p (k s) -> p k s", k=QT)
                sin_q = constant("sin_q").rearrange("p (k s) -> p k s", k=QT)

                def query_head(h):
                    dve.wait_ge(hk_high, h + 1)
                    low(hk_pair[:, 1, :], bank(0), hk_pair[:, 0, :]).then_inc(hk_low, 1)
                    dve.wait_ge(absorb_high, h + 1)
                    low(absorb_pair[:, 1, :], bank(0)[:, 0:QT * P], absorb_pair[:, 0, :]).then_inc(absorb_low, 1)
                    for k in range(QT):
                        dve.wait_ge(q_big, 2 * h + k + 1) if k < 2 else dve.wait_ge(chunk_used, DB + 2 * h + 1)
                        dve.tensor_tensor(by_batch(by_cos[:, k, :]), by_batch(bank(1 + k)),
                                          over_batches(cos_q[:, k, :]), ALU.mult).then_inc(turn_step, 1)
                        dve.wait_ge(q_turned, 2 * h + k + 1) if k < 2 else dve.wait_ge(chunk_used, DB + 2 * h + 2)
                        dve.tensor_tensor(by_batch(by_sin[:, k % 2, :]), by_batch(bank(1 + QT + k)),
                                          over_batches(sin_q[:, k, :]), ALU.mult).then_inc(turn_step, 1)
                        dve.wait_ge(turn_step, 3 * QT * h + 3 * k + 2)
                        dve.tensor_tensor(by_cos[:, k, :], by_cos[:, k, :], by_sin[:, k % 2, :], ALU.add
                                          ).then_inc(turn_step, 1)
                    for k in range(QT):
                        dve.wait_ge(rope_high, QT * h + k + 1)
                        low(turned_pair[:, 1, k, :], by_cos[:, k, :], turned_pair[:, 0, k, :]).then_inc(rope_low, 1)

                with dve.Fori(0, XH) as h:
                    query_head(h)

                def keys_in(b, buffer, part):
                    dve.wait_ge(keys_high, 5 * b + part + (1 if part < 3 else 2))
                    at, width = 512 * part, min(512, CTX - 512 * part)
                    ins = low(kv_t[:, buffer, 1, at:at + width], bank(7)[:, 0:width], kv_t[:, buffer, 0, at:at + width])
                    if part == 3:
                        ins = low(kv_t[:, buffer, 1, CTX:CTX + 1], bank(7)[:, width - 1:width],
                                  kv_t[:, buffer, 0, CTX:CTX + 1])
                    ins.then_inc(keys_low, 1)

                def unit_queries(i, k):
                    unit = 8 * i + k
                    dve.wait_ge(qu_high, unit + 1)
                    low(q_pair[:, k % 2, 1, :], big[:, bass.ds(256 * unit, 256)], q_pair[:, k % 2, 0, :]
                        ).then_inc(qu_low, 1)

                def row_max(i, k, r):
                    row = 2 * (8 * i + k) + r
                    for half in range(2):
                        dve.wait_ge(scored, 4 * row + 2 * half + 2)
                        dve.tensor_reduce(part_max[:, r, half:half + 1], psum[:, 2 * half:2 * half + 2, 0:402],
                                          mybir.AxisListType.XY, ALU.max).then_inc(max_part, 1)
                    dve.wait_ge(max_part, 2 * row + 2)
                    dve.tensor_reduce(neg_m[:, r:r + 1], part_max[:, r, :], AX_X, ALU.max, negate=True
                                      ).then_inc(max_done, 1)

                def row_scales(i, k):
                    unit = 8 * i + k
                    for r in range(2):
                        dve.wait_ge(exp_done, 6 * unit + 3 * r + 6)
                        dve.tensor_reduce(sums[:, r, 0:1], part_sum[:, r, :], AX_X, ALU.add).then_inc(summed, 1)
                    for r in range(2):
                        dve.wait_ge(summed, 2 * unit + r + 1)
                        dve.reciprocal(sums[:, r, 1:2], sums[:, r, 0:1]).then_inc(inverted, 1)
                    for r in range(2):
                        dve.wait_ge(inverted, 2 * unit + r + 1)
                        dve.tensor_scalar(diag[:, k % 2, r, :], constant("ident"), sums[:, r, 1:2], float(H),
                                          ALU.mult, ALU.mult).then_inc(diagonal, 1)

                def exp_t_in(i, k, q):
                    dve.wait_ge(exp_t_high, 7 * (8 * i + k) + q + 1)
                    rows, width = (P, 512) if q < 6 else (LASTK, 256)
                    low(expo_t[0:rows, q % 3, 1, 0:width], bank(4 + q % 2)[0:rows, 0:width],
                        expo_t[0:rows, q % 3, 0, 0:width]).then_inc(exp_t_low, 1)

                def units(i, last):
                    for k in range(8):
                        unit = 8 * i + k
                        ahead = k < 7 or not last
                        nxt = (i, k + 1) if k < 7 else (i + 1, 0)
                        turned_b = {2: (2 * i + 1, 1), 6: None if last else (2 * i + 2, 0)}.get(k)
                        keys = (lambda part: keys_in(*turned_b, part)) if turned_b else (lambda part: None)
                        if ahead:
                            row_max(*nxt, 0)
                        keys(0)
                        exp_t_in(i, k, 0)
                        exp_t_in(i, k, 1)
                        keys(1)
                        exp_t_in(i, k, 2)
                        keys(2)
                        exp_t_in(i, k, 3)
                        keys(3)
                        if ahead:
                            row_max(*nxt, 1)
                        exp_t_in(i, k, 4)
                        exp_t_in(i, k, 5)
                        exp_t_in(i, k, 6)
                        if ahead:
                            row_scales(*nxt)
                        if k < 6:
                            unit_queries(i, k + 2)
                        elif not last:
                            unit_queries(i + 1, k - 6)
                        dve.wait_ge(scale_out, unit + 1)
                        dve.wait_ge(context_in, unit + 2)
                        dve.tensor_tensor(big[:, bass.ds(256 * unit, 256)], out_c[:, :], bank(7)[:, 0:256],
                                          ALU.mult).then_inc(context_done, 1)

                dve.sem_inc(keys_low, 1)
                dve.sem_inc(context_done, 1)
                for k in range(2):
                    unit_queries(0, k)
                for part in range(4):
                    keys_in(0, 0, part)
                for r in range(2):
                    row_max(0, 0, r)
                row_scales(0, 0)
                with dve.Fori(0, B // 2 - 1) as i:
                    units(i, False)
                units(B // 2 - 1, True)

                def head_context(h, buffer):
                    dve.wait_ge(ctx_high, h + 1)
                    dve.tensor_tensor(by_batch(ctx_pair[:, buffer, 1, :]),
                                      big[:, :].rearrange("p (b c) -> p b c", b=B)[:, :, bass.ds(h * S, S)],
                                      by_batch(ctx_pair[:, buffer, 0, :]).bitcast(F32), ALU.subtract
                                      ).then_inc(ctx_low, 1)

                def latents_in(h, buffer):
                    dve.wait_ge(lat_high, h + 1)
                    low(lat_pair[:, buffer, 1, :], bank(buffer), lat_pair[:, buffer, 0, :]).then_inc(lat_low, 1)

                head_context(0, 0)
                head_context(1, 1)
                with dve.Fori(0, XH // 2 - 1) as i:
                    for j in range(2):
                        latents_in(2 * i + j, j)
                        head_context(2 * i + j + 2, j)
                for j in range(2):
                    latents_in(XH - 2 + j, j)
                for m in range(FT):
                    dve.wait_ge(d_out, m + 1) if m < FT - 1 else dve.wait_ge(chunk_used, D3B + XH + 1)
                    add_tile(m, 4 + m)

            if runs("E"):
                layer_norm(4)
                upto = constant("upto")
                conv_w, conv_b = small_at("conv_w"), small_at("conv_b")
                dve.memset(sq_sum[:, :], 0.0)
                dve.memset(conv_in[:, :, :, 0:CONV_K - 1], 0.0).then_inc(conv_pad, 1)

                def convolve(v, m, tile):
                    acc = by_batch(conv_acc[:, m, :])
                    dve.wait_ge(xs_copied, v + 1)
                    if not (isinstance(v, int) and v < 2):
                        dve.wait_ge(conv_silu, v - 1)
                    dve.tensor_scalar(acc, conv_in[:, m, :, 0:S], conv_w[:, bass.ds(CONV_K * tile, 1)],
                                      conv_b[:, bass.ds(tile, 1)], ALU.mult, ALU.add).then_inc(conv_step, 1)
                    for t in range(1, CONV_K):
                        dve.wait_ge(conv_step, 4 * v + t)
                        dve.scalar_tensor_tensor(out=acc, in0=conv_in[:, m, :, t:t + S],
                                                 scalar=conv_w[:, bass.ds(CONV_K * tile + t, 1)], in1=acc,
                                                 op0=ALU.mult, op1=ALU.add).then_inc(conv_step, 1)

                def heads(ap):
                    return ap.rearrange("p (g h) -> p g h", h=MH)

                dt, a = heads(dt_s[:, 0, :]), heads(dt_s[:, 1, :])
                dve.wait_ge(dt_done, 1)
                dve.tensor_tensor(dt, heads(bank(2)[:, 0:G * MH]), small_at("dt_bias").unsqueeze(1).broadcast_to([P, G, MH]),
                                  ALU.add).then_inc(dt_step, 1)
                dve.wait_ge(dt_step, 1)
                dve.tensor_scalar(dt_s[:, 1, :], dt_s[:, 0, :], 0.0, None, ALU.max).then_inc(dt_step, 1)
                dve.scalar_tensor_tensor(out=dt_s[:, 2, :], in0=dt_s[:, 0, :], scalar=-1.0, in1=dt_s[:, 0, :],
                                         op0=ALU.mult, op1=ALU.min).then_inc(dt_step, 1)
                convolve(0, 0, IT)
                convolve(1, 1, IT + 1)
                dve.wait_ge(dt_exp, 2)
                dve.wait_ge(dt_step, 3)
                dve.tensor_tensor(dt_s[:, 0, :], dt_s[:, 1, :], dt_s[:, 4, :], ALU.add).then_inc(dt_step, 1)
                dve.wait_ge(dt_step, 4)
                dve.wait_ge(a_exp, 1)
                dve.scalar_tensor_tensor(out=a, in0=dt, scalar=-1.0, in1=exp_a[:, :].unsqueeze(1).broadcast_to([P, G, MH]),
                                         op0=ALU.mult, op1=ALU.mult).then_inc(dt_step, 1)
                dve.wait_ge(dt_step, 5)
                dve.wait_ge(g_done, 1)
                dve.tensor_tensor(g_mask[:, :, :], bank(3).rearrange("p (g t) -> p g t", g=G),
                                  upto.unsqueeze(1).broadcast_to([P, G, P]), ALU.mult).then_inc(g_masked, 1)

                def outputs_a(i, buffer):
                    for m in range(2):
                        dve.wait_ge(y_done, 2 * i + m + 1)
                        dve.scalar_tensor_tensor(out=y_sum[:, m, :], in0=xs_t[:, buffer, m, :],
                                                 scalar=small_at("skip")[:, bass.ds(2 * i + m, 1)], in1=bank(4 + m),
                                                 op0=ALU.mult, op1=ALU.add).then_inc(y_step, 1)
                    for m in range(2):
                        dve.wait_ge(y_step, 8 * i + m + 1)
                        dve.wait_ge(gate_silu, 2 * i + m + 1)
                        dve.tensor_tensor(y_gated[:, m, :], y_sum[:, m, :], silu_g[:, buffer, m, :], ALU.mult
                                          ).then_inc(y_step, 1)

                def outputs_b(i):
                    for m in range(2):
                        dve.wait_ge(y_step, 8 * i + m + 3)
                        dve.tensor_scalar(big[:, bass.ds(T * (2 * i + m), T)], y_gated[:, m, :],
                                          small_at("norm_w")[:, bass.ds(2 * i + m, 1)], None, ALU.mult
                                          ).then_inc(y_step, 1)
                    for m in range(2):
                        dve.wait_ge(y_squared, 2 * i + m + 1)
                        dve.wait_ge(y_step, 8 * i + m + 6)
                        dve.tensor_tensor(sq_sum[:, :], sq_sum[:, :], y_sq[:, m, :], ALU.add).then_inc(y_step, 1)

                def mamba_tiles(i, buffer):
                    for g in range(G):
                        dve.tensor_tensor(decay_in[:, g, :, :], upto.unsqueeze(1).broadcast_to([P, 4, P]),
                                          a[:, g, bass.ds(4 * i, 4)].unsqueeze(2).broadcast_to([P, 4, P]), ALU.mult
                                          ).then_inc(decay_ready, 1)
                    for m in range(2):
                        convolve(2 * i + m + 2, m, 2 * i + m)
                    if not (isinstance(i, int) and i == 0):
                        outputs_a(i - 1, 1 - buffer)
                    for g in range(G):
                        dve.wait_ge(decay_exp, 4 * i + g + 1)
                        dve.tensor_tensor(mix[:, g, :, :], decay[:, g % 2, :, :],
                                          g_mask[:, g, :].unsqueeze(1).broadcast_to([P, 4, P]), ALU.mult
                                          ).then_inc(mixed, 1)
                    dve.wait_ge(xs_turned, i + 1)
                    for m in range(2):
                        dve.tensor_tensor(xdt[:, :, 2 * m:2 * m + 2, :],
                                          bank(4 + m).rearrange("p (g h d) -> p g h d", g=G, h=2),
                                          dt[:, :, bass.ds(4 * i + 2 * m, 2)].unsqueeze(3).broadcast_to([P, G, 2, MP]),
                                          ALU.mult).then_inc(xdt_ready, 1)
                    if not (isinstance(i, int) and i == 0):
                        outputs_b(i - 1)

                for i in range(2):
                    mamba_tiles(i, i)
                with dve.Fori(1, IT // 4) as i:
                    for j in range(2):
                        mamba_tiles(2 * i + j, j)
                outputs_a(IT // 2 - 1, 1)
                outputs_b(IT // 2 - 1)

                def gated_low(c, j):
                    for kk in range(2):
                        dve.wait_ge(gh_high, 2 * c + kk + 1)
                        buffer = 2 * (j % 2) + kk
                        low(gated_pair[:, buffer, 1, :], big[:, bass.ds(T * (2 * c + kk), T)],
                            gated_pair[:, buffer, 0, :]).then_inc(gh_low, 1)

                with dve.Fori(0, 4) as i:
                    for j in range(2):
                        gated_low(2 * i + j, j)
                dve.wait_ge(norm_inv, 1)
                for m in range(FT):
                    dve.wait_ge(e_out, m + 1) if m < FT - 1 else dve.wait_ge(chunk_used, E_OUT + 8)
                    if m >= 2:
                        dve.wait_ge(x_ready, 4 * 4 + m - 1)
                    dve.tensor_tensor(y_sum[:, m % 2, :], bank(4 + m), rstd[:, :], ALU.mult).then_inc(e_scaled, 1)
                    dve.wait_ge(e_scaled, m + 1)
                    dve.tensor_tensor(x[:, m, :], x[:, m, :], y_sum[:, m % 2, :], ALU.add).then_inc(x_ready, 1)

            if runs("F"):
                layer_norm(5)
                gate_f()
                rows_copy(2)
                dve.wait_ge(lora_in, 1)
                dve.wait_ge(lora_done, 1)
                dve.tensor_tensor(lora_w[:, :], lora_h[:, :], bank(4), ALU.mult).then_inc(lora_in, 1)
                dve.wait_ge(lora_in, 2)
                dve.tensor_copy(lora_pair[:, 0, :], lora_w[:, :]).then_inc(lora_in, 1)
                dve.wait_ge(lora_in, 3)
                low(lora_pair[:, 1, :], lora_w[:, :], lora_pair[:, 0, :]).then_inc(lora_in, 1)

                def expert_f(e):
                    if not isinstance(e, int):
                        dve.wait_ge(second, 2 * NE + e + 1)
                    dve.wait_ge(chunk_used, f_chunks(e)[1] + 1)
                    middle(2 * NE + e, e, lambda m: bank(2 + m),
                           None if isinstance(e, int) else f_chunks(e)[1] + 1)

                dve.wait_ge(spread_in, SPREAD_0[2] + NE)
                expert_f(0)
                with dve.Fori(1, NE) as e:
                    expert_f(e)
                for m in range(FT):
                    sum_ready(2, m, FB + 25)
                    add_tile(m, 4 + m)


STAGES = ("A", "B", "C", "D", "E", "F")
LAST_STAGE = "F"


def kernel(**inputs):
    import concourse.bacc as bacc
    from concourse.bass_utils import run_bass_kernel_spmd

    nc = bacc.Bacc("TRN2", target_bir_lowering=False, num_devices=1)
    arrays = lay_out({name: np.asarray(a) for name, a in inputs.items()})
    order = ("x", "ctx_first", "ctx", "weights", "small", "constants", "rope_k")
    args = [nc.dram_tensor(f"in_{name}", arrays[name].shape, F32, kind="ExternalInput").ap() for name in order]
    out = nc.dram_tensor("out", (P, FT, T), F32, kind="ExternalOutput").ap()
    perceiver_stack(nc, *args, out)
    r = run_bass_kernel_spmd(nc, [{f"in_{name}": arrays[name] for name in order}], core_ids=[0])
    return np.ascontiguousarray(r.results[0]["out"].transpose(2, 1, 0).reshape(B, S, H))
```

```python
from contextlib import ExitStack

import numpy as np

import concourse.bass as bass
from concourse import mybir

F32 = mybir.dt.float32
F32R = mybir.dt.float32r
BF16 = mybir.dt.bfloat16
ALU = mybir.AluOpType
ACT = mybir.ActivationFunctionType
AX_X = mybir.AxisListType.X

P = 128
B, S, H = 8, 64, 512
T = B * S
FT = H // P
G = T // P
CTX, CD = 1601, 128
NH, HD = 16, 32
HPT = P // HD
NE = 8
GATED = 6
FF = 256
XH, XQ, XR = 16, 384, 64
QT = XQ // P
KT = 13
LASTK = CTX - (KT - 1) * P
MH, MP, MN = 32, 64, 128
INNER = MH * MP
IT = INNER // P
CONV_K = 4
LORA = 16
MASKED = -1e30
CHUNK = 8 * P


def stream_plan():
    up, down, half = CHUNK, CHUNK, CHUNK // 2
    plan = [("A", (6 * P, 6 * P), 2), ("A", (CHUNK, CHUNK), 1),
            ("B", (CHUNK, half), 4), ("B", (CHUNK, CHUNK), 1)]
    for _ in range(2):
        plan += [("C", (up, half), 1), ("C", (up, down, half) * 2, 3), ("C", (up, down, half, down), 1)]
    plan += [("D1", (CHUNK, 6 * P), XH),
             ("D3", (P,), 1), ("D3", (5 * P, 5 * P), 7), ("D3", (5 * P, 4 * P), 1),
             ("E", (CHUNK,), 1), ("E", (CHUNK, CHUNK), IT // 2), ("E", (CHUNK, CHUNK), 4),
             ("F", (half, CHUNK, CHUNK, half), 1), ("F", (CHUNK,) * 6, 3), ("F", (CHUNK,) * 4, 1)]
    return plan


def plan_starts():
    starts, n = {}, 0
    for stage, widths, reps in stream_plan():
        starts.setdefault(stage, n)
        n += len(widths) * reps
    starts["end"] = n
    return starts


def offsets(fields):
    at, found = 0, {}
    for name, width in fields:
        found[name] = (at, width)
        at += width
    return found, at


CONSTANTS, CONSTANT_COLS = offsets([
    ("ident", P), ("mean", P), ("rope", P), ("causal", P), ("batch", P), ("upto", P), ("after", P),
    ("cos_b", S), ("sin_b", S), ("cos_q", QT * S), ("sin_q", QT * S),
    ("lower", NE * NE), ("select", NE * P), ("select_lora", P)])
SMALLS, SMALL_COLS = offsets([
    ("c_gate", 2 * FT * NE), ("c_gate_bias", 2 * NE), ("c_up_bias", NE * 2), ("c_sw_bias", NE * 2),
    ("c_down_bias", H), ("f_gate", FT * NE), ("dt_w", FT * MH), ("dt_bias", MH), ("a_log", MH),
    ("conv_w", (IT + 2) * CONV_K), ("conv_b", IT + 2), ("skip", IT), ("norm_w", IT)])


def shape_constants():
    c = np.zeros((P, CONSTANT_COLS), np.float32)

    def put(name, a):
        first, width = CONSTANTS[name]
        c[:a.shape[0], first:first + width] = a.reshape(a.shape[0], width)

    i = np.arange(P)
    same = i[:, None] // S == i[None, :] // S
    put("ident", np.eye(P, dtype=np.float32))
    put("mean", np.full((P, P), 1.0 / H, np.float32))
    rope = np.zeros((P, P), np.float32)
    rope[i[1::2], i[0::2]] = -1.0
    rope[i[0::2], i[1::2]] = 1.0
    put("rope", rope)
    put("causal", np.where(same & (i[None, :] <= i[:, None]), 0.0, MASKED).astype(np.float32))
    put("batch", np.where(same, 0.0, MASKED).astype(np.float32))
    put("upto", (same & (i[:, None] <= i[None, :])).astype(np.float32))
    put("after", (same & (i[:, None] > i[None, :])).astype(np.float32))

    def angles(n, dim):
        exponent = (np.arange(0, dim, 2, dtype=np.float32) / np.float32(dim)).astype(np.float64)
        inv = np.float32(1.0) / (10000.0 ** exponent).astype(np.float32)
        f = np.arange(n, dtype=np.float32)[:, None] * inv[None, :]
        return np.repeat(f, 2, axis=1)

    fb = np.tile(angles(S, HD).T, (HPT, 1))
    put("cos_b", np.cos(fb))
    put("sin_b", np.sin(fb))
    fq = angles(S, XQ).T
    sign_q = np.where(np.arange(XQ) < XQ // 2, -1.0, 1.0).astype(np.float32)[:, None]
    tiles = lambda a: a.reshape(QT, P, S).transpose(1, 0, 2)
    put("cos_q", tiles(np.cos(fq)))
    put("sin_q", tiles(np.sin(fq) * sign_q))
    e = np.arange(NE)
    put("lower", np.broadcast_to((e[None, :] < e[:, None]).astype(np.float32).reshape(1, -1), (P, NE * NE)))
    put("select", np.repeat(np.eye(NE, dtype=np.float32), P, axis=1))
    put("select_lora", np.where(i[None, :] // LORA == e[:, None], 2.0, 0.0).astype(np.float32))
    fk = angles(KT * P, CD)
    sign_k = np.where(np.arange(CD) < CD // 2, -1.0, 1.0).astype(np.float32)[None, :]
    by_tile = lambda a: np.ascontiguousarray(a.reshape(KT, P, CD).transpose(1, 0, 2))
    return c, np.stack([by_tile(np.cos(fk)), by_tile(np.sin(fk) * sign_k)]).astype(np.float32)


def lay_out(i):
    def tile(w, k, m):
        return w[k * P:(k + 1) * P, m * P:(m + 1) * P]

    def rows(a):
        return np.concatenate([a, np.zeros((P - a.shape[0], a.shape[1]), a.dtype)]) if a.shape[0] < P else a

    chunks = []

    def chunk(*tiles):
        chunks.append(np.concatenate(tiles, axis=1))

    wq, wkv, wo = i["L0_xattn_Wq"].T, i["L0_xattn_Wkv_expand"].T, i["L0_xattn_Wout"].T
    for f in range(FT):
        chunk(*[tile(wq, k, f) for k in range(FT)], tile(wkv, 0, f), tile(wkv, 0, FT + f))

    def projection(w):
        for m in range(0, FT, 2):
            chunk(*[tile(w, k, n) for n in (m, m + 1) for k in range(FT)])

    projection(wo)
    w = i["L0_attn_w_qkv"]
    for f in range(FT):
        chunk(*[tile(w, k, o + f) for o in (0, FT) for k in range(FT)])
        chunk(*[tile(w, k, 2 * FT + f) for k in range(FT)])
    projection(i["L0_attn_w_proj"])

    def up_c(e):
        w, o = (i["L0_ffn_Wup"][e], 0) if e < GATED else (i["L0_ffn_Wsu"], 2 * (e - GATED))
        chunk(*[tile(w, k, o + m) for m in range(2) for k in range(FT)])

    def sw_c(e):
        w = i["L0_ffn_Wsw"][e] if e < GATED else i["L0_ffn_Wsa"]
        chunk(*[tile(w, k, m) for m in range(2) for k in range(2)])

    def down_c(e):
        w = i["L0_ffn_Wdn"][e] if e < GATED else i["L0_ffn_Wsd"][(e - GATED) * FF:(e - GATED + 1) * FF]
        chunk(*[tile(w, k, m) for m in range(FT) for k in range(2)])

    for _ in range(2):
        up_c(0)
        sw_c(0)
        for e in range(1, NE):
            up_c(e)
            down_c(e - 1)
            sw_c(e)
        down_c(NE - 1)

    wq = i["L1_xattn_Wq"].T
    turn = (np.arange(XQ) + XQ // 2) % XQ
    for h in range(XH):
        kc = i["L1_xattn_w_kc_q"][h]
        chunk(*[tile(wq, k, h) for k in range(FT)], kc, rows(i["L1_xattn_W_kr"][h].T))
        chunk(kc[:, turn], rows(i["L1_xattn_W_qr"][h].T))
    wo = i["L1_xattn_Wo"].T
    lat = lambda h: i["L1_xattn_w_kc_kv"][h].T
    out = lambda h: [tile(wo, h, m) for m in range(FT)]
    chunk(lat(0))
    for h in range(1, XH):
        chunk(lat(h), *out(h - 1))
    chunk(*out(XH - 1))

    w = i["L1_attn_W_in"].T
    four = lambda m: [tile(w, k, m) for k in range(FT)]
    chunk(*four(2 * IT), *four(2 * IT + 1))
    for m in range(0, IT, 2):
        chunk(*four(IT + m), *four(IT + m + 1))
        chunk(*four(m), *four(m + 1))
    wo = i["L1_attn_W_out"].T
    for k in range(0, IT, 2):
        chunk(*[tile(wo, n, m) for n in (k, k + 1) for m in range(FT)])

    lora_a = i["L1_ffn_A"].transpose(1, 0, 2).reshape(H, NE * LORA)
    lora_b = i["L1_ffn_B"].reshape(NE * LORA, H)
    chunk(*[tile(lora_a, k, 0) for k in range(FT)])
    wide = lambda w: chunk(*[tile(w, k, m) for m in range(2) for k in range(FT)])
    deep = lambda w: chunk(*[tile(w, k, m) for m in range(FT) for k in range(2)])
    wide(i["L1_ffn_Wg"][0])
    wide(i["L1_ffn_Wu"][0])
    chunk(lora_b)
    for e in range(1, NE):
        wide(i["L1_ffn_Wg"][e])
        wide(i["L1_ffn_Wu"][e])
        deep(i["L1_ffn_Wd"][e - 1])
    deep(i["L1_ffn_Wd"][NE - 1])

    widths = [w for _, body, reps in stream_plan() for _ in range(reps) for w in body]
    assert [c.shape for c in chunks] == [(P, w) for w in widths]
    stream = np.concatenate([np.ascontiguousarray(c).reshape(-1) for c in chunks])

    small = np.zeros((P, SMALL_COLS), np.float32)

    def put(name, a):
        first, width = SMALLS[name]
        small[:a.shape[0], first:first + width] = a.reshape(a.shape[0], width)

    every = lambda a: np.broadcast_to(a.reshape(1, -1), (P, a.size))
    put("c_gate", i["L0_ffn_Wg"].reshape(2, FT, P, NE).transpose(2, 0, 1, 3))
    put("c_gate_bias", every(i["L0_ffn_bg"]))
    up_bias = np.concatenate([i["L0_ffn_bup"], i["L0_ffn_bsu"].reshape(2, FF)])
    sw_bias = np.concatenate([i["L0_ffn_bsw"], i["L0_ffn_bsa"][None], i["L0_ffn_bsa"][None]])
    put("c_up_bias", up_bias.reshape(NE, 2, P).transpose(2, 0, 1))
    put("c_sw_bias", sw_bias.reshape(NE, 2, P).transpose(2, 0, 1))
    put("c_down_bias", np.concatenate([i["L0_ffn_bdn"], i["L0_ffn_bsd"][None], np.zeros((1, H), np.float32)]))
    put("f_gate", i["L1_ffn_gate_w"].reshape(FT, P, NE).transpose(1, 0, 2))
    put("dt_w", np.ascontiguousarray(w[:, 2 * INNER + 2 * MN:]).reshape(FT, P, MH).transpose(1, 0, 2))
    put("dt_bias", every(i["L1_attn_dt_bias"]))
    put("a_log", every(i["L1_attn_A_log"]))
    put("conv_w", i["L1_attn_conv_w"].reshape(IT + 2, P, CONV_K).transpose(1, 0, 2))
    put("conv_b", i["L1_attn_conv_b"].reshape(IT + 2, P).T)
    put("skip", np.repeat(i["L1_attn_D_param"], MP).reshape(IT, P).T)
    put("norm_w", i["L1_attn_norm_w"].reshape(IT, P).T)

    constants, rope_k = shape_constants()
    ctx = i["ctx_512"]
    tiles = np.concatenate([ctx, np.zeros((B, KT * P - CTX, CD), np.float32)], axis=1)
    return {
        "x": np.ascontiguousarray(i["x"].reshape(T, FT, P).transpose(2, 1, 0)),
        "ctx_first": np.ascontiguousarray(ctx[:, :S].reshape(T, CD).T),
        "ctx": np.ascontiguousarray(tiles.reshape(B, KT, P, CD).transpose(0, 2, 1, 3)),
        "weights": stream, "small": small, "constants": constants, "rope_k": rope_k,
    }


def perceiver_stack(nc, x_in, ctx_first, ctx_in, weights, small_in, constants_in, rope_k_in, x_out):
    starts = plan_starts()
    last_stage = LAST_STAGE

    with ExitStack() as held:
        def sb(name, shape, dt=F32, scope=None):
            return (scope or held).enter_context(nc.sbuf_tensor(name, shape, dt))

        def sem(name):
            return held.enter_context(nc.semaphore(name))

        x = sb("x", [P, FT, T])
        landing = sb("landing", [P, 2, CHUNK])
        wpair = sb("wpair", [P, 2, 2, CHUNK], F32R)
        const = sb("const", [P, CONSTANT_COLS])
        small = sb("small", [P, SMALL_COLS])
        eps = sb("eps", [P, 1])
        zero_b = sb("zero_b", [P, T], BF16)
        big = sb("big", [P, B * XH * S])
        psum = held.enter_context(nc.psum_tensor("psum", [P, 8, 512], F32))

        def bank(k):
            return psum[:, k, :]

        def by_batch(ap):
            return ap.rearrange("p (b s) -> p b s", s=S)

        def over_batches(ap):
            return ap.unsqueeze(1).broadcast_to([P, B, S])

        def constant(name, rows=P):
            first, width = CONSTANTS[name]
            return const[0:rows, first:first + width]

        def small_at(name, rows=P):
            first, width = SMALLS[name]
            return small[0:rows, first:first + width]

        ln_scope = ExitStack()
        xn = sb("xn", [P, 2, FT, T], F32R, ln_scope)
        xc = sb("xc", [P, FT, T], F32, ln_scope)
        sq = sb("sq", [P, FT, T], F32, ln_scope)
        rstd = sb("rstd", [P, T], F32, ln_scope)

        with ExitStack() as scope:
            first_pair = sb("first_pair", [P, 2, T], F32R, scope)
            first_raw = sb("first_raw", [P, T], F32, scope)
            ident_b = sb("ident_b", [P, P], BF16, scope)
            mask_b = sb("mask_b", [P, 2, G, P], BF16, scope)
            q_raw = sb("q_raw", [P, T], F32, scope)
            k_raw = sb("k_raw", [P, T], F32, scope)
            q_t = sb("q_t", [P, T], F32, scope)
            k_t = sb("k_t", [P, T], F32, scope)
            turned = sb("turned", [P, 2, T], F32, scope)
            v_tok = sb("v_tok", [P, G, P], F32, scope)
            prob = sb("prob", [P, HPT, G, P], F32, scope)
            prob_t = sb("prob_t", [P, 2, G, P], F32, scope)
            neg_max = sb("neg_max", [P, HPT, G], F32, scope)
            row_sum = sb("row_sum", [P, HPT, G], F32, scope)
            row_inv = sb("row_inv", [P, HPT, G], F32, scope)
            heads_out = sb("heads_out", [P, 2, FT, T], F32R, scope)
        with ExitStack() as scope:
            wide_w = sb("wide_w", [P, NE, T], F32, scope)
            gate_s = sb("gate_s", [P, 8, G, NE], F32, scope)
            pairs_s = sb("pairs_s", [P, 2, G, NE, NE], F32, scope)
            gate_col = sb("gate_col", [P, 4, G, 1], F32, scope)
            w_rows = sb("w_rows", [NE, T], F32, scope)
            hid = sb("hid", [P, 2, T], F32, scope)
            hid_pair = sb("hid_pair", [P, 2, 2, T], F32R, scope)
            act_o = sb("act_o", [P, 2, T], F32, scope)
            mid = sb("mid", [P, 2, T], F32, scope)
            mid_pair = sb("mid_pair", [P, 2, 2, T], F32R, scope)
            lora_h = sb("lora_h", [P, T], F32, scope)
            lora_w = sb("lora_w", [P, T], F32, scope)
            lora_pair = sb("lora_pair", [P, 2, T], F32R, scope)
        with ExitStack() as scope:
            hk_pair = sb("hk_pair", [P, 2, T], F32R, scope)
            by_cos, by_sin = sq, xc
            turned_pair = sb("turned_pair", [P, 2, 2, QT, T], F32R, scope)
            absorb_pair = sb("absorb_pair", [P, 2, 2, QT * P], F32R, scope)
        with ExitStack() as scope:
            conv_in = sb("conv_in", [P, 2, B, S + CONV_K - 1], F32, scope)
            conv_acc = sb("conv_acc", [P, 2, T], F32, scope)
            bc_t = sb("bc_t", [P, 2, T], F32, scope)
            dt_s = sb("dt_s", [P, 5, G * MH], F32, scope)
            exp_a = sb("exp_a", [P, MH], F32, scope)
            g_mask = sb("g_mask", [P, G, P], F32, scope)
            xs_t = sb("xs_t", [P, 2, 2, T], F32, scope)
            silu_g = sb("silu_g", [P, 2, 2, T], F32, scope)
            decay_in = sb("decay_in", [P, G, 4, P], F32, scope)
            decay = sb("decay", [P, 2, 4, P], F32, scope)
            mix = sb("mix", [P, G, 4, P], F32, scope)
            xdt = sb("xdt", [P, G, 4, MP], F32, scope)
            y_sum = sb("y_sum", [P, 2, T], F32, scope)
            y_gated = sb("y_gated", [P, 2, T], F32, scope)
            y_sq = sb("y_sq", [P, 2, T], F32, scope)
            sq_sum = sb("sq_sum", [P, T], F32, scope)
            gated_pair = sb("gated_pair", [P, 4, 2, T], F32R, scope)
        with ExitStack() as scope:
            ctx_pair = sb("ctx_pair", [P, 2, 2, T], F32R, scope)
            lat_pair = sb("lat_pair", [P, 2, 2, T], F32R, scope)
        ln_scope.close()
        with ExitStack() as scope:
            kv_t = sb("kv_t", [P, 2, 2, CTX + 1], F32R, scope)
            expo = sb("expo", [P, 2, 2, CTX + 1], F32, scope)
            expo_t = sb("expo_t", [P, 4, 2, 512], F32R, scope)
            q_pair = sb("q_pair", [P, 2, 2, 256], F32R, scope)
            out_c = sb("out_c", [P, 256], F32, scope)
            diag = sb("diag", [P, 2, 2, P], F32, scope)
            part_max = sb("part_max", [P, 2, 2], F32, scope)
            neg_m = sb("neg_m", [P, 2], F32, scope)
            part_sum = sb("part_sum", [P, 2, 2, 3], F32, scope)
            sums = sb("sums", [P, 2, 2], F32, scope)
            kv_pair = sb("kv_pair", [P, 2, 2, KT, CD], F32R, scope)
            rope_k = sb("rope_k", [P, 2, KT, CD], F32, scope)
            kv = sb("kv", [P, KT, CD], F32, scope)
            kv_turn = sb("kv_turn", [P, KT, CD], F32, scope)

        inputs_in = sem("inputs_in")
        smalls_in = sem("smalls_in")
        chunk_in = [sem("chunk_in_0"), sem("chunk_in_1")]
        chunk_high = sem("chunk_high")
        chunk_split = sem("chunk_split")
        pool_started = sem("pool_started")
        chunk_used = sem("chunk_used")
        setup = sem("setup")
        x_ready = sem("x_ready")
        ln_mean, ln_centred, ln_squared, ln_var = sem("ln_mean"), sem("ln_centred"), sem("ln_squared"), sem("ln_var")
        ln_log, ln_rstd, ln_normal = sem("ln_log"), sem("ln_rstd"), sem("ln_normal")
        ln_high, ln_low = sem("ln_high"), sem("ln_low")
        stored = sem("stored")

        projected = sem("projected")
        q_in, k_in, v_in = sem("q_in"), sem("k_in"), sem("v_in")
        qk_turned, rope_steps = sem("qk_turned"), sem("rope_steps")
        scores, maxed, expd = sem("scores"), sem("maxed"), sem("expd")
        row_inverted, normal = sem("row_inverted"), sem("normal")
        prob_turned, prob_in = sem("prob_turned"), sem("prob_in")
        attended, heads_high, heads_low = sem("attended"), sem("heads_high"), sem("heads_low")
        heads_read = sem("heads_read")
        out_done = sem("out_done")
        gated, gate_exp = sem("gated"), sem("gate_exp")
        gate_step = sem("gate_step")
        rows_turned, rows_in = sem("rows_turned"), sem("rows_in")
        spread, spread_in = sem("spread"), sem("spread_in")
        first, second = sem("first"), sem("second")
        hid_in, hid_high, hid_low = sem("hid_in"), sem("hid_high"), sem("hid_low")
        silu_done, mid_step = sem("silu_done"), sem("mid_step")
        mid_high, mid_low = sem("mid_high"), sem("mid_low")
        lora_done, lora_in = sem("lora_done"), sem("lora_in")
        mixed_out = sem("mixed_out")
        second_in = sem("second_in")

        hk_done, hk_high, hk_low = sem("hk_done"), sem("hk_high"), sem("hk_low")
        absorbed, absorb_high, absorb_low = sem("absorbed"), sem("absorb_high"), sem("absorb_low")
        q_big, q_turned = sem("q_big"), sem("q_turned")
        turn_step = sem("turn_step")
        rope_high, rope_low = sem("rope_high"), sem("rope_low")
        q_lat, q_lat_in = sem("q_lat"), sem("q_lat_in")
        tables_in, ctx_loaded = sem("tables_in"), sem("ctx_loaded")
        kv_step = sem("kv_step")
        values_high, values_split = sem("values_high"), sem("values_split")
        keys_t, keys_high, keys_low = sem("keys_t"), sem("keys_high"), sem("keys_low")
        qu_high, qu_low = sem("qu_high"), sem("qu_low")
        scored = sem("scored")
        max_part, max_done = sem("max_part"), sem("max_done")
        exp_done = sem("exp_done")
        summed, inverted, diagonal = sem("summed"), sem("inverted"), sem("diagonal")
        exp_t, exp_t_high, exp_t_low = sem("exp_t"), sem("exp_t_high"), sem("exp_t_low")
        context_sum, context_in = sem("context_sum"), sem("context_in")
        context_done = sem("context_done")
        ctx_high, ctx_low = sem("ctx_high"), sem("ctx_low")
        lat_done, lat_high, lat_low = sem("lat_done"), sem("lat_high"), sem("lat_low")
        d_out = sem("d_out")
        bc_done, conv_pad = sem("bc_done"), sem("conv_pad")
        conv_step, conv_silu = sem("conv_step"), sem("conv_silu")
        dt_done, dt_step, dt_exp, a_exp = sem("dt_done"), sem("dt_step"), sem("dt_exp"), sem("a_exp")
        g_done, g_masked = sem("g_done"), sem("g_masked")
        xs_done, gate_done, xs_copied, gate_silu = sem("xs_done"), sem("gate_done"), sem("xs_copied"), sem("gate_silu")
        decay_ready, decay_sum, decay_exp, mixed = sem("decay_ready"), sem("decay_sum"), sem("decay_exp"), sem("mixed")
        xs_turned, xdt_ready = sem("xs_turned"), sem("xdt_ready")
        y_done, y_step, y_squared = sem("y_done"), sem("y_step"), sem("y_squared")
        norm_sum, norm_log, norm_inv = sem("norm_sum"), sem("norm_log"), sem("norm_inv")
        gh_high, gh_low = sem("gh_high"), sem("gh_low")
        e_out, e_scaled = sem("e_out"), sem("e_scaled")

        block = held.enter_context(nc.Block())

        def chunk_regions():
            n = at = 0
            for stage, widths, reps in stream_plan():
                yield stage, n, at, widths, reps
                n += len(widths) * reps
                at += sum(widths) * P * reps

        def run_region(eng, region, step):
            _, n0, at0, widths, reps = region
            ats = [at0 + P * sum(widths[:j]) for j in range(len(widths))]
            if reps == 1:
                for j, w in enumerate(widths):
                    step(n0 + j, (n0 + j) // 2, ats[j], (n0 + j) % 2, w)
                return
            first = 0
            if n0 == 0:
                for j, w in enumerate(widths):
                    step(j, 0, ats[j], j % 2, w)
                first = 1
            with eng.Fori(first, reps) as i:
                for j, w in enumerate(widths):
                    step(n0 + j + i * len(widths), (n0 + j) // 2 + i * (len(widths) // 2),
                         ats[j] + i * (sum(widths) * P), (n0 + j) % 2, w)

        def unslotted(n):
            return isinstance(n, int) and n < 2

        REGIONS = [r for r in chunk_regions() if STAGES.index(r[0][0]) <= STAGES.index(last_stage)]

        def weight(slot, part, t, rows=P):
            return wpair[0:rows, slot, part, t * P:(t + 1) * P]

        @block.sync
        def _(sp):
            sp.dma_start(x[:, :, :], x_in).then_inc(inputs_in, 16)
            sp.dma_start(const[:, :], constants_in).then_inc(smalls_in, 16)
            sp.dma_start(small[:, :], small_in).then_inc(smalls_in, 16)
            sp.dma_start(first_raw[:, :], ctx_first).then_inc(inputs_in, 16)

            def load(n, _, at, slot, width):
                if not unslotted(n):
                    sp.wait_ge(chunk_split, n - 1)
                sp.dma_start(landing[:, slot, 0:width],
                             weights[bass.ds(at, P * width)].rearrange("(p n) -> p n", p=P)
                             ).then_inc(chunk_in[slot], 16)

            for region in REGIONS:
                if region[0] == "D1":
                    sp.wait_ge(x_ready, 4 * 3)
                    sp.dma_start(rope_k[:, :, :, :], rope_k_in.rearrange("a p k d -> p a k d")).then_inc(tables_in, 16)
                    sp.dma_start(kv[:, :, :], ctx_in[0]).then_inc(ctx_loaded, 16)
                run_region(sp, region, load)
                if region[0] == "D1":
                    with sp.Fori(1, B) as b:
                        sp.wait_ge(keys_t, 4 * b)
                        sp.wait_ge(values_split, b)
                        sp.dma_start(kv[:, :, :], ctx_in[bass.ds(b, 1)].rearrange("a p k d -> (a p) k d")
                                     ).then_inc(ctx_loaded, 16)

            sp.wait_ge(x_ready, 4 * (STAGES.index(last_stage) + 1))
            sp.dma_start(x_out, x[:, :, :]).then_inc(stored, 16)
            sp.wait_ge(stored, 16)

        @block.gpsimd
        def _(pool):
            def split(n, use, _, slot, width):
                pool.wait_ge(chunk_in[slot], 16 * use + 16)
                if not unslotted(n):
                    pool.wait_ge(chunk_used, n - 1)
                pool.sem_inc(pool_started, 1)
                pool.tensor_scalar(wpair[:, slot, 0, 0:width], landing[:, slot, 0:width], 1.0, 1.0,
                                   ALU.mult, ALU.mult).then_inc(chunk_high, 1)
                pool.wait_ge(chunk_high, n + 1)
                pool.tensor_tensor(wpair[:, slot, 1, 0:width], landing[:, slot, 0:width],
                                   wpair[:, slot, 0, 0:width].bitcast(F32), ALU.subtract
                                   ).then_inc(chunk_split, 1)

            def context_steps(b, buffer, reused):
                half = CD // 2
                cos, sin = rope_k[:, 0, :, :], rope_k[:, 1, :, :]
                pool.wait_ge(ctx_loaded, 16 * b + 16)
                pool.tensor_tensor(kv_turn[:, :, 0:half], kv[:, :, half:CD], sin[:, :, 0:half], ALU.mult)
                pool.tensor_tensor(kv_turn[:, :, half:CD], kv[:, :, 0:half], sin[:, :, half:CD],
                                   ALU.mult).then_inc(kv_step, 1)
                yield
                pool.wait_ge(kv_step, 3 * b + 1)
                pool.tensor_tensor(kv[:, :, :], kv[:, :, :], cos, ALU.mult).then_inc(kv_step, 1)
                yield
                pool.wait_ge(kv_step, 3 * b + 2)
                pool.tensor_tensor(kv[:, :, :], kv[:, :, :], kv_turn[:, :, :], ALU.add).then_inc(kv_step, 1)
                yield
                pool.wait_ge(kv_step, 3 * b + 3)
                if reused:
                    pool.wait_ge(context_sum, 4 * b - 4)
                pool.sem_inc(pool_started, 1)
                pool.tensor_scalar(kv_pair[:, buffer, 0, :, :], kv[:, :, :], 1.0, 1.0, ALU.mult, ALU.mult
                                   ).then_inc(values_high, 1)
                yield
                pool.wait_ge(values_high, b + 1)
                pool.tensor_tensor(kv_pair[:, buffer, 1, :, :], kv[:, :, :],
                                   kv_pair[:, buffer, 0, :, :].bitcast(F32), ALU.subtract
                                   ).then_inc(values_split, 1)
                yield

            def whole(steps):
                for _ in steps:
                    pass

            for region in REGIONS:
                if region[0] != "D1":
                    run_region(pool, region, split)
                    continue
                _, n0, at0, widths, _ = region
                pool.wait_ge(tables_in, 16)
                steps = context_steps(0, 0, False)
                for part in range(5):
                    run_region(pool, ("D1", n0 + 6 * part, at0 + 3 * part * sum(widths) * P, widths, 3), split)
                    next(steps)
                run_region(pool, ("D1", n0 + 30, at0 + 15 * sum(widths) * P, widths, 1), split)
                whole(context_steps(1, 1, False))
                with pool.Fori(1, B // 2) as i:
                    for j in range(2):
                        whole(context_steps(2 * i + j, j, True))

        CB, DB, EB, FB = starts["C"], starts["D1"], starts["E"], starts["F"]
        D3B = starts["D3"]
        A_OUT, B_OUT, E_OUT = FT, starts["B"] + 2 * FT, EB + 1 + IT
        SPREADS = (GATED, GATED, NE + 1)
        SPREAD_0 = (0, GATED, 2 * GATED)
        GATE_STEPS = (12, 12, 16)
        GATE_0 = (0, 12, 24)
        ROW_CHUNKS = ((0, 400), (400, 400), (800, 400), (1200, 401))

        def c_chunks(p, e):
            base = CB + 3 * NE * p
            return (base, base + 1) if isinstance(e, int) and e == 0 else (base + 3 * e - 1, base + 3 * e + 1)

        def turned_batch(i, k, last):
            return {1: 2 * i + 1, 5: None if last else 2 * i + 2}.get(k)

        TURN_BANKS = (4, 5, 7)

        def context_groups(k, last):
            order = [("exps", q) for q in range(3, 7)]
            if turned_batch(0, k, last) is not None:
                order = [g for part, exps in enumerate(order) for g in (exps, ("keys", part))]
            before = [("exps", q) for q in range(3)] + order
            return [(*g, TURN_BANKS[n % 3], before[n]) for n, g in enumerate(order)]

        def f_chunks(e):
            return (FB + 1, FB + 2) if isinstance(e, int) and e == 0 else (FB + 3 * e + 1, FB + 3 * e + 2)

        def runs(stage):
            return STAGES.index(stage) <= STAGES.index(last_stage)

        @block.tensor
        def _(pe):
            def product(out, w, act, start=False, stop=False):
                pe.matmul(out, w(0), act(0), start=start, stop=False)
                pe.matmul(out, w(0), act(1), start=False, stop=False)
                return pe.matmul(out, w(1), act(0), start=False, stop=stop)

            def tokens(pair, k):
                return lambda part: pair[:, part, k, :]

            def tile_of(slot, t):
                return lambda part: weight(slot, part, t)

            def chunk_ready(n):
                pe.wait_ge(chunk_split, n + 1)

            def open_sums():
                for m in range(FT):
                    pe.matmul(bank(4 + m), zero_b[:, 0:P], zero_b[:, :], start=True, stop=False)

            def layer_norm(k):
                if k:
                    pe.wait_ge(x_ready, 4 * k)
                else:
                    pe.wait_ge(inputs_in, 32)
                    pe.wait_ge(smalls_in, 32)
                for f in range(FT):
                    mm = pe.matmul(bank(6), constant("mean"), x[:, f, :], start=f == 0, stop=f == FT - 1)
                mm.then_inc(ln_mean, 1)
                for f in range(FT):
                    pe.wait_ge(ln_squared, 4 * k + f + 1)
                    mm = pe.matmul(bank(7), constant("mean"), sq[:, f, :], start=f == 0, stop=f == FT - 1)
                mm.then_inc(ln_var, 1)
                pe.wait_ge(ln_low, 4 * k + 4)

            def wide(slot, first_tile, act, out, kts=FT, close=True):
                for k in range(kts):
                    mm = product(out, tile_of(slot, first_tile + k), tokens(act, k),
                                 start=k == 0, stop=close and k == kts - 1)
                return mm

            def attention_tile(u, mask, rope):
                if rope:
                    for side, (raw, arrived) in enumerate(((q_raw, q_in), (k_raw, k_in))):
                        pe.wait_ge(arrived, u + 1)
                        pe.matmul(bank(3 + side), constant("rope"), raw[:, :], start=True, stop=True
                                  ).then_inc(qk_turned, 1)
                    pe.wait_ge(rope_steps, 6 * (u - FT) + 6)
                else:
                    pe.wait_ge(q_in, u + 1)
                    pe.wait_ge(k_in, u + 1)
                for h in range(HPT):
                    rows = slice(h * HD, (h + 1) * HD)
                    pe.matmul(bank(3 + h), ident_b[:, :], mask_b[:, mask, :, :].rearrange("p g k -> p (g k)"),
                              start=True, stop=False)
                    for g in range(G):
                        mm = pe.matmul(bank(3 + h)[:, g * P:(g + 1) * P], q_t[rows, g * P:(g + 1) * P],
                                       k_t[rows, g * P:(g + 1) * P], start=False, stop=g == G - 1)
                    mm.then_inc(scores, 1)

                def transposes(h):
                    pe.wait_ge(normal, HPT * u + h + 1)
                    for g in range(G):
                        mm = pe.transpose(bank(h % 2)[:, g * P:(g + 1) * P], prob[:, h, g, :], constant("ident"))
                    mm.then_inc(prob_turned, 1)

                def values(h):
                    pe.wait_ge(prob_in, HPT * u + h + 1)
                    if h == 0:
                        pe.wait_ge(v_in, u + 1)
                        pe.wait_ge(heads_read, u + 1)
                    for g in range(G):
                        mm = pe.matmul(bank(7)[h * HD:(h + 1) * HD, g * P:(g + 1) * P],
                                       v_tok[:, g, h * HD:(h + 1) * HD], prob_t[:, h % 2, g, :],
                                       start=True, stop=True)
                    if h == HPT - 1:
                        mm.then_inc(attended, 1)

                transposes(0)
                transposes(1)
                values(0)
                transposes(2)
                values(1)
                transposes(3)
                values(2)
                values(3)

            def value_tile(slot, first_tile, act, kts):
                for g in range(G):
                    for k in range(kts):
                        group = lambda part, k=k: act(part, k)[:, g * P:(g + 1) * P]
                        mm = product(bank(2)[:, g * P:(g + 1) * P], group, tile_of(slot, first_tile + k),
                                     start=k == 0, stop=k == kts - 1)
                return mm

            def out_projection(n0, tiles):
                pe.wait_ge(heads_low, tiles)
                for c in range(2):
                    chunk_ready(n0 + c)
                    slot = (n0 + c) % 2
                    wide(slot, 0, heads_out, bank(2 * c)).then_inc(out_done, 1)
                    wide(slot, FT, heads_out, bank(2 * c + 1)).then_inc(chunk_used, 1)

            layer_norm(0)
            pe.wait_ge(setup, 7)
            with pe.Fori(0, FT // 2) as i:
                for j in range(2):
                    u = 2 * i + j
                    chunk_ready(u)
                    wide(j, 0, xn, bank(0)).then_inc(projected, 1)
                    product(bank(1), tile_of(j, FT), lambda part: first_pair[:, part, :], start=True, stop=True
                            ).then_inc(projected, 1)
                    value_tile(j, FT + 1, lambda part, k: first_pair[:, part, :], 1).then_inc(chunk_used, 1)
                    attention_tile(u, 0, False)
            out_projection(A_OUT, FT)

            if runs("B"):
                layer_norm(1)
                n0, slot = starts["B"], starts["B"] % 2
                with pe.Fori(0, FT) as f:
                    chunk_ready(n0 + 2 * f)
                    wide(slot, 0, xn, bank(0)).then_inc(projected, 1)
                    wide(slot, FT, xn, bank(1)).then_inc(chunk_used, 1)
                    chunk_ready(n0 + 2 * f + 1)
                    value_tile(1 - slot, 0, lambda part, k: xn[:, part, k, :], FT).then_inc(chunk_used, 1)
                    attention_tile(FT + f, 1, True)
                out_projection(B_OUT, 2 * FT)

            def gate_logits(src, w):
                for g in range(G):
                    for k in range(FT):
                        mm = pe.matmul(bank(4)[:, g * NE:(g + 1) * NE], src[:, k, g * P:(g + 1) * P],
                                       w[:, k, :], start=k == 0, stop=k == FT - 1)
                mm.then_inc(gated, 1)

            def turn_rows(p):
                pe.wait_ge(gate_step, GATE_0[p] + GATE_STEPS[p])
                for g in range(G):
                    mm = pe.transpose(bank(5)[0:NE, g * P:(g + 1) * P], gate_s[:, 5, g, :], constant("ident"))
                mm.then_inc(rows_turned, 1)
                pe.wait_ge(rows_in, p + 1)

            def spread_rows(p, first_spread, experts):
                for e in range(experts):
                    if e >= 2:
                        pe.wait_ge(spread_in, first_spread + e - 1)
                    pe.matmul(bank(5 + e % 2), constant("select", NE)[:, e * P:(e + 1) * P], w_rows[:, :],
                              start=True, stop=True).then_inc(spread, 1)
                pe.wait_ge(spread_in, first_spread + experts)

            def two_tiles(n, slot, act, first_bank, signal, kts=FT):
                chunk_ready(n)
                wide(slot, 0, act, bank(first_bank), kts).then_inc(signal, 1)
                wide(slot, kts, act, bank(first_bank + 1), kts).then_inc(chunk_used, 1)

            def down(n, slot, expert, last=False):
                chunk_ready(n)
                pe.wait_ge(mid_low, 2 * expert + 2)
                for m in range(FT):
                    for k in range(2):
                        mm = product(bank(4 + m), tile_of(slot, 2 * m + k),
                                     lambda part, k=k: mid_pair[:, part, k, :], stop=last and k == 1)
                    if last and m < FT - 1:
                        mm.then_inc(mixed_out, 1)
                mm.then_inc(chunk_used, 1)

            def second_products(p, e, n, slot):
                pe.wait_ge(hid_low, 2 * (NE * p + e) + 2)
                two_tiles(n, slot, hid_pair, 2, second, 2)

            if runs("C"):
                layer_norm(2)
            for p in range(2 if runs("C") else 0):
                cb = CB + 3 * NE * p
                if p:
                    pe.wait_ge(second_in, 3 * FT)
                first_c, width_c = SMALLS["c_gate"]
                w = small[:, first_c + p * FT * NE:first_c + (p + 1) * FT * NE].rearrange("p (k e) -> p k e", e=NE)
                gate_logits(sq if p else xc, w)
                two_tiles(cb, cb % 2, xn, 0, first)
                second_products(p, 0, cb + 1, (cb + 1) % 2)
                turn_rows(p)
                spread_rows(p, SPREAD_0[p], GATED)
                for m in range(FT):
                    pe.matmul(bank(4 + m), small_at("c_down_bias", NE)[:, m * P:(m + 1) * P], w_rows[:, :],
                              start=True, stop=False)

                def expert_c(e, n, slot):
                    two_tiles(n, slot, xn, 0, first)
                    down(n + 1, 1 - slot, NE * p + e - 1)
                    second_products(p, e, n + 2, slot)

                with pe.Fori(0, 3) as i:
                    for j in range(2):
                        expert_c(2 * i + j + 1, cb + 2 + 6 * i + 3 * j, (cb + 3 * j) % 2)
                expert_c(NE - 1, cb + 20, cb % 2)
                down(cb + 23, (cb + 23) % 2, NE * p + NE - 1, True)

            if runs("D"):
                layer_norm(3)

                def absorbed_queries(h, buffer):
                    pe.wait_ge(rope_low, QT * h + QT)
                    for k in range(QT):
                        mm = product(bank(7), lambda part, k=k: absorb_pair[:, buffer, part, k * P:(k + 1) * P],
                                     lambda part, k=k: turned_pair[:, buffer, part, k, :],
                                     start=k == 0, stop=k == QT - 1)
                    mm.then_inc(q_lat, 1)

                def query_head(h, slot, buffer, before):
                    n = DB + 2 * h
                    chunk_ready(n)
                    if before:
                        pe.wait_ge(hk_low, h)
                    wide(slot, 0, xn, bank(0)).then_inc(hk_done, 1)
                    chunk_ready(n + 1)
                    if before:
                        pe.wait_ge(q_lat_in, h)
                    for k in range(QT):
                        mm = product(bank(7)[:, k * P:(k + 1) * P],
                                     lambda part, k=k: weight(1 - slot, part, QT + k, XR),
                                     lambda part: weight(slot, part, FT + QT, XR), start=True, stop=True)
                    mm.then_inc(absorbed, 1)
                    pe.wait_ge(hk_low, h + 1)
                    for side in range(2):
                        if before:
                            pe.wait_ge(turn_step, 3 * QT * h - (2 * QT, 1)[side])
                        for k in range(QT):
                            mm = product(bank(1 + QT * side + k),
                                         tile_of(slot, FT + k) if side == 0 else tile_of(1 - slot, k),
                                         lambda part: hk_pair[:, part, :], start=True, stop=True)
                            mm.then_inc(chunk_used if k == QT - 1 else (q_big, q_turned)[side], 1)
                    pe.wait_ge(absorb_low, h + 1)
                    if before:
                        absorbed_queries(h - 1, 1 - buffer)

                slot = DB % 2
                query_head(0, slot, 0, False)
                with pe.Fori(0, (XH - 2) // 2) as i:
                    for j in (1, 2):
                        query_head(2 * i + j, slot, j % 2, True)
                query_head(XH - 1, slot, 1, True)
                pe.wait_ge(q_lat_in, XH)
                absorbed_queries(XH - 1, 1)

                def turn_keys(b, part, k_bank):
                    if part == 0:
                        pe.wait_ge(kv_step, 3 * b + 3)
                    for k in range(4 * part, min(4 * part + 4, KT)):
                        rows = P if k < KT - 1 else LASTK
                        at = (k - 4 * part) * P
                        mm = pe.transpose(bank(k_bank)[:, at:at + rows], kv[0:rows, k, :],
                                          constant("ident", rows)[:, 0:rows])
                    mm.then_inc(keys_t, 1)

                def score_row(i, k, r):
                    unit, buffer, keys = 8 * i + k, k % 2, (k // 4) % 2
                    if r == 0:
                        pe.wait_ge(qu_low, unit + 1)
                        if k % 4 == 0:
                            pe.wait_ge(keys_low, 4 * (2 * i + k // 4) + 4)
                    for c in range(4):
                        pe.wait_ge(exp_done, 6 * unit + 3 * r + (1, 1, 2, 3)[c])
                        product(bank(c)[:, 0:402],
                                lambda part: q_pair[:, buffer, part, r * P:(r + 1) * P],
                                lambda part, c=c: kv_t[:, keys, part, 400 * c:400 * c + 402],
                                start=True, stop=True).then_inc(scored, 1)

                def turn_exp(i, k, q, k_bank):
                    if q == 0:
                        pe.wait_ge(exp_done, 6 * (8 * i + k) + 9)
                    for t in range(2 * q, min(2 * q + 2, KT)):
                        rows = P if t < KT - 1 else LASTK
                        for r in range(2):
                            at = (t % 2) * 256 + r * P
                            mm = pe.transpose(bank(k_bank)[0:rows, at:at + P],
                                              expo[:, k % 2, r, t * P:t * P + rows], constant("ident"))
                    mm.then_inc(exp_t, 1)

                def add_values(i, k, q):
                    unit, buffer = 8 * i + k, (k // 4) % 2
                    if q == 0:
                        if k % 4 == 0:
                            pe.wait_ge(values_split, 2 * i + k // 4 + 1)
                        pe.wait_ge(diagonal, 2 * unit + 2)
                        pe.wait_ge(context_done, unit + 1)
                        pe.matmul(bank(6)[:, 256:512], constant("mean"),
                                  diag[:, k % 2, :, :].rearrange("p r q -> p (r q)"), start=True, stop=True)
                    pe.wait_ge(exp_t_low, 7 * unit + q + 1)
                    for t in range(2 * q, min(2 * q + 2, KT)):
                        rows = P if t < KT - 1 else LASTK
                        cols = slice((t % 2) * 256, (t % 2) * 256 + 256)
                        mm = product(bank(6)[:, 0:256],
                                     lambda part, t=t, rows=rows: kv_pair[0:rows, buffer, part, t, :],
                                     lambda part, rows=rows, cols=cols: expo_t[0:rows, q % 4, part, cols],
                                     start=t == 0, stop=t == KT - 1)
                    if q == 6:
                        mm.then_inc(context_sum, 1)

                def units(i, last):
                    for k in range(8):
                        unit, batch = 8 * i + k, turned_batch(i, k, last)
                        groups = iter(context_groups(k, last))

                        def turn():
                            for _ in range(1 if batch is None else 2):
                                kind, q, k_bank, (before, n) = next(groups)
                                if before == "keys":
                                    pe.wait_ge(keys_low, 4 * batch + n + 1)
                                else:
                                    pe.wait_ge(exp_t_low, 7 * unit + n + 1)
                                if kind == "keys":
                                    turn_keys(batch, q, k_bank)
                                else:
                                    turn_exp(i, k, q, k_bank)

                        def turn_ahead(q):
                            if q == 0:
                                pe.wait_ge(exp_t_low, 7 * unit + 7)
                            elif batch is not None:
                                pe.wait_ge(keys_low, 4 * batch + 5 - q)
                            if k < 7:
                                turn_exp(i, k + 1, q, TURN_BANKS[q])
                            elif not last:
                                turn_exp(i + 1, 0, q, TURN_BANKS[q])

                        if k < 7:
                            score_row(i, k + 1, 1)
                        elif not last:
                            score_row(i + 1, 0, 1)
                        for q in range(4):
                            add_values(i, k, q)
                            turn()
                        if k < 6:
                            score_row(i, k + 2, 0)
                        elif not last:
                            score_row(i + 1, k - 6, 0)
                        for q in range(3):
                            add_values(i, k, 4 + q)
                            turn_ahead(q)

                pe.wait_ge(q_lat_in, XH + 1)
                for part in range(4):
                    if part == 3:
                        pe.wait_ge(keys_low, 1)
                    turn_keys(0, part, TURN_BANKS[part % 3])
                for unit, r in ((0, 0), (0, 1), (1, 0)):
                    score_row(0, unit, r)
                for q in range(3):
                    turn_exp(0, 0, q, TURN_BANKS[q])
                with pe.Fori(0, B // 2 - 1) as i:
                    units(i, False)
                units(B // 2 - 1, True)

                def value_latents(h, slot, buffer):
                    chunk_ready(D3B + h)
                    pe.wait_ge(ctx_low, h + 1)
                    return product(bank(buffer), tile_of(slot, 0), lambda part: ctx_pair[:, buffer, part, :],
                                   start=True, stop=True)

                def latent_outputs(h, n, slot, first_tile, buffer, last=False):
                    chunk_ready(n)
                    pe.wait_ge(lat_low, h + 1)
                    for m in range(FT):
                        mm = product(bank(4 + m), tile_of(slot, first_tile + m),
                                     lambda part: lat_pair[:, buffer, part, :], stop=last)
                        if last and m < FT - 1:
                            mm.then_inc(d_out, 1)
                    mm.then_inc(chunk_used, 1)

                value_latents(0, D3B % 2, 0).then_inc(chunk_used, 1)
                pe.wait_ge(context_done, 4 * B + 1)
                open_sums()

                def latent_head(h, j):
                    slot = (D3B + j) % 2
                    value_latents(h, slot, j % 2).then_inc(lat_done, 1)
                    latent_outputs(h - 1, D3B + h, slot, 1, 1 - j % 2)

                with pe.Fori(0, 7) as i:
                    for j in (1, 2):
                        latent_head(2 * i + j, j)
                latent_head(XH - 1, XH - 1)
                latent_outputs(XH - 1, D3B + XH, (D3B + XH) % 2, 0, (XH - 1) % 2, True)

            if runs("E"):
                layer_norm(4)
                chunk_ready(EB)
                wide(EB % 2, 0, xn, bank(0)).then_inc(bc_done, 1)
                wide(EB % 2, FT, xn, bank(1)).then_inc(chunk_used, 1)
                dt_w = small_at("dt_w").rearrange("p (k h) -> p k h", h=MH)
                for g in range(G):
                    for k in range(FT):
                        mm = pe.matmul(bank(2)[:, g * MH:(g + 1) * MH], xc[:, k, g * P:(g + 1) * P], dt_w[:, k, :],
                                       start=k == 0, stop=k == FT - 1)
                mm.then_inc(dt_done, 1)
                pe.wait_ge(conv_silu, 2)
                for g in range(G):
                    cols = slice(g * P, (g + 1) * P)
                    mm = pe.matmul(bank(3)[:, cols], bc_t[:, 0, cols], bc_t[:, 1, cols], start=True, stop=True)
                mm.then_inc(g_done, 1)
                pe.wait_ge(dt_step, 1)
                pe.wait_ge(g_masked, 1)

                def mamba_outputs(i):
                    pe.wait_ge(mixed, 4 * i + 4)
                    for m in range(2):
                        pe.wait_ge(xdt_ready, 2 * i + 2)
                        for hh in range(2):
                            for g in range(G):
                                mm = pe.matmul(bank(4 + m)[hh * MP:(hh + 1) * MP, g * P:(g + 1) * P],
                                               xdt[:, g, 2 * m + hh, :], mix[:, g, 2 * m + hh, :],
                                               start=True, stop=True)
                        mm.then_inc(y_done, 1)

                def mamba_tiles(i, buffer, before):
                    n = EB + 1 + 2 * i
                    slot = (EB + 1) % 2
                    pe.wait_ge(xs_copied, 2 * i + 2)
                    two_tiles(n, slot, xn, 0, xs_done)
                    if before:
                        mamba_outputs(i - 1)
                    for g in range(G):
                        pe.wait_ge(decay_ready, 4 * i + g + 1)
                        if g >= 2:
                            pe.wait_ge(decay_exp, 4 * i + g - 1)
                        pe.matmul(bank(6 + g % 2), constant("after"),
                                  decay_in[:, g, :, :].rearrange("p h t -> p (h t)"), start=True, stop=True
                                  ).then_inc(decay_sum, 1)
                    if before:
                        pe.wait_ge(gate_silu, 2 * i)
                    two_tiles(n + 1, 1 - slot, xn, 2, gate_done)
                    pe.wait_ge(conv_silu, 2 * i + 4)
                    if before:
                        pe.wait_ge(y_step, 8 * i - 6)
                    for m in range(2):
                        for g in range(G):
                            cols = slice(g * P, (g + 1) * P)
                            mm = pe.transpose(bank(4 + m)[:, cols], xs_t[:, buffer, m, cols], constant("ident"))
                    mm.then_inc(xs_turned, 1)

                for i in range(2):
                    mamba_tiles(i, i, i > 0)
                with pe.Fori(1, IT // 4) as i:
                    for j in range(2):
                        mamba_tiles(2 * i + j, j, True)
                mamba_outputs(IT // 2 - 1)
                pe.wait_ge(y_step, 4 * IT)
                pe.matmul(bank(3), constant("mean"), sq_sum[:, :], start=True, stop=True).then_inc(norm_sum, 1)
                open_sums()

                def output_chunk(c, j, last=False):
                    n = E_OUT + c
                    chunk_ready(n)
                    pe.wait_ge(gh_low, 2 * c + 2)
                    for kk in range(2):
                        for m in range(FT):
                            mm = product(bank(4 + m), tile_of((E_OUT + j) % 2, FT * kk + m),
                                         lambda part, kk=kk: gated_pair[:, 2 * (j % 2) + kk, part, :],
                                         stop=last and kk == 1)
                            if last and kk == 1 and m < FT - 1:
                                mm.then_inc(e_out, 1)
                    mm.then_inc(chunk_used, 1)

                with pe.Fori(0, 3) as i:
                    for j in range(2):
                        output_chunk(2 * i + j, j)
                output_chunk(6, 0)
                output_chunk(7, 1, True)

            if runs("F"):
                layer_norm(5)
                gate_logits(xc, small_at("f_gate").rearrange("p (k e) -> p k e", e=NE))
                chunk_ready(FB)
                wide(FB % 2, 0, xn, bank(7)).then_inc(chunk_used, 1)
                two_tiles(FB + 1, (FB + 1) % 2, xn, 0, first)
                two_tiles(FB + 2, FB % 2, xn, 2, second)
                turn_rows(2)
                pe.matmul(bank(4), constant("select_lora", NE), w_rows[:, :], start=True, stop=True
                          ).then_inc(lora_done, 1)
                spread_rows(2, SPREAD_0[2], NE)
                chunk_ready(FB + 3)
                pe.wait_ge(lora_in, 4)
                for m in range(FT):
                    mm = product(bank(4 + m), tile_of((FB + 3) % 2, m), lambda part: lora_pair[:, part, :],
                                 start=True)
                mm.then_inc(chunk_used, 1)

                def expert_f(e, n, slot):
                    pe.wait_ge(silu_done, 2 * (2 * NE + e))
                    two_tiles(n, slot, xn, 0, first)
                    pe.wait_ge(mid_step, 4 * (2 * NE + e))
                    two_tiles(n + 1, 1 - slot, xn, 2, second)
                    down(n + 2, slot, 2 * NE + e - 1)

                with pe.Fori(0, 3) as i:
                    for j in range(2):
                        expert_f(2 * i + j + 1, FB + 4 + 6 * i + 3 * j, (FB + 3 * j) % 2)
                expert_f(NE - 1, FB + 22, FB % 2)
                down(FB + 25, (FB + 25) % 2, 3 * NE - 1, True)

        @block.scalar
        def _(act):
            def layer_norm(k):
                for f in range(FT):
                    act.wait_ge(ln_centred, 4 * k + f + 1)
                    act.activation(sq[:, f, :], xc[:, f, :], ACT.Square).then_inc(ln_squared, 1)
                act.wait_ge(ln_var, k + 1)
                act.activation(rstd[:, :], bank(7), ACT.Ln, bias=eps[:, 0:1]).then_inc(ln_log, 1)
                act.wait_ge(ln_log, k + 1)
                act.activation(rstd[:, :], rstd[:, :], ACT.Exp, scale=-0.5).then_inc(ln_rstd, 1)
                for f in range(FT):
                    act.wait_ge(ln_normal, 4 * k + f + 1)
                    act.copy(xn[:, 0, f, :], xc[:, f, :]).then_inc(ln_high, 1)

            def attention_tile(u, f, q_at, v_at, rope):
                act.wait_ge(projected, q_at)
                act.mul((q_raw if rope else q_t)[:, :], bank(0), HD ** -0.5).then_inc(q_in, 1)
                act.wait_ge(chunk_used, v_at)
                act.copy(v_tok[:, :, :].rearrange("p g d -> p (g d)"), bank(2)).then_inc(v_in, 1)

                def exps(h):
                    act.wait_ge(maxed, HPT * u + h + 1)
                    for g in range(G):
                        act.activation(prob[:, h, g, :], bank(3 + h)[:, g * P:(g + 1) * P], ACT.Exp,
                                       bias=neg_max[:, h, g:g + 1], accum_out=row_sum[:, h, g:g + 1]
                                       ).then_inc(expd, 1)

                def turned_in(h):
                    act.wait_ge(prob_turned, HPT * u + h + 1)
                    act.copy(prob_t[:, h % 2, :, :].rearrange("p g k -> p (g k)"), bank(h % 2)).then_inc(prob_in, 1)

                exps(0)
                exps(1)
                exps(2)
                turned_in(0)
                exps(3)
                turned_in(1)
                turned_in(2)
                turned_in(3)
                act.wait_ge(attended, u + 1)
                act.copy(heads_out[:, 0, bass.ds(f, 1), :].rearrange("p a t -> p (a t)"), bank(7)
                         ).then_inc(heads_high, 1)

            act.wait_ge(setup, 7)
            layer_norm(0)
            with act.Fori(0, FT) as u:
                attention_tile(u, u, 2 * u + 1, u + 1, False)
            if runs("B"):
                layer_norm(1)
                with act.Fori(0, FT) as f:
                    attention_tile(FT + f, f, 2 * FT + f + 1, starts["B"] + 2 * f + 2, True)

            def spread_copies(first_spread, count, first_bank, targets):
                for e in range(count):
                    act.wait_ge(spread, first_spread + e + 1)
                    act.copy(targets(e), bank(first_bank(e))).then_inc(spread_in, 1)

            def gate_exps(p, steps):
                act.wait_ge(gate_step, GATE_0[p] + steps)
                act.activation(gate_s[:, 2, :, :], gate_s[:, 1, :, :], ACT.Exp).then_inc(gate_exp, 1)

            def expert_c(p, e):
                expert = NE * p + e
                up, sw = c_chunks(p, e)
                if not (isinstance(expert, int) and expert == 0):
                    act.wait_ge(mid_step, 4 * expert)
                for m in range(2):
                    act.wait_ge(first, expert + 1) if m == 0 else act.wait_ge(chunk_used, up + 1)
                    act.activation(hid[:, m, :], bank(m), ACT.Identity,
                                   bias=small_at("c_up_bias")[:, bass.ds(2 * e + m, 1)]).then_inc(hid_in, 1)
                for m in range(2):
                    act.wait_ge(second, expert + 1) if m == 0 else act.wait_ge(chunk_used, sw + 1)
                    act.activation(act_o[:, m, :], bank(2 + m), ACT.Silu,
                                   bias=small_at("c_sw_bias")[:, bass.ds(2 * e + m, 1)]).then_inc(silu_done, 1)

            if runs("C"):
                layer_norm(2)
                for p in range(2):
                    gate_exps(p, 3)
                    expert_c(p, 0)
                    spread_copies(SPREAD_0[p], GATED, lambda e: 5 + e % 2, lambda e: wide_w[:, e, :])
                    with act.Fori(1, NE) as e:
                        expert_c(p, e)

            if runs("D"):
                layer_norm(3)

                def latent_queries_in(h):
                    act.wait_ge(q_lat, h + 1)
                    act.copy(big[:, :].rearrange("p (b c) -> p b c", b=B)[:, :, bass.ds(h * S, S)],
                             by_batch(bank(7))).then_inc(q_lat_in, 1)

                def query_head(h, buffer, before):
                    act.wait_ge(hk_done, h + 1)
                    act.copy(hk_pair[:, 0, :], bank(0)).then_inc(hk_high, 1)
                    act.wait_ge(absorbed, h + 1)
                    act.copy(absorb_pair[:, buffer, 0, :], bank(7)[:, 0:QT * P]).then_inc(absorb_high, 1)
                    for k in range(QT):
                        if k == QT - 1 and before:
                            latent_queries_in(h - 1)
                        act.wait_ge(turn_step, 3 * QT * h + QT + 2 * k + 2)
                        act.copy(turned_pair[:, buffer, 0, k, :], by_cos[:, k, :]).then_inc(rope_high, 1)

                act.sem_inc(q_lat_in, 1)
                query_head(0, 0, False)
                with act.Fori(0, (XH - 2) // 2) as i:
                    for j in (1, 2):
                        query_head(2 * i + j, j % 2, True)
                query_head(XH - 1, 1, True)
                latent_queries_in(XH - 1)

                def keys_in(b, buffer, part, k_bank):
                    act.wait_ge(keys_t, 4 * b + part + 1)
                    at, width = 512 * part, min(512, CTX - 512 * part)
                    act.copy(kv_t[:, buffer, 0, at:at + width], bank(k_bank)[:, 0:width]).then_inc(keys_high, 1)
                    if part == 3:
                        act.copy(kv_t[:, buffer, 0, CTX:CTX + 1], bank(k_bank)[:, width - 1:width]
                                 ).then_inc(keys_high, 1)

                def unit_queries(i, k):
                    act.copy(q_pair[:, k % 2, 0, :], big[:, bass.ds(256 * (8 * i + k), 256)]).then_inc(qu_high, 1)

                def exps(i, k, r):
                    act.wait_ge(max_done, 2 * (8 * i + k) + r + 1)
                    buffer = k % 2
                    act.activation(expo[:, buffer, r, 0:800].rearrange("p (c n) -> p c n", c=2),
                                   psum[:, 0:2, 0:400], ACT.Exp, bias=neg_m[:, r:r + 1],
                                   accum_out=part_sum[:, buffer, r, 0:1]).then_inc(exp_done, 1)
                    for c in (2, 3):
                        at, width = ROW_CHUNKS[c]
                        act.activation(expo[:, buffer, r, at:at + width], bank(c)[:, 0:width], ACT.Exp,
                                       bias=neg_m[:, r:r + 1], accum_out=part_sum[:, buffer, r, c - 1:c]
                                       ).then_inc(exp_done, 1)

                def exp_t_in(i, k, q, k_bank):
                    act.wait_ge(exp_t, 7 * (8 * i + k) + q + 1)
                    rows, width = (P, 512) if q < 6 else (LASTK, 256)
                    act.copy(expo_t[0:rows, q % 4, 0, 0:width], bank(k_bank)[0:rows, 0:width]
                             ).then_inc(exp_t_high, 1)

                def units(i, last):
                    for k in range(8):
                        batch = turned_batch(i, k, last)
                        groups = iter(context_groups(k, last))

                        def turned_in(count):
                            for _ in range(count):
                                kind, q, k_bank, _ = next(groups)
                                if kind == "keys":
                                    keys_in(batch, 1 if k < 4 else 0, q, k_bank)
                                else:
                                    exp_t_in(i, k, q, k_bank)

                        if k < 6:
                            unit_queries(i, k + 2)
                        elif not last:
                            unit_queries(i + 1, k - 6)
                        turned_in(1)
                        if k < 7:
                            exps(i, k + 1, 1)
                        elif not last:
                            exps(i + 1, 0, 1)
                        turned_in(3 if batch is None else 7)
                        if k < 6:
                            exps(i, k + 2, 0)
                        elif not last:
                            exps(i + 1, k - 6, 0)
                        act.wait_ge(context_sum, 8 * i + k + 1)
                        act.copy(out_c[:, :], bank(6)[:, 0:256]).then_inc(context_in, 1)
                        for q in range(3):
                            if k < 7:
                                exp_t_in(i, k + 1, q, TURN_BANKS[q])
                            elif not last:
                                exp_t_in(i + 1, 0, q, TURN_BANKS[q])

                act.sem_inc(exp_done, 3)
                act.wait_ge(q_lat_in, XH + 1)
                for k in range(2):
                    unit_queries(0, k)
                for part in range(4):
                    keys_in(0, 0, part, TURN_BANKS[part % 3])
                for unit, r in ((0, 0), (0, 1), (1, 0)):
                    exps(0, unit, r)
                for q in range(3):
                    exp_t_in(0, 0, q, TURN_BANKS[q])
                with act.Fori(0, B // 2 - 1) as i:
                    units(i, False)
                units(B // 2 - 1, True)

                def head_context(h, buffer):
                    act.copy(by_batch(ctx_pair[:, buffer, 0, :]),
                             big[:, :].rearrange("p (b c) -> p b c", b=B)[:, :, bass.ds(h * S, S)]
                             ).then_inc(ctx_high, 1)

                def latents_in(h, buffer):
                    if isinstance(h, int) and h == 0:
                        act.wait_ge(chunk_used, D3B + 1)
                    else:
                        act.wait_ge(lat_done, h)
                    act.copy(lat_pair[:, buffer, 0, :], bank(buffer)).then_inc(lat_high, 1)

                act.wait_ge(context_done, 4 * B + 1)
                head_context(0, 0)
                head_context(1, 1)
                latents_in(0, 0)
                head_context(2, 0)
                latents_in(1, 1)
                head_context(3, 1)
                with act.Fori(1, XH // 2 - 1) as i:
                    for j in range(2):
                        latents_in(2 * i + j, j)
                        head_context(2 * i + j + 2, j)
                for j in range(2):
                    latents_in(XH - 2 + j, j)

            if runs("E"):
                layer_norm(4)
                act.activation(exp_a[:, :], small_at("a_log"), ACT.Exp).then_inc(a_exp, 1)
                act.wait_ge(conv_pad, 1)

                def conv_input(m, earlier):
                    if earlier is not None:
                        act.wait_ge(conv_step, earlier)
                    act.copy(conv_in[:, m, :, CONV_K - 1:], by_batch(bank(m))).then_inc(xs_copied, 1)

                act.wait_ge(bc_done, 1)
                conv_input(0, None)
                act.wait_ge(chunk_used, EB + 1)
                conv_input(1, None)
                act.wait_ge(dt_step, 3)
                act.activation(dt_s[:, 3, :], dt_s[:, 2, :], ACT.Exp).then_inc(dt_exp, 1)
                act.wait_ge(dt_exp, 1)
                act.activation(dt_s[:, 4, :], dt_s[:, 3, :], ACT.Ln, bias=1.0).then_inc(dt_exp, 1)
                for m in range(2):
                    act.wait_ge(conv_step, 4 * m + 4)
                    act.activation(bc_t[:, m, :], conv_acc[:, m, :], ACT.Silu).then_inc(conv_silu, 1)

                def squares(i):
                    for m in range(2):
                        act.wait_ge(y_step, 8 * i + 3 + m)
                        act.activation(y_sq[:, m, :], y_gated[:, m, :], ACT.Square).then_inc(y_squared, 1)

                def mamba_tiles(i, buffer):
                    n = EB + 1 + 2 * i
                    for m in range(2):
                        act.wait_ge(xs_done, i + 1) if m == 0 else act.wait_ge(chunk_used, n + 1)
                        conv_input(m, 8 * i + 4 * m + 4)
                    for g in range(G):
                        act.wait_ge(decay_sum, 4 * i + g + 1)
                        if not (isinstance(i, int) and 4 * i + g < 2):
                            act.wait_ge(mixed, 4 * i + g - 1)
                        act.activation(decay[:, g % 2, :, :].rearrange("p h t -> p (h t)"), bank(6 + g % 2),
                                       ACT.Exp).then_inc(decay_exp, 1)
                    if not (isinstance(i, int) and i < 2):
                        act.wait_ge(y_step, 8 * i - 12)
                    for m in range(2):
                        act.wait_ge(conv_step, 8 * i + 4 * m + 12)
                        act.activation(xs_t[:, buffer, m, :], conv_acc[:, m, :], ACT.Silu).then_inc(conv_silu, 1)
                    for m in range(2):
                        act.wait_ge(gate_done, i + 1) if m == 0 else act.wait_ge(chunk_used, n + 2)
                        act.activation(silu_g[:, buffer, m, :], bank(2 + m), ACT.Silu).then_inc(gate_silu, 1)
                    if not (isinstance(i, int) and i == 0):
                        squares(i - 1)

                for i in range(2):
                    mamba_tiles(i, i)
                with act.Fori(1, IT // 4) as i:
                    for j in range(2):
                        mamba_tiles(2 * i + j, j)
                squares(IT // 2 - 1)

                def gated_high(c, j):
                    for kk in range(2):
                        act.copy(gated_pair[:, 2 * (j % 2) + kk, 0, :], big[:, bass.ds(T * (2 * c + kk), T)]
                                 ).then_inc(gh_high, 1)

                act.wait_ge(y_step, 4 * IT)
                gated_high(0, 0)
                gated_high(1, 1)
                act.wait_ge(norm_sum, 1)
                act.activation(rstd[:, :], bank(3), ACT.Ln, bias=eps[:, 0:1], scale=H / INNER).then_inc(norm_log, 1)
                act.wait_ge(norm_log, 1)
                act.activation(rstd[:, :], rstd[:, :], ACT.Exp, scale=-0.5).then_inc(norm_inv, 1)
                with act.Fori(1, 4) as i:
                    for j in range(2):
                        act.wait_ge(chunk_used, E_OUT + 2 * i + j - 1)
                        gated_high(2 * i + j, j)

            if runs("F"):
                layer_norm(5)
                gate_exps(2, 3)
                act.wait_ge(chunk_used, FB + 1)
                act.copy(lora_h[:, :], bank(7)).then_inc(lora_in, 1)

                def expert_f(e):
                    expert = 2 * NE + e
                    act.wait_ge(mid_step, 4 * expert)
                    for m in range(2):
                        act.wait_ge(first, expert + 1) if m == 0 else act.wait_ge(chunk_used, f_chunks(e)[0] + 1)
                        act.activation(act_o[:, m, :], bank(m), ACT.Silu).then_inc(silu_done, 1)

                expert_f(0)
                spread_copies(SPREAD_0[2], NE, lambda e: 5 + e % 2, lambda e: wide_w[:, e, :])
                with act.Fori(1, NE) as e:
                    expert_f(e)

        @block.vector
        def _(dve):
            def low(out, value, high):
                return dve.tensor_tensor(out, value, high.bitcast(F32), ALU.subtract)

            def layer_norm(k):
                dve.wait_ge(ln_mean, k + 1)
                for f in range(FT):
                    dve.tensor_tensor(xc[:, f, :], x[:, f, :], bank(6), ALU.subtract).then_inc(ln_centred, 1)
                dve.wait_ge(ln_rstd, k + 1)
                for f in range(FT):
                    dve.tensor_tensor(xc[:, f, :], xc[:, f, :], rstd[:, :], ALU.mult).then_inc(ln_normal, 1)
                for f in range(FT):
                    dve.wait_ge(ln_high, 4 * k + f + 1)
                    low(xn[:, 1, f, :], xc[:, f, :], xn[:, 0, f, :]).then_inc(ln_low, 1)

            def add_tile(m, k):
                dve.tensor_tensor(x[:, m, :], x[:, m, :], bank(k), ALU.add).then_inc(x_ready, 1)

            def add_projection(stage, n0):
                for c in range(2):
                    dve.wait_ge(out_done, 2 * stage + c + 1)
                    add_tile(2 * c, 2 * c)
                    dve.wait_ge(chunk_used, n0 + c + 1)
                    add_tile(2 * c + 1, 2 * c + 1)

            dve.memset(zero_b[:, :], 0.0).then_inc(setup, 1)
            dve.memset(eps[:, :], 1e-5).then_inc(setup, 1)
            dve.wait_ge(smalls_in, 32)
            dve.tensor_copy(ident_b[:, :], constant("ident")).then_inc(setup, 1)
            for n, name in enumerate(("causal", "batch")):
                dve.tensor_copy(mask_b[:, n, :, :], constant(name).unsqueeze(1).broadcast_to([P, G, P])).then_inc(setup, 1)
            dve.wait_ge(inputs_in, 32)
            dve.tensor_copy(first_pair[:, 0, :], first_raw[:, :]).then_inc(setup, 1)
            dve.wait_ge(setup, 6)
            low(first_pair[:, 1, :], first_raw[:, :], first_pair[:, 0, :]).then_inc(setup, 1)

            def rope(u, side, raw, arrived, out):
                at = 6 * (u - FT) + 3 * side
                dve.wait_ge(qk_turned, 2 * (u - FT) + side + 1)
                dve.tensor_tensor(by_batch(turned[:, side, :]), by_batch(bank(3 + side)),
                                  over_batches(constant("sin_b")), ALU.mult).then_inc(rope_steps, 1)
                dve.wait_ge(arrived, u + 1)
                dve.tensor_tensor(by_batch(out[:, :]), by_batch(raw[:, :]), over_batches(constant("cos_b")),
                                  ALU.mult).then_inc(rope_steps, 1)
                dve.wait_ge(rope_steps, at + 2)
                dve.tensor_tensor(out[:, :], out[:, :], turned[:, side, :], ALU.add).then_inc(rope_steps, 1)

            def attention_tile(u, f, k_at, with_rope):
                dve.wait_ge(*k_at)
                dve.tensor_copy((k_raw if with_rope else k_t)[:, :], bank(1)).then_inc(k_in, 1)
                if with_rope:
                    rope(u, 0, q_raw, q_in, q_t)
                    rope(u, 1, k_raw, k_in, k_t)

                def row_max(h):
                    dve.wait_ge(scores, HPT * u + h + 1)
                    dve.tensor_reduce(neg_max[:, h, :], bank(3 + h).rearrange("p (g k) -> p g k", g=G), AX_X,
                                      ALU.max, negate=True).then_inc(maxed, 1)

                def normalise(h):
                    dve.wait_ge(expd, G * (HPT * u + h) + G)
                    dve.reciprocal(row_inv[:, h, :], row_sum[:, h, :]).then_inc(row_inverted, 1)
                    dve.wait_ge(row_inverted, HPT * u + h + 1)
                    dve.tensor_tensor(prob[:, h, :, :], prob[:, h, :, :],
                                      row_inv[:, h, :].unsqueeze(2).broadcast_to([P, G, P]), ALU.mult
                                      ).then_inc(normal, 1)

                row_max(0)
                row_max(1)
                row_max(2)
                normalise(0)
                row_max(3)
                normalise(1)
                normalise(2)
                normalise(3)
                dve.wait_ge(heads_high, u + 1)
                tile = bass.ds(f, 1)
                dve.tensor_tensor(heads_out[:, 1, tile, :].rearrange("p a t -> p (a t)"), bank(7),
                                  heads_out[:, 0, tile, :].rearrange("p a t -> p (a t)").bitcast(F32),
                                  ALU.subtract).then_inc(heads_low, 1)
                dve.wait_ge(heads_low, u + 1)
                dve.sem_inc(heads_read, 1)

            dve.sem_inc(heads_read, 1)
            layer_norm(0)
            with dve.Fori(0, FT) as u:
                attention_tile(u, u, (projected, 2 * u + 2), False)
            add_projection(0, A_OUT)
            if runs("B"):
                layer_norm(1)
                with dve.Fori(0, FT) as f:
                    attention_tile(FT + f, f, (chunk_used, starts["B"] + 2 * f + 1), True)
                add_projection(1, B_OUT)

            class Steps:
                at = 0

                def __call__(self, ins):
                    ins.then_inc(gate_step, 1)
                    self.at += 1
                    dve.wait_ge(gate_step, self.at)

            step = Steps()

            def bcast(ap):
                return ap.broadcast_to([P, G, NE])

            def take_top(values, count, weights_in):
                theirs = values.unsqueeze(2).broadcast_to([P, G, NE, NE])
                own = values.unsqueeze(3).broadcast_to([P, G, NE, NE])
                lower = constant("lower").rearrange("p (e j) -> p e j", e=NE)
                step(dve.tensor_tensor(pairs_s[:, 0, :, :, :], theirs, own, ALU.is_gt))
                step(dve.tensor_tensor(pairs_s[:, 1, :, :, :], theirs, own, ALU.is_equal))
                step(dve.tensor_tensor(pairs_s[:, 1, :, :, :], pairs_s[:, 1, :, :, :],
                                       lower.unsqueeze(1).broadcast_to([P, G, NE, NE]), ALU.mult))
                step(dve.tensor_tensor(pairs_s[:, 0, :, :, :], pairs_s[:, 0, :, :, :], pairs_s[:, 1, :, :, :], ALU.add))
                step(dve.tensor_reduce(gate_s[:, 3, :, :], pairs_s[:, 0, :, :, :], AX_X, ALU.add))
                step(dve.scalar_tensor_tensor(out=gate_s[:, 4, :, :], in0=gate_s[:, 3, :, :], scalar=count - 0.5,
                                              in1=weights_in, op0=ALU.is_lt, op1=ALU.mult))

            def gate_c(p):
                first_b, _ = SMALLS["c_gate_bias"]
                bias = small[:, first_b + NE * p:first_b + NE * (p + 1)]
                dve.wait_ge(gated, p + 1)
                step(dve.tensor_tensor(gate_s[:, 0, :, :], bank(4)[:, 0:G * NE].rearrange("p (g e) -> p g e", e=NE),
                                       bias.unsqueeze(1).broadcast_to([P, G, NE]), ALU.add))
                step(dve.tensor_reduce(gate_col[:, 0, :, :], gate_s[:, 0, :, :], AX_X, ALU.max))
                step(dve.tensor_tensor(gate_s[:, 1, :, :], gate_s[:, 0, :, :], bcast(gate_col[:, 0, :, :]), ALU.subtract))
                dve.wait_ge(gate_exp, p + 1)
                take_top(gate_s[:, 0, :, :], GATED, gate_s[:, 2, :, :])
                step(dve.tensor_reduce(gate_col[:, 1, :, :], gate_s[:, 4, :, :], AX_X, ALU.add))
                step(dve.reciprocal(gate_col[:, 2, :, :], gate_col[:, 1, :, :]))
                step(dve.tensor_tensor(gate_s[:, 5, :, 0:GATED], gate_s[:, 4, :, 0:GATED],
                                       gate_col[:, 2, :, :].broadcast_to([P, G, GATED]), ALU.mult))

            def gate_f():
                dve.wait_ge(gated, 3)
                step(dve.tensor_copy(gate_s[:, 0, :, :], bank(4)[:, 0:G * NE].rearrange("p (g e) -> p g e", e=NE)))
                step(dve.tensor_reduce(gate_col[:, 0, :, :], gate_s[:, 0, :, :], AX_X, ALU.max))
                step(dve.tensor_tensor(gate_s[:, 1, :, :], gate_s[:, 0, :, :], bcast(gate_col[:, 0, :, :]), ALU.subtract))
                dve.wait_ge(gate_exp, 3)
                step(dve.tensor_reduce(gate_col[:, 1, :, :], gate_s[:, 2, :, :], AX_X, ALU.add))
                step(dve.reciprocal(gate_col[:, 2, :, :], gate_col[:, 1, :, :]))
                step(dve.tensor_tensor(gate_s[:, 6, :, :], gate_s[:, 2, :, :], bcast(gate_col[:, 2, :, :]), ALU.mult))
                take_top(gate_s[:, 6, :, :], 2, gate_s[:, 6, :, :])
                step(dve.tensor_reduce(gate_col[:, 1, :, :], gate_s[:, 4, :, :], AX_X, ALU.add))
                step(dve.tensor_scalar(gate_col[:, 2, :, :], gate_col[:, 1, :, :], 1e-9, None, ALU.max))
                step(dve.reciprocal(gate_col[:, 3, :, :], gate_col[:, 2, :, :]))
                step(dve.tensor_tensor(gate_s[:, 5, :, :], gate_s[:, 4, :, :], bcast(gate_col[:, 3, :, :]), ALU.mult))

            def rows_copy(p):
                dve.wait_ge(rows_turned, p + 1)
                dve.tensor_copy(w_rows[:, :], bank(5)[0:NE, :]).then_inc(rows_in, 1)

            def hidden(expert):
                for m in range(2):
                    dve.wait_ge(hid_in, 2 * expert + m + 1)
                    dve.tensor_copy(hid_pair[:, 0, m, :], hid[:, m, :]).then_inc(hid_high, 1)
                for m in range(2):
                    dve.wait_ge(hid_high, 2 * expert + m + 1)
                    low(hid_pair[:, 1, m, :], hid[:, m, :], hid_pair[:, 0, m, :]).then_inc(hid_low, 1)

            def middle(expert, e, other, down_before=None):
                wide_e = wide_w[:, bass.ds(e, 1), :].rearrange("p a t -> p (a t)")
                if not (isinstance(expert, int) and expert == 0):
                    dve.wait_ge(mid_low, 2 * expert)
                for m in range(2):
                    dve.wait_ge(silu_done, 2 * expert + m + 1)
                    dve.tensor_tensor(mid[:, m, :], act_o[:, m, :], other(m), ALU.mult).then_inc(mid_step, 1)
                for m in range(2):
                    dve.wait_ge(mid_step, 4 * expert + m + 1)
                    dve.tensor_tensor(mid[:, m, :], mid[:, m, :], wide_e, ALU.mult).then_inc(mid_step, 1)
                if down_before is not None:
                    dve.wait_ge(chunk_used, down_before + 1)
                for m in range(2):
                    dve.wait_ge(mid_step, 4 * expert + m + 3)
                    dve.tensor_copy(mid_pair[:, 0, m, :], mid[:, m, :]).then_inc(mid_high, 1)
                for m in range(2):
                    dve.wait_ge(mid_high, 2 * expert + m + 1)
                    low(mid_pair[:, 1, m, :], mid[:, m, :], mid_pair[:, 0, m, :]).then_inc(mid_low, 1)

            def sum_ready(p, m, last_chunk):
                dve.wait_ge(mixed_out, 3 * p + m + 1) if m < FT - 1 else dve.wait_ge(chunk_used, last_chunk + 1)

            if runs("C"):
                layer_norm(2)
                dve.memset(gate_s[:, 5, :, GATED:NE], 1.0)
                dve.memset(wide_w[:, GATED:NE, :], 1.0)
                for p in range(2):
                    gate_c(p)
                    hidden(NE * p)
                    rows_copy(p)
                    dve.wait_ge(spread_in, SPREAD_0[p] + GATED)
                    middle(NE * p, 0, lambda m: hid[:, m, :])
                    with dve.Fori(1, NE) as e:
                        hidden(NE * p + e)
                        middle(NE * p + e, e, lambda m: hid[:, m, :])
                    last_chunk = CB + 3 * NE * (p + 1) - 1
                    for m in range(FT):
                        sum_ready(p, m, last_chunk)
                        dve.tensor_tensor(sq[:, m, :], xc[:, m, :], bank(4 + m), ALU.add).then_inc(second_in, 1)
                    for m in range(FT):
                        dve.wait_ge(second_in, 3 * FT * p + m + 1)
                        if p == 0:
                            dve.tensor_copy(xn[:, 0, m, :], sq[:, m, :]).then_inc(second_in, 1)
                        else:
                            dve.tensor_tensor(x[:, m, :], x[:, m, :], sq[:, m, :], ALU.add).then_inc(x_ready, 1)
                    for m in range(FT if p == 0 else 0):
                        dve.wait_ge(second_in, FT + m + 1)
                        low(xn[:, 1, m, :], sq[:, m, :], xn[:, 0, m, :]).then_inc(second_in, 1)

            if runs("D"):
                layer_norm(3)
                cos_q = constant("cos_q").rearrange("p (k s) -> p k s", k=QT)
                sin_q = constant("sin_q").rearrange("p (k s) -> p k s", k=QT)

                def query_head(h, buffer):
                    dve.wait_ge(hk_high, h + 1)
                    low(hk_pair[:, 1, :], bank(0), hk_pair[:, 0, :]).then_inc(hk_low, 1)
                    dve.wait_ge(absorb_high, h + 1)
                    low(absorb_pair[:, buffer, 1, :], bank(7)[:, 0:QT * P], absorb_pair[:, buffer, 0, :]
                        ).then_inc(absorb_low, 1)
                    for k in range(QT):
                        dve.wait_ge(q_big, 2 * h + k + 1) if k < 2 else dve.wait_ge(chunk_used, DB + 2 * h + 1)
                        dve.tensor_tensor(by_batch(by_cos[:, k, :]), by_batch(bank(1 + k)),
                                          over_batches(cos_q[:, k, :]), ALU.mult).then_inc(turn_step, 1)
                    for k in range(QT):
                        dve.wait_ge(q_turned, 2 * h + k + 1) if k < 2 else dve.wait_ge(chunk_used, DB + 2 * h + 2)
                        dve.tensor_tensor(by_batch(by_sin[:, k % 2, :]), by_batch(bank(1 + QT + k)),
                                          over_batches(sin_q[:, k, :]), ALU.mult).then_inc(turn_step, 1)
                        dve.wait_ge(turn_step, 3 * QT * h + QT + 2 * k + 1)
                        dve.tensor_tensor(by_cos[:, k, :], by_cos[:, k, :], by_sin[:, k % 2, :], ALU.add
                                          ).then_inc(turn_step, 1)
                    for k in range(QT):
                        dve.wait_ge(rope_high, QT * h + k + 1)
                        low(turned_pair[:, buffer, 1, k, :], by_cos[:, k, :], turned_pair[:, buffer, 0, k, :]
                            ).then_inc(rope_low, 1)

                with dve.Fori(0, XH // 2) as i:
                    for j in range(2):
                        query_head(2 * i + j, j)

                def keys_in(b, buffer, part, k_bank):
                    dve.wait_ge(keys_high, 5 * b + part + (1 if part < 3 else 2))
                    at, width = 512 * part, min(512, CTX - 512 * part)
                    ins = low(kv_t[:, buffer, 1, at:at + width], bank(k_bank)[:, 0:width],
                              kv_t[:, buffer, 0, at:at + width])
                    if part == 3:
                        ins = low(kv_t[:, buffer, 1, CTX:CTX + 1], bank(k_bank)[:, width - 1:width],
                                  kv_t[:, buffer, 0, CTX:CTX + 1])
                    ins.then_inc(keys_low, 1)

                def unit_queries(i, k):
                    unit = 8 * i + k
                    dve.wait_ge(qu_high, unit + 1)
                    low(q_pair[:, k % 2, 1, :], big[:, bass.ds(256 * unit, 256)], q_pair[:, k % 2, 0, :]
                        ).then_inc(qu_low, 1)

                def half_max(i, k, r, half):
                    row = 2 * (8 * i + k) + r
                    dve.wait_ge(scored, 4 * row + 2 * half + 2)
                    dve.tensor_reduce(part_max[:, r, half:half + 1], psum[:, 2 * half:2 * half + 2, 0:402],
                                      mybir.AxisListType.XY, ALU.max).then_inc(max_part, 1)

                def row_max(i, k, r):
                    half_max(i, k, r, 1)
                    dve.wait_ge(max_part, 2 * (2 * (8 * i + k) + r) + 2)
                    dve.tensor_reduce(neg_m[:, r:r + 1], part_max[:, r, :], AX_X, ALU.max, negate=True
                                      ).then_inc(max_done, 1)

                def row_scales(i, k):
                    unit = 8 * i + k
                    dve.wait_ge(exp_done, 6 * unit + 9)
                    dve.tensor_reduce(sums[:, 0, :], part_sum[:, k % 2, :, :], AX_X, ALU.add).then_inc(summed, 1)
                    dve.wait_ge(summed, unit + 1)
                    dve.reciprocal(sums[:, 1, :], sums[:, 0, :]).then_inc(inverted, 1)
                    dve.wait_ge(inverted, unit + 1)
                    for r in range(2):
                        dve.tensor_scalar(diag[:, k % 2, r, :], constant("ident"), sums[:, 1, r:r + 1], float(H),
                                          ALU.mult, ALU.mult).then_inc(diagonal, 1)

                def exp_t_in(i, k, q, k_bank):
                    dve.wait_ge(exp_t_high, 7 * (8 * i + k) + q + 1)
                    rows, width = (P, 512) if q < 6 else (LASTK, 256)
                    low(expo_t[0:rows, q % 4, 1, 0:width], bank(k_bank)[0:rows, 0:width],
                        expo_t[0:rows, q % 4, 0, 0:width]).then_inc(exp_t_low, 1)

                def units(i, last):
                    for k in range(8):
                        unit, batch = 8 * i + k, turned_batch(i, k, last)
                        groups = iter(context_groups(k, last))

                        def turned_in(count):
                            for _ in range(count):
                                kind, q, k_bank, _ = next(groups)
                                if kind == "keys":
                                    keys_in(batch, 1 if k < 4 else 0, q, k_bank)
                                else:
                                    exp_t_in(i, k, q, k_bank)

                        second_row = (i, k + 1) if k < 7 else None if last else (i + 1, 0)
                        first_row = (i, k + 2) if k < 6 else None if last else (i + 1, k - 6)
                        if second_row is not None:
                            half_max(*second_row, 1, 0)
                            row_max(*second_row, 1)
                        exp_t_in(i, k, 2, TURN_BANKS[2])
                        turned_in(1)
                        if first_row is not None:
                            unit_queries(*first_row)
                        turned_in(1 if batch is None else 3)
                        if second_row is not None:
                            row_scales(*second_row)
                        turned_in(1 if batch is None else 3)
                        if first_row is not None:
                            half_max(*first_row, 0, 0)
                        turned_in(1)
                        if first_row is not None:
                            row_max(*first_row, 0)
                        dve.wait_ge(context_in, unit + 1)
                        dve.tensor_tensor(big[:, bass.ds(256 * unit, 256)], out_c[:, :], bank(6)[:, 256:512],
                                          ALU.mult).then_inc(context_done, 1)
                        if second_row is not None:
                            for q in range(2):
                                exp_t_in(*second_row, q, TURN_BANKS[q])

                dve.sem_inc(context_done, 1)
                for k in range(2):
                    unit_queries(0, k)
                for part in range(4):
                    keys_in(0, 0, part, TURN_BANKS[part % 3])
                for unit, r in ((0, 0), (0, 1), (1, 0)):
                    half_max(0, unit, r, 0)
                    row_max(0, unit, r)
                    if r == 1:
                        row_scales(0, 0)
                for q in range(2):
                    exp_t_in(0, 0, q, TURN_BANKS[q])
                with dve.Fori(0, B // 2 - 1) as i:
                    units(i, False)
                units(B // 2 - 1, True)

                def head_context(h, buffer):
                    dve.wait_ge(ctx_high, h + 1)
                    dve.tensor_tensor(by_batch(ctx_pair[:, buffer, 1, :]),
                                      big[:, :].rearrange("p (b c) -> p b c", b=B)[:, :, bass.ds(h * S, S)],
                                      by_batch(ctx_pair[:, buffer, 0, :]).bitcast(F32), ALU.subtract
                                      ).then_inc(ctx_low, 1)

                def latents_in(h, buffer):
                    dve.wait_ge(lat_high, h + 1)
                    low(lat_pair[:, buffer, 1, :], bank(buffer), lat_pair[:, buffer, 0, :]).then_inc(lat_low, 1)

                head_context(0, 0)
                head_context(1, 1)
                with dve.Fori(0, XH // 2 - 1) as i:
                    for j in range(2):
                        latents_in(2 * i + j, j)
                        head_context(2 * i + j + 2, j)
                for j in range(2):
                    latents_in(XH - 2 + j, j)
                for m in range(FT):
                    dve.wait_ge(d_out, m + 1) if m < FT - 1 else dve.wait_ge(chunk_used, D3B + XH + 1)
                    add_tile(m, 4 + m)

            if runs("E"):
                layer_norm(4)
                upto = constant("upto")
                conv_w, conv_b = small_at("conv_w"), small_at("conv_b")
                dve.memset(sq_sum[:, :], 0.0)
                dve.memset(conv_in[:, :, :, 0:CONV_K - 1], 0.0).then_inc(conv_pad, 1)

                def convolve(v, m, tile):
                    acc = by_batch(conv_acc[:, m, :])
                    dve.wait_ge(xs_copied, v + 1)
                    if not (isinstance(v, int) and v < 2):
                        dve.wait_ge(conv_silu, v - 1)
                    dve.tensor_scalar(acc, conv_in[:, m, :, 0:S], conv_w[:, bass.ds(CONV_K * tile, 1)],
                                      conv_b[:, bass.ds(tile, 1)], ALU.mult, ALU.add).then_inc(conv_step, 1)
                    for t in range(1, CONV_K):
                        dve.wait_ge(conv_step, 4 * v + t)
                        dve.scalar_tensor_tensor(out=acc, in0=conv_in[:, m, :, t:t + S],
                                                 scalar=conv_w[:, bass.ds(CONV_K * tile + t, 1)], in1=acc,
                                                 op0=ALU.mult, op1=ALU.add).then_inc(conv_step, 1)

                def heads(ap):
                    return ap.rearrange("p (g h) -> p g h", h=MH)

                dt, a = heads(dt_s[:, 0, :]), heads(dt_s[:, 1, :])
                dve.wait_ge(dt_done, 1)
                dve.tensor_tensor(dt, heads(bank(2)[:, 0:G * MH]), small_at("dt_bias").unsqueeze(1).broadcast_to([P, G, MH]),
                                  ALU.add).then_inc(dt_step, 1)
                dve.wait_ge(dt_step, 1)
                dve.tensor_scalar(dt_s[:, 1, :], dt_s[:, 0, :], 0.0, None, ALU.max).then_inc(dt_step, 1)
                dve.scalar_tensor_tensor(out=dt_s[:, 2, :], in0=dt_s[:, 0, :], scalar=-1.0, in1=dt_s[:, 0, :],
                                         op0=ALU.mult, op1=ALU.min).then_inc(dt_step, 1)
                convolve(0, 0, IT)
                convolve(1, 1, IT + 1)
                dve.wait_ge(dt_exp, 2)
                dve.wait_ge(dt_step, 3)
                dve.tensor_tensor(dt_s[:, 0, :], dt_s[:, 1, :], dt_s[:, 4, :], ALU.add).then_inc(dt_step, 1)
                dve.wait_ge(dt_step, 4)
                dve.wait_ge(a_exp, 1)
                dve.scalar_tensor_tensor(out=a, in0=dt, scalar=-1.0, in1=exp_a[:, :].unsqueeze(1).broadcast_to([P, G, MH]),
                                         op0=ALU.mult, op1=ALU.mult).then_inc(dt_step, 1)
                dve.wait_ge(dt_step, 5)
                dve.wait_ge(g_done, 1)
                dve.tensor_tensor(g_mask[:, :, :], bank(3).rearrange("p (g t) -> p g t", g=G),
                                  upto.unsqueeze(1).broadcast_to([P, G, P]), ALU.mult).then_inc(g_masked, 1)

                def outputs_a(i, buffer):
                    for m in range(2):
                        dve.wait_ge(y_done, 2 * i + m + 1)
                        dve.scalar_tensor_tensor(out=y_sum[:, m, :], in0=xs_t[:, buffer, m, :],
                                                 scalar=small_at("skip")[:, bass.ds(2 * i + m, 1)], in1=bank(4 + m),
                                                 op0=ALU.mult, op1=ALU.add).then_inc(y_step, 1)
                    for m in range(2):
                        dve.wait_ge(y_step, 8 * i + m + 1)
                        dve.wait_ge(gate_silu, 2 * i + m + 1)
                        dve.tensor_tensor(y_gated[:, m, :], y_sum[:, m, :], silu_g[:, buffer, m, :], ALU.mult
                                          ).then_inc(y_step, 1)

                def outputs_b(i):
                    for m in range(2):
                        dve.wait_ge(y_step, 8 * i + m + 3)
                        dve.tensor_scalar(big[:, bass.ds(T * (2 * i + m), T)], y_gated[:, m, :],
                                          small_at("norm_w")[:, bass.ds(2 * i + m, 1)], None, ALU.mult
                                          ).then_inc(y_step, 1)
                    for m in range(2):
                        dve.wait_ge(y_squared, 2 * i + m + 1)
                        dve.wait_ge(y_step, 8 * i + m + 6)
                        dve.tensor_tensor(sq_sum[:, :], sq_sum[:, :], y_sq[:, m, :], ALU.add).then_inc(y_step, 1)

                def mamba_tiles(i, buffer):
                    for g in range(G):
                        dve.tensor_tensor(decay_in[:, g, :, :], upto.unsqueeze(1).broadcast_to([P, 4, P]),
                                          a[:, g, bass.ds(4 * i, 4)].unsqueeze(2).broadcast_to([P, 4, P]), ALU.mult
                                          ).then_inc(decay_ready, 1)
                    for m in range(2):
                        convolve(2 * i + m + 2, m, 2 * i + m)
                    if not (isinstance(i, int) and i == 0):
                        outputs_a(i - 1, 1 - buffer)
                    for g in range(G):
                        dve.wait_ge(decay_exp, 4 * i + g + 1)
                        dve.tensor_tensor(mix[:, g, :, :], decay[:, g % 2, :, :],
                                          g_mask[:, g, :].unsqueeze(1).broadcast_to([P, 4, P]), ALU.mult
                                          ).then_inc(mixed, 1)
                    dve.wait_ge(xs_turned, i + 1)
                    for m in range(2):
                        dve.tensor_tensor(xdt[:, :, 2 * m:2 * m + 2, :],
                                          bank(4 + m).rearrange("p (g h d) -> p g h d", g=G, h=2),
                                          dt[:, :, bass.ds(4 * i + 2 * m, 2)].unsqueeze(3).broadcast_to([P, G, 2, MP]),
                                          ALU.mult).then_inc(xdt_ready, 1)
                    if not (isinstance(i, int) and i == 0):
                        outputs_b(i - 1)

                for i in range(2):
                    mamba_tiles(i, i)
                with dve.Fori(1, IT // 4) as i:
                    for j in range(2):
                        mamba_tiles(2 * i + j, j)
                outputs_a(IT // 2 - 1, 1)
                outputs_b(IT // 2 - 1)

                def gated_low(c, j):
                    for kk in range(2):
                        dve.wait_ge(gh_high, 2 * c + kk + 1)
                        buffer = 2 * (j % 2) + kk
                        low(gated_pair[:, buffer, 1, :], big[:, bass.ds(T * (2 * c + kk), T)],
                            gated_pair[:, buffer, 0, :]).then_inc(gh_low, 1)

                with dve.Fori(0, 4) as i:
                    for j in range(2):
                        gated_low(2 * i + j, j)
                dve.wait_ge(norm_inv, 1)
                for m in range(FT):
                    dve.wait_ge(e_out, m + 1) if m < FT - 1 else dve.wait_ge(chunk_used, E_OUT + 8)
                    if m >= 2:
                        dve.wait_ge(x_ready, 4 * 4 + m - 1)
                    dve.tensor_tensor(y_sum[:, m % 2, :], bank(4 + m), rstd[:, :], ALU.mult).then_inc(e_scaled, 1)
                    dve.wait_ge(e_scaled, m + 1)
                    dve.tensor_tensor(x[:, m, :], x[:, m, :], y_sum[:, m % 2, :], ALU.add).then_inc(x_ready, 1)

            if runs("F"):
                layer_norm(5)
                gate_f()
                rows_copy(2)
                dve.wait_ge(lora_in, 1)
                dve.wait_ge(lora_done, 1)
                dve.tensor_tensor(lora_w[:, :], lora_h[:, :], bank(4), ALU.mult).then_inc(lora_in, 1)
                dve.wait_ge(lora_in, 2)
                dve.tensor_copy(lora_pair[:, 0, :], lora_w[:, :]).then_inc(lora_in, 1)
                dve.wait_ge(lora_in, 3)
                low(lora_pair[:, 1, :], lora_w[:, :], lora_pair[:, 0, :]).then_inc(lora_in, 1)

                def expert_f(e):
                    if not isinstance(e, int):
                        dve.wait_ge(second, 2 * NE + e + 1)
                    dve.wait_ge(chunk_used, f_chunks(e)[1] + 1)
                    middle(2 * NE + e, e, lambda m: bank(2 + m),
                           None if isinstance(e, int) else f_chunks(e)[1] + 1)

                dve.wait_ge(spread_in, SPREAD_0[2] + NE)
                expert_f(0)
                with dve.Fori(1, NE) as e:
                    expert_f(e)
                for m in range(FT):
                    sum_ready(2, m, FB + 25)
                    add_tile(m, 4 + m)


STAGES = ("A", "B", "C", "D", "E", "F")
LAST_STAGE = "F"


def kernel(**inputs):
    import concourse.bacc as bacc
    from concourse.bass_utils import run_bass_kernel_spmd

    nc = bacc.Bacc("TRN2", target_bir_lowering=False, num_devices=1)
    arrays = lay_out({name: np.asarray(a) for name, a in inputs.items()})
    order = ("x", "ctx_first", "ctx", "weights", "small", "constants", "rope_k")
    args = [nc.dram_tensor(f"in_{name}", arrays[name].shape, F32, kind="ExternalInput").ap() for name in order]
    out = nc.dram_tensor("out", (P, FT, T), F32, kind="ExternalOutput").ap()
    perceiver_stack(nc, *args, out)
    r = run_bass_kernel_spmd(nc, [{f"in_{name}": arrays[name] for name in order}], core_ids=[0])
    return np.ascontiguousarray(r.results[0]["out"].transpose(2, 1, 0).reshape(B, S, H))
```

```python
from contextlib import ExitStack

import numpy as np

import concourse.bass as bass
from concourse import mybir

F32 = mybir.dt.float32
F32R = mybir.dt.float32r
BF16 = mybir.dt.bfloat16
ALU = mybir.AluOpType
ACT = mybir.ActivationFunctionType
AX_X = mybir.AxisListType.X

P = 128
B, S, H = 8, 64, 512
T = B * S
FT = H // P
G = T // P
CTX, CD = 1601, 128
NH, HD = 16, 32
HPT = P // HD
NE = 8
GATED = 6
FF = 256
XH, XQ, XR = 16, 384, 64
QT = XQ // P
KT = 13
LASTK = CTX - (KT - 1) * P
MH, MP, MN = 32, 64, 128
INNER = MH * MP
IT = INNER // P
CONV_K = 4
LORA = 16
MASKED = -1e30
CHUNK = 8 * P


def stream_plan():
    half = CHUNK // 2
    plan = [("A", (CHUNK,) + (half,) * FT + (CHUNK, CHUNK), 1),
            ("B", (CHUNK, CHUNK), 1), ("B", (half, half), FT), ("B", (CHUNK, CHUNK), 1)]
    for _ in range(2):
        plan += [("C", (half,) * 10, NE // 2)]
    plan += [("D1", (CHUNK, 6 * P), XH),
             ("D3", (P,), 1), ("D3", (5 * P, 5 * P), 7), ("D3", (5 * P, 4 * P), 1),
             ("E", (CHUNK,), 1), ("E", (CHUNK, CHUNK), IT // 2), ("E", (CHUNK, CHUNK), 4),
             ("F", (half, CHUNK, CHUNK, half), 1), ("F", (CHUNK,) * 6, 3), ("F", (CHUNK,) * 4, 1)]
    return plan


def plan_starts():
    starts, n = {}, 0
    for stage, widths, reps in stream_plan():
        starts.setdefault(stage, n)
        n += len(widths) * reps
    starts["end"] = n
    return starts


def offsets(fields):
    at, found = 0, {}
    for name, width in fields:
        found[name] = (at, width)
        at += width
    return found, at


CONSTANTS, CONSTANT_COLS = offsets([
    ("ident", P), ("mean", P), ("rope", P), ("causal", P), ("batch", P), ("upto", P), ("after", P),
    ("cos_b", S), ("sin_b", S), ("cos_q", QT * S), ("sin_q", QT * S),
    ("lower", NE * NE), ("select", NE * P), ("select_lora", P)])
SMALLS, SMALL_COLS = offsets([
    ("c_gate", 2 * FT * NE), ("c_gate_bias", 2 * NE), ("c_up_bias", NE * 2), ("c_sw_bias", NE * 2),
    ("c_down_bias", H), ("f_gate", FT * NE), ("dt_w", FT * MH), ("dt_bias", MH), ("a_log", MH),
    ("conv_w", (IT + 2) * CONV_K), ("conv_b", IT + 2), ("skip", IT), ("norm_w", IT)])


def shape_constants():
    c = np.zeros((P, CONSTANT_COLS), np.float32)

    def put(name, a):
        first, width = CONSTANTS[name]
        c[:a.shape[0], first:first + width] = a.reshape(a.shape[0], width)

    i = np.arange(P)
    same = i[:, None] // S == i[None, :] // S
    put("ident", np.eye(P, dtype=np.float32))
    put("mean", np.full((P, P), 1.0 / H, np.float32))
    rope = np.zeros((P, P), np.float32)
    rope[i[1::2], i[0::2]] = -1.0
    rope[i[0::2], i[1::2]] = 1.0
    put("rope", rope)
    put("causal", np.where(same & (i[None, :] <= i[:, None]), 0.0, MASKED).astype(np.float32))
    put("batch", np.where(same, 0.0, MASKED).astype(np.float32))
    put("upto", (same & (i[:, None] <= i[None, :])).astype(np.float32))
    put("after", (same & (i[:, None] > i[None, :])).astype(np.float32))

    def angles(n, dim):
        exponent = (np.arange(0, dim, 2, dtype=np.float32) / np.float32(dim)).astype(np.float64)
        inv = np.float32(1.0) / (10000.0 ** exponent).astype(np.float32)
        f = np.arange(n, dtype=np.float32)[:, None] * inv[None, :]
        return np.repeat(f, 2, axis=1)

    fb = np.tile(angles(S, HD).T, (HPT, 1))
    put("cos_b", np.cos(fb))
    put("sin_b", np.sin(fb))
    fq = angles(S, XQ).T
    sign_q = np.where(np.arange(XQ) < XQ // 2, -1.0, 1.0).astype(np.float32)[:, None]
    tiles = lambda a: a.reshape(QT, P, S).transpose(1, 0, 2)
    put("cos_q", tiles(np.cos(fq)))
    put("sin_q", tiles(np.sin(fq) * sign_q))
    e = np.arange(NE)
    put("lower", np.broadcast_to((e[None, :] < e[:, None]).astype(np.float32).reshape(1, -1), (P, NE * NE)))
    put("select", np.repeat(np.eye(NE, dtype=np.float32), P, axis=1))
    put("select_lora", np.where(i[None, :] // LORA == e[:, None], 2.0, 0.0).astype(np.float32))
    fk = angles(KT * P, CD)
    sign_k = np.where(np.arange(CD) < CD // 2, -1.0, 1.0).astype(np.float32)[None, :]
    by_tile = lambda a: np.ascontiguousarray(a.reshape(KT, P, CD).transpose(1, 0, 2))
    return c, np.stack([by_tile(np.cos(fk)), by_tile(np.sin(fk) * sign_k)]).astype(np.float32)


def lay_out(i):
    def tile(w, k, m):
        return w[k * P:(k + 1) * P, m * P:(m + 1) * P]

    def rows(a):
        return np.concatenate([a, np.zeros((P - a.shape[0], a.shape[1]), a.dtype)]) if a.shape[0] < P else a

    chunks = []

    def chunk(*tiles):
        chunks.append(np.concatenate(tiles, axis=1))

    wq, wkv, wo = i["L0_xattn_Wq"].T, i["L0_xattn_Wkv_expand"].T, i["L0_xattn_Wout"].T
    chunk(*[tile(wkv, 0, FT + m) for m in range(FT)], *[tile(wkv, 0, m) for m in range(FT)])
    for f in range(FT):
        chunk(*[tile(wq, k, f) for k in range(FT)])

    def projection(w):
        for m in range(0, FT, 2):
            chunk(*[tile(w, k, n) for n in (m, m + 1) for k in range(FT)])

    projection(wo)
    w = i["L0_attn_w_qkv"]
    for k in range(0, FT, 2):
        chunk(*[tile(w, n, 2 * FT + m) for n in (k, k + 1) for m in range(FT)])
    for f in range(FT):
        for o in (0, FT):
            chunk(*[tile(w, k, o + f) for k in range(FT)])
    projection(i["L0_attn_w_proj"])

    def up_c(e):
        w, o = (i["L0_ffn_Wup"][e], 0) if e < GATED else (i["L0_ffn_Wsu"], 2 * (e - GATED))
        for m in range(2):
            chunk(*[tile(w, k, o + m) for k in range(FT)])

    def sw_c(e):
        w = i["L0_ffn_Wsw"][e] if e < GATED else i["L0_ffn_Wsa"]
        chunk(*[tile(w, k, m) for m in range(2) for k in range(2)])

    def down_c(e):
        w = i["L0_ffn_Wdn"][e] if e < GATED else i["L0_ffn_Wsd"][(e - GATED) * FF:(e - GATED + 1) * FF]
        for m in range(0, FT, 2):
            chunk(*[tile(w, k, n) for n in (m, m + 1) for k in range(2)])

    for _ in range(2):
        up_c(0)
        sw_c(0)
        up_c(1)
        for e in range(1, NE):
            down_c(e - 1)
            sw_c(e)
            if e < NE - 1:
                up_c(e + 1)
        down_c(NE - 1)

    wq = i["L1_xattn_Wq"].T
    turn = (np.arange(XQ) + XQ // 2) % XQ
    for h in range(XH):
        kc = i["L1_xattn_w_kc_q"][h]
        chunk(*[tile(wq, k, h) for k in range(FT)], kc, rows(i["L1_xattn_W_kr"][h].T))
        chunk(kc[:, turn], rows(i["L1_xattn_W_qr"][h].T))
    wo = i["L1_xattn_Wo"].T
    lat = lambda h: i["L1_xattn_w_kc_kv"][h].T
    out = lambda h: [tile(wo, h, m) for m in range(FT)]
    chunk(lat(0))
    for h in range(1, XH):
        chunk(lat(h), *out(h - 1))
    chunk(*out(XH - 1))

    w = i["L1_attn_W_in"].T
    four = lambda m: [tile(w, k, m) for k in range(FT)]
    chunk(*four(2 * IT), *four(2 * IT + 1))
    for m in range(0, IT, 2):
        chunk(*four(IT + m), *four(IT + m + 1))
        chunk(*four(m), *four(m + 1))
    wo = i["L1_attn_W_out"].T
    for k in range(0, IT, 2):
        chunk(*[tile(wo, n, m) for n in (k, k + 1) for m in range(FT)])

    lora_a = i["L1_ffn_A"].transpose(1, 0, 2).reshape(H, NE * LORA)
    lora_b = i["L1_ffn_B"].reshape(NE * LORA, H)
    chunk(*[tile(lora_a, k, 0) for k in range(FT)])
    wide = lambda w: chunk(*[tile(w, k, m) for m in range(2) for k in range(FT)])
    deep = lambda w: chunk(*[tile(w, k, m) for m in range(FT) for k in range(2)])
    wide(i["L1_ffn_Wg"][0])
    wide(i["L1_ffn_Wu"][0])
    chunk(lora_b)
    for e in range(1, NE):
        wide(i["L1_ffn_Wg"][e])
        wide(i["L1_ffn_Wu"][e])
        deep(i["L1_ffn_Wd"][e - 1])
    deep(i["L1_ffn_Wd"][NE - 1])

    widths = [w for _, body, reps in stream_plan() for _ in range(reps) for w in body]
    assert [c.shape for c in chunks] == [(P, w) for w in widths]
    stream = np.concatenate([np.ascontiguousarray(c).reshape(-1) for c in chunks])

    small = np.zeros((P, SMALL_COLS), np.float32)

    def put(name, a):
        first, width = SMALLS[name]
        small[:a.shape[0], first:first + width] = a.reshape(a.shape[0], width)

    every = lambda a: np.broadcast_to(a.reshape(1, -1), (P, a.size))
    put("c_gate", i["L0_ffn_Wg"].reshape(2, FT, P, NE).transpose(2, 0, 1, 3))
    put("c_gate_bias", every(i["L0_ffn_bg"]))
    up_bias = np.concatenate([i["L0_ffn_bup"], i["L0_ffn_bsu"].reshape(2, FF)])
    sw_bias = np.concatenate([i["L0_ffn_bsw"], i["L0_ffn_bsa"][None], i["L0_ffn_bsa"][None]])
    put("c_up_bias", up_bias.reshape(NE, 2, P).transpose(2, 0, 1))
    put("c_sw_bias", sw_bias.reshape(NE, 2, P).transpose(2, 0, 1))
    put("c_down_bias", np.concatenate([i["L0_ffn_bdn"], i["L0_ffn_bsd"][None], np.zeros((1, H), np.float32)]))
    put("f_gate", i["L1_ffn_gate_w"].reshape(FT, P, NE).transpose(1, 0, 2))
    put("dt_w", np.ascontiguousarray(w[:, 2 * INNER + 2 * MN:]).reshape(FT, P, MH).transpose(1, 0, 2))
    put("dt_bias", every(i["L1_attn_dt_bias"]))
    put("a_log", every(i["L1_attn_A_log"]))
    put("conv_w", i["L1_attn_conv_w"].reshape(IT + 2, P, CONV_K).transpose(1, 0, 2))
    put("conv_b", i["L1_attn_conv_b"].reshape(IT + 2, P).T)
    put("skip", np.repeat(i["L1_attn_D_param"], MP).reshape(IT, P).T)
    put("norm_w", i["L1_attn_norm_w"].reshape(IT, P).T)

    constants, rope_k = shape_constants()
    ctx = i["ctx_512"]
    tiles = np.concatenate([ctx, np.zeros((B, KT * P - CTX, CD), np.float32)], axis=1)
    return {
        "x": np.ascontiguousarray(i["x"].reshape(T, FT, P).transpose(2, 1, 0)),
        "ctx_first": np.ascontiguousarray(ctx[:, :S].reshape(T, CD).T),
        "ctx": np.ascontiguousarray(tiles.reshape(B, KT, P, CD).transpose(0, 2, 1, 3)),
        "weights": stream, "small": small, "constants": constants, "rope_k": rope_k,
    }


def perceiver_stack(nc, x_in, ctx_first, ctx_in, weights, small_in, constants_in, rope_k_in, x_out):
    starts = plan_starts()
    last_stage = LAST_STAGE

    with ExitStack() as held:
        def sb(name, shape, dt=F32, scope=None):
            return (scope or held).enter_context(nc.sbuf_tensor(name, shape, dt))

        def sem(name):
            return held.enter_context(nc.semaphore(name))

        x = sb("x", [P, FT, T])
        landing = sb("landing", [P, 2, CHUNK])
        wpair = sb("wpair", [P, 2, 2, CHUNK], F32R)
        const = sb("const", [P, CONSTANT_COLS])
        small = sb("small", [P, SMALL_COLS])
        eps = sb("eps", [P, 1])
        gate_w = sb("gate_w", [P, 2, 3, FT, NE], F32R)
        zero_b = sb("zero_b", [P, T], BF16)
        big = sb("big", [P, B * XH * S])
        psum = held.enter_context(nc.psum_tensor("psum", [P, 8, 512], F32))

        def bank(k):
            return psum[:, k, :]

        def by_batch(ap):
            return ap.rearrange("p (b s) -> p b s", s=S)

        def over_batches(ap):
            return ap.unsqueeze(1).broadcast_to([P, B, S])

        def constant(name, rows=P):
            first, width = CONSTANTS[name]
            return const[0:rows, first:first + width]

        def small_at(name, rows=P):
            first, width = SMALLS[name]
            return small[0:rows, first:first + width]

        ln_scope = ExitStack()
        xn = sb("xn", [P, 2, FT, T], F32R, ln_scope)
        xc = sb("xc", [P, FT, T], F32, ln_scope)
        sq = sb("sq", [P, FT, T], F32, ln_scope)
        rstd = sb("rstd", [P, T], F32, ln_scope)

        with ExitStack() as scope:
            first_pair = sb("first_pair", [P, 2, T], F32R, scope)
            first_raw = sb("first_raw", [P, T], F32, scope)
            ident_b = sb("ident_b", [P, P], BF16, scope)
            mask_b = sb("mask_b", [P, 2, G, P], BF16, scope)
            q_raw = sb("q_raw", [P, T], F32, scope)
            k_raw = sb("k_raw", [P, T], F32, scope)
            q_t = sb("q_t", [P, T], F32, scope)
            k_t = sb("k_t", [P, FT, T], F32, scope)
            turned = sb("turned", [P, 2, T], F32, scope)
            v_tok = sb("v_tok", [P, G, H], F32, scope)
            prob = sb("prob", [P, HPT, G, P], F32, scope)
            prob_t = sb("prob_t", [P, 2, G, P], F32, scope)
            neg_max = sb("neg_max", [P, HPT, G], F32, scope)
            row_sum = sb("row_sum", [P, HPT, G], F32, scope)
            row_inv = sb("row_inv", [P, HPT, G], F32, scope)
            heads_out = sb("heads_out", [P, 2, FT, T], F32R, scope)
        with ExitStack() as scope:
            wide_w = sb("wide_w", [P, NE, T], F32, scope)
            gate_s = sb("gate_s", [P, 8, G, NE], F32, scope)
            pairs_s = sb("pairs_s", [P, 2, G, NE, NE], F32, scope)
            gate_col = sb("gate_col", [P, 4, G, 1], F32, scope)
            w_rows = sb("w_rows", [NE, T], F32, scope)
            hid = sb("hid", [P, 2, T], F32, scope)
            hid_pair = sb("hid_pair", [P, 2, 2, T], F32R, scope)
            act_o = sb("act_o", [P, 2, T], F32, scope)
            mid = sb("mid", [P, 2, T], F32, scope)
            mid_pair = sb("mid_pair", [P, 2, 2, T], F32R, scope)
            lora_h = sb("lora_h", [P, T], F32, scope)
            lora_w = sb("lora_w", [P, T], F32, scope)
            lora_pair = sb("lora_pair", [P, 2, T], F32R, scope)
        with ExitStack() as scope:
            hk_pair = sb("hk_pair", [P, 2, T], F32R, scope)
            by_cos, by_sin = sq, xc
            turned_pair = sb("turned_pair", [P, 2, 2, QT, T], F32R, scope)
            absorb_pair = sb("absorb_pair", [P, 2, 2, QT * P], F32R, scope)
        with ExitStack() as scope:
            conv_in = sb("conv_in", [P, 2, B, S + CONV_K - 1], F32, scope)
            conv_acc = sb("conv_acc", [P, 2, T], F32, scope)
            bc_t = sb("bc_t", [P, 2, T], F32, scope)
            dt_s = sb("dt_s", [P, 5, G * MH], F32, scope)
            exp_a = sb("exp_a", [P, MH], F32, scope)
            g_mask = sb("g_mask", [P, G, P], F32, scope)
            xs_t = sb("xs_t", [P, 2, 2, T], F32, scope)
            silu_g = sb("silu_g", [P, 2, 2, T], F32, scope)
            decay_in = sb("decay_in", [P, 2, G, 4, P], F32R, scope)
            a_pair = sb("a_pair", [P, 2, G * MH], F32R, scope)
            after_r = sb("after_r", [P, P], F32R, scope)
            decay = sb("decay", [P, G, 4, P], F32, scope)
            mix = sb("mix", [P, G, 4, P], F32, scope)
            xdt = sb("xdt", [P, G, 4, MP], F32, scope)
            y_sum = sb("y_sum", [P, 2, T], F32, scope)
            y_gated = sb("y_gated", [P, 2, T], F32, scope)
            y_sq = sb("y_sq", [P, 2, T], F32, scope)
            sq_sum = sb("sq_sum", [P, T], F32, scope)
            gated_pair = decay_in[:, :, :, :, :].rearrange("p a g h t -> p (a g) (h t)").rearrange(
                "p (k a) t -> p k a t", a=2)
        with ExitStack() as scope:
            ctx_pair = sb("ctx_pair", [P, 2, 2, T], F32R, scope)
            lat_pair = sb("lat_pair", [P, 2, 2, T], F32R, scope)
        ln_scope.close()
        with ExitStack() as scope:
            kv_t = sb("kv_t", [P, 2, 2, CTX + 1], F32R, scope)
            expo = sb("expo", [P, 2, 2, CTX + 1], F32, scope)
            expo_t = sb("expo_t", [P, 4, 2, 512], F32R, scope)
            q_pair = sb("q_pair", [P, 2, 2, 256], F32R, scope)
            out_c = sb("out_c", [P, 256], F32, scope)
            diag = sb("diag", [P, 2, 2, P], F32, scope)
            part_max = sb("part_max", [P, 2, 2], F32, scope)
            neg_m = sb("neg_m", [P, 2], F32, scope)
            part_sum = sb("part_sum", [P, 2, 2, 3], F32, scope)
            sums = sb("sums", [P, 2, 2], F32, scope)
            kv_pair = sb("kv_pair", [P, 2, 2, KT, CD], F32R, scope)
            rope_k = sb("rope_k", [P, 2, KT, CD], F32, scope)
            kv = sb("kv", [P, KT, CD], F32, scope)
            kv_turn = sb("kv_turn", [P, KT, CD], F32, scope)

        inputs_in = sem("inputs_in")
        smalls_in = sem("smalls_in")
        chunk_in = [sem("chunk_in_0"), sem("chunk_in_1")]
        chunk_high = sem("chunk_high")
        chunk_split = sem("chunk_split")
        pool_started = sem("pool_started")
        chunk_used = sem("chunk_used")
        setup = sem("setup")
        x_ready = sem("x_ready")
        ln_mean, ln_centred, ln_squared, ln_var = sem("ln_mean"), sem("ln_centred"), sem("ln_squared"), sem("ln_var")
        ln_log, ln_rstd, ln_normal = sem("ln_log"), sem("ln_rstd"), sem("ln_normal")
        ln_high, ln_low = sem("ln_high"), sem("ln_low")
        stored = sem("stored")

        v_done, keys_done = sem("v_done"), sem("keys_done")
        q_in, k_in, v_in = sem("q_in"), sem("k_in"), sem("v_in")
        qk_turned, rope_steps = sem("qk_turned"), sem("rope_steps")
        scores, maxed, expd = sem("scores"), sem("maxed"), sem("expd")
        row_inverted, normal = sem("row_inverted"), sem("normal")
        prob_turned, prob_in = sem("prob_turned"), sem("prob_in")
        attended, heads_high, heads_low = sem("attended"), sem("heads_high"), sem("heads_low")
        heads_read = sem("heads_read")
        out_done = sem("out_done")
        logits, logits_in = sem("logits"), sem("logits_in")
        gated, gate_exp = sem("gated"), sem("gate_exp")
        gate_step = sem("gate_step")
        rows_turned, rows_in = sem("rows_turned"), sem("rows_in")
        spread, spread_in = sem("spread"), sem("spread_in")
        first, second = sem("first"), sem("second")
        hid_in, hid_high, hid_low = sem("hid_in"), sem("hid_high"), sem("hid_low")
        silu_done, mid_step = sem("silu_done"), sem("mid_step")
        mid_high, mid_low = sem("mid_high"), sem("mid_low")
        lora_done, lora_in = sem("lora_done"), sem("lora_in")
        mixed_out = sem("mixed_out")
        second_in = sem("second_in")

        hk_done, hk_high, hk_low = sem("hk_done"), sem("hk_high"), sem("hk_low")
        absorbed, absorb_high, absorb_low = sem("absorbed"), sem("absorb_high"), sem("absorb_low")
        q_big, q_turned = sem("q_big"), sem("q_turned")
        turn_step = sem("turn_step")
        rope_high, rope_low = sem("rope_high"), sem("rope_low")
        q_lat, q_lat_in = sem("q_lat"), sem("q_lat_in")
        tables_in, ctx_loaded = sem("tables_in"), sem("ctx_loaded")
        kv_step = sem("kv_step")
        values_high, values_split = sem("values_high"), sem("values_split")
        keys_t, keys_high, keys_low = sem("keys_t"), sem("keys_high"), sem("keys_low")
        qu_high, qu_low = sem("qu_high"), sem("qu_low")
        scored = sem("scored")
        max_part, max_done = sem("max_part"), sem("max_done")
        exp_done = sem("exp_done")
        summed, inverted, diagonal = sem("summed"), sem("inverted"), sem("diagonal")
        exp_t, exp_t_high, exp_t_low = sem("exp_t"), sem("exp_t_high"), sem("exp_t_low")
        context_sum, context_in = sem("context_sum"), sem("context_in")
        context_done = sem("context_done")
        ctx_high, ctx_low = sem("ctx_high"), sem("ctx_low")
        lat_done, lat_high, lat_low = sem("lat_done"), sem("lat_high"), sem("lat_low")
        d_out = sem("d_out")
        bc_done, conv_pad = sem("bc_done"), sem("conv_pad")
        conv_step, conv_silu = sem("conv_step"), sem("conv_silu")
        dt_done, dt_step, dt_exp, a_exp = sem("dt_done"), sem("dt_step"), sem("dt_exp"), sem("a_exp")
        g_done, g_masked = sem("g_done"), sem("g_masked")
        xs_done, gate_done, xs_copied, gate_silu = sem("xs_done"), sem("gate_done"), sem("xs_copied"), sem("gate_silu")
        decay_low = sem("decay_low")
        decay_ready, decay_sum, decay_exp, mixed = sem("decay_ready"), sem("decay_sum"), sem("decay_exp"), sem("mixed")
        xs_turned, xdt_ready = sem("xs_turned"), sem("xdt_ready")
        y_done, y_step, y_squared = sem("y_done"), sem("y_step"), sem("y_squared")
        norm_sum, norm_log, norm_inv = sem("norm_sum"), sem("norm_log"), sem("norm_inv")
        gh_high, gh_low = sem("gh_high"), sem("gh_low")
        e_out, e_scaled = sem("e_out"), sem("e_scaled")

        block = held.enter_context(nc.Block())

        def chunk_regions():
            n = at = 0
            for stage, widths, reps in stream_plan():
                yield stage, n, at, widths, reps
                n += len(widths) * reps
                at += sum(widths) * P * reps

        def run_region(eng, region, step):
            _, n0, at0, widths, reps = region
            ats = [at0 + P * sum(widths[:j]) for j in range(len(widths))]
            if reps == 1:
                for j, w in enumerate(widths):
                    step(n0 + j, (n0 + j) // 2, ats[j], (n0 + j) % 2, w)
                return
            first = 0
            if n0 == 0:
                for j, w in enumerate(widths):
                    step(j, 0, ats[j], j % 2, w)
                first = 1
            with eng.Fori(first, reps) as i:
                for j, w in enumerate(widths):
                    step(n0 + j + i * len(widths), (n0 + j) // 2 + i * (len(widths) // 2),
                         ats[j] + i * (sum(widths) * P), (n0 + j) % 2, w)

        def unslotted(n):
            return isinstance(n, int) and n < 2

        REGIONS = [r for r in chunk_regions() if STAGES.index(r[0][0]) <= STAGES.index(last_stage)]

        def weight(slot, part, t, rows=P):
            return wpair[0:rows, slot, part, t * P:(t + 1) * P]

        @block.sync
        def _(sp):
            sp.dma_start(x[:, :, :], x_in).then_inc(inputs_in, 16)
            sp.dma_start(const[:, :], constants_in).then_inc(smalls_in, 16)
            sp.dma_start(small[:, :], small_in).then_inc(smalls_in, 16)
            sp.dma_start(first_raw[:, :], ctx_first).then_inc(inputs_in, 16)

            def load(n, _, at, slot, width):
                if not unslotted(n):
                    sp.wait_ge(chunk_split, n - 1)
                sp.dma_start(landing[:, slot, 0:width],
                             weights[bass.ds(at, P * width)].rearrange("(p n) -> p n", p=P)
                             ).then_inc(chunk_in[slot], 16)

            for region in REGIONS:
                if region[0] == "D1":
                    sp.wait_ge(x_ready, 4 * 3)
                    sp.dma_start(rope_k[:, :, :, :], rope_k_in.rearrange("a p k d -> p a k d")).then_inc(tables_in, 16)
                    sp.dma_start(kv[:, :, :], ctx_in[0]).then_inc(ctx_loaded, 16)
                run_region(sp, region, load)
                if region[0] == "D1":
                    with sp.Fori(1, B) as b:
                        sp.wait_ge(keys_t, 4 * b)
                        sp.wait_ge(values_split, b)
                        sp.dma_start(kv[:, :, :], ctx_in[bass.ds(b, 1)].rearrange("a p k d -> (a p) k d")
                                     ).then_inc(ctx_loaded, 16)

            sp.wait_ge(x_ready, 4 * (STAGES.index(last_stage) + 1))
            sp.dma_start(x_out, x[:, :, :]).then_inc(stored, 16)
            sp.wait_ge(stored, 16)

        @block.gpsimd
        def _(pool):
            def split(n, use, _, slot, width):
                pool.wait_ge(chunk_in[slot], 16 * use + 16)
                if not unslotted(n):
                    pool.wait_ge(chunk_used, n - 1)
                pool.sem_inc(pool_started, 1)
                pool.tensor_scalar(wpair[:, slot, 0, 0:width], landing[:, slot, 0:width], 1.0, 1.0,
                                   ALU.mult, ALU.mult).then_inc(chunk_high, 1)
                pool.wait_ge(chunk_high, n + 1)
                pool.tensor_tensor(wpair[:, slot, 1, 0:width], landing[:, slot, 0:width],
                                   wpair[:, slot, 0, 0:width].bitcast(F32), ALU.subtract
                                   ).then_inc(chunk_split, 1)

            def context_steps(b, buffer, reused):
                half = CD // 2
                cos, sin = rope_k[:, 0, :, :], rope_k[:, 1, :, :]
                pool.wait_ge(ctx_loaded, 16 * b + 16)
                pool.tensor_tensor(kv_turn[:, :, 0:half], kv[:, :, half:CD], sin[:, :, 0:half], ALU.mult)
                pool.tensor_tensor(kv_turn[:, :, half:CD], kv[:, :, 0:half], sin[:, :, half:CD],
                                   ALU.mult).then_inc(kv_step, 1)
                yield
                pool.wait_ge(kv_step, 3 * b + 1)
                pool.tensor_tensor(kv[:, :, :], kv[:, :, :], cos, ALU.mult).then_inc(kv_step, 1)
                yield
                pool.wait_ge(kv_step, 3 * b + 2)
                pool.tensor_tensor(kv[:, :, :], kv[:, :, :], kv_turn[:, :, :], ALU.add).then_inc(kv_step, 1)
                yield
                pool.wait_ge(kv_step, 3 * b + 3)
                if reused:
                    pool.wait_ge(context_sum, 4 * b - 4)
                pool.sem_inc(pool_started, 1)
                pool.tensor_scalar(kv_pair[:, buffer, 0, :, :], kv[:, :, :], 1.0, 1.0, ALU.mult, ALU.mult
                                   ).then_inc(values_high, 1)
                yield
                pool.wait_ge(values_high, b + 1)
                pool.tensor_tensor(kv_pair[:, buffer, 1, :, :], kv[:, :, :],
                                   kv_pair[:, buffer, 0, :, :].bitcast(F32), ALU.subtract
                                   ).then_inc(values_split, 1)
                yield

            def whole(steps):
                for _ in steps:
                    pass

            def decays_low(i):
                upto = constant("upto").unsqueeze(1).broadcast_to([P, 4, P])
                a_low = a_pair[:, 1, :].bitcast(F32).rearrange("p (g h) -> p g h", h=MH)
                for g in range(G):
                    pool.tensor_tensor(decay_in[:, 1, g, :, :], upto,
                                       a_low[:, g, bass.ds(4 * i, 4)].unsqueeze(2).broadcast_to([P, 4, P]), ALU.mult
                                       ).then_inc(decay_low, 1)

            for region in REGIONS:
                if region[0] == "E" and region[1] == starts["E"] + 1:
                    _, n0, at0, widths, reps = region

                    def split_chunk(i, j):
                        split(n0 + 2 * i + j, (n0 + j) // 2 + i, at0, (n0 + j) % 2, widths[j])

                    split_chunk(0, 0)
                    pool.wait_ge(dt_step, 7)
                    decays_low(0)
                    with pool.Fori(0, reps - 1) as i:
                        split_chunk(i, 1)
                        split(n0 + 2 + 2 * i, n0 // 2 + 1 + i, at0, n0 % 2, widths[0])
                        pool.wait_ge(decay_sum, 4 * i + 4)
                        decays_low(i + 1)
                    split_chunk(reps - 1, 1)
                    continue
                if region[0] != "D1":
                    run_region(pool, region, split)
                    continue
                _, n0, at0, widths, _ = region
                pool.wait_ge(tables_in, 16)
                steps = context_steps(0, 0, False)
                for part in range(5):
                    run_region(pool, ("D1", n0 + 6 * part, at0 + 3 * part * sum(widths) * P, widths, 3), split)
                    next(steps)
                run_region(pool, ("D1", n0 + 30, at0 + 15 * sum(widths) * P, widths, 1), split)
                whole(context_steps(1, 1, False))
                with pool.Fori(1, B // 2) as i:
                    for j in range(2):
                        whole(context_steps(2 * i + j, j, True))

        CB, DB, EB, FB = starts["C"], starts["D1"], starts["E"], starts["F"]
        D3B = starts["D3"]
        BB = starts["B"]
        A_OUT, B_OUT, E_OUT = 1 + FT, BB + 2 + 2 * FT, EB + 1 + IT
        SPREAD_0 = (0, GATED, 2 * GATED)
        GATE_STEPS = (12, 12, 16)
        GATE_0 = (0, 12, 24)
        LN_BANKS = ((6, 7),) * 3 + ((0, 1),) * 3
        ROW_CHUNKS = ((0, 400), (400, 400), (800, 400), (1200, 401))

        C_CHUNKS = 5 * NE

        def c_chunks(p, e):
            base = CB + C_CHUNKS * p
            return (*((base, base + 1) if isinstance(e, int) and e == 0 else (base + 5 * e - 2, base + 5 * e - 1)),
                    base + 5 * e + 2)

        def turned_batch(i, k, last):
            return {1: 2 * i + 1, 5: None if last else 2 * i + 2}.get(k)

        TURN_BANKS = (4, 5, 7)

        def context_groups(k, last):
            order = [("exps", q) for q in range(3, 7)]
            if turned_batch(0, k, last) is not None:
                order = [g for part, exps in enumerate(order) for g in (exps, ("keys", part))]
            before = [("exps", q) for q in range(3)] + order
            return [(*g, TURN_BANKS[n % 3], before[n]) for n, g in enumerate(order)]

        def f_chunks(e):
            return (FB + 1, FB + 2) if isinstance(e, int) and e == 0 else (FB + 3 * e + 1, FB + 3 * e + 2)

        def runs(stage):
            return STAGES.index(stage) <= STAGES.index(last_stage)

        @block.tensor
        def _(pe):
            def product(out, w, act, start=False, stop=False):
                pe.matmul(out, w(0), act(0), start=start, stop=False)
                pe.matmul(out, w(0), act(1), start=False, stop=False)
                return pe.matmul(out, w(1), act(0), start=False, stop=stop)

            def tokens(pair, k):
                return lambda part: pair[:, part, k, :]

            def tile_of(slot, t):
                return lambda part: weight(slot, part, t)

            def chunk_ready(n):
                pe.wait_ge(chunk_split, n + 1)

            def open_sums():
                for m in range(FT):
                    pe.matmul(bank(4 + m), zero_b[:, 0:P], zero_b[:, :], start=True, stop=False)

            def layer_norm(k, meanwhile=None):
                mean_bank, var_bank = LN_BANKS[k]
                if not k:
                    pe.wait_ge(inputs_in, 32)
                    pe.wait_ge(smalls_in, 32)
                for f in range(FT):
                    if k:
                        pe.wait_ge(x_ready, 4 * (k - 1) + f + 1)
                    mm = pe.matmul(bank(mean_bank), constant("mean"), x[:, f, :], start=f == 0, stop=f == FT - 1)
                mm.then_inc(ln_mean, 1)
                for f in range(FT):
                    pe.wait_ge(ln_squared, 4 * k + f + 1)
                    mm = pe.matmul(bank(var_bank), constant("mean"), sq[:, f, :], start=f == 0, stop=f == FT - 1)
                mm.then_inc(ln_var, 1)
                if meanwhile is not None:
                    meanwhile()

            def wide(slot, first_tile, act, out, kts=FT, close=True, norm=None):
                for k in range(kts):
                    if norm is not None:
                        pe.wait_ge(ln_low, 4 * norm + k + 1)
                    mm = product(out, tile_of(slot, first_tile + k), tokens(act, k),
                                 start=k == 0, stop=close and k == kts - 1)
                return mm

            TURNED = (1, 2)

            def attention_tile(u, h0, mask, rope, ahead):
                pe.wait_ge(q_in, u + 1)
                pe.wait_ge(k_in, u + 1)
                if rope:
                    pe.wait_ge(rope_steps, 6 * (u - FT) + 6)
                for h in range(HPT):
                    rows = slice(h * HD, (h + 1) * HD)
                    pe.matmul(bank(3 + h), ident_b[:, :], mask_b[:, mask, :, :].rearrange("p g k -> p (g k)"),
                              start=True, stop=False)
                    for g in range(G):
                        mm = pe.matmul(bank(3 + h)[:, g * P:(g + 1) * P], q_t[rows, g * P:(g + 1) * P],
                                       k_t[rows, 0 if rope else u, g * P:(g + 1) * P], start=False, stop=g == G - 1)
                    mm.then_inc(scores, 1)
                if ahead is not None:
                    ahead()

                def transposes(h):
                    pe.wait_ge(normal, HPT * u + h + 1)
                    if rope and ahead is not None and h == 1:
                        pe.wait_ge(rope_steps, 6 * (u + 1 - FT) + 1)
                    for g in range(G):
                        mm = pe.transpose(bank(TURNED[h % 2])[:, g * P:(g + 1) * P], prob[:, h, g, :],
                                          constant("ident"))
                    mm.then_inc(prob_turned, 1)

                def values(h):
                    pe.wait_ge(prob_in, HPT * u + h + 1)
                    if h == 0:
                        pe.wait_ge(heads_read, u + 1)
                    for g in range(G):
                        mm = pe.matmul(bank(7)[h * HD:(h + 1) * HD, g * P:(g + 1) * P],
                                       v_tok[:, g, h0 + h * HD:h0 + (h + 1) * HD], prob_t[:, h % 2, g, :],
                                       start=True, stop=True)
                    if h == HPT - 1:
                        mm.then_inc(attended, 1)

                transposes(0)
                transposes(1)
                values(0)
                transposes(2)
                values(1)
                transposes(3)
                values(2)
                values(3)

            def all_values(slot, g, act, kts, first_k=0, last=True):
                for k in range(kts):
                    mm = product(bank(g), lambda part, k=k: act(part, first_k + k)[:, g * P:(g + 1) * P],
                                 lambda part, k=k: wpair[:, slot, part, H * k:H * (k + 1)],
                                 start=first_k + k == 0, stop=last and k == kts - 1)
                return mm

            def out_projection(n0, tiles):
                pe.wait_ge(heads_low, tiles)
                for c in range(2):
                    chunk_ready(n0 + c)
                    slot = (n0 + c) % 2
                    wide(slot, 0, heads_out, bank(2 * c)).then_inc(out_done, 1)
                    wide(slot, FT, heads_out, bank(2 * c + 1)).then_inc(chunk_used, 1)

            def context_products():
                pe.wait_ge(setup, 7)
                chunk_ready(0)
                for g in range(G):
                    all_values(0, g, lambda part, k: first_pair[:, part, :], 1).then_inc(v_done, 1)
                for m in range(FT):
                    if m == 3:
                        pe.wait_ge(ln_log, 1)
                    product(bank(4 + m), tile_of(0, FT + m), lambda part: first_pair[:, part, :],
                            start=True, stop=True).then_inc(keys_done if m < FT - 1 else chunk_used, 1)

            def project(n, slot, k_bank, norm=None):
                chunk_ready(n)
                return wide(slot, 0, xn, bank(k_bank), norm=norm).then_inc(chunk_used, 1)

            layer_norm(0, context_products)
            pe.wait_ge(v_in, 4)
            project(1, 1, 0, norm=0)
            pe.wait_ge(k_in, FT)
            for u in range(FT):
                attention_tile(u, P * u, 0, False,
                               (lambda: project(u + 2, u % 2, 0)) if u < FT - 1 else None)
            out_projection(A_OUT, FT)

            if runs("B"):
                layer_norm(1)
                slot = BB % 2
                for c in range(2):
                    chunk_ready(BB + c)
                    pe.wait_ge(ln_low, 4 + 2 * c + 2)
                    for g in range(G):
                        mm = all_values((BB + c) % 2, g, lambda part, k: xn[:, part, k, :], 2, 2 * c, c == 1)
                        if c == 1 and g < G - 1:
                            mm.then_inc(v_done, 1)
                    mm.then_inc(chunk_used, 1)

                def queries_and_keys(f, first):
                    for side in range(2):
                        if first:
                            pe.wait_ge(v_in, G + side + 1)
                        project(BB + 2 + 2 * f + side, (slot, 1 - slot)[side], side)
                    if first:
                        pe.wait_ge(v_in, G + 3)
                    for side, (raw, arrived) in enumerate(((q_raw, q_in), (k_raw, k_in))):
                        pe.wait_ge(arrived, FT + f + 1)
                        pe.matmul(bank((2, 0)[side]), constant("rope"), raw[:, :], start=True, stop=True
                                  ).then_inc(qk_turned, 1)

                queries_and_keys(0, True)
                pe.wait_ge(v_in, 2 * G)
                for f in range(FT):
                    attention_tile(FT + f, P * f, 1, True,
                                   (lambda: queries_and_keys(f + 1, False)) if f < FT - 1 else None)
                out_projection(B_OUT, 2 * FT)

            def gate_products(p):
                pe.wait_ge(setup, 11)
                for k in range(FT):
                    mm = product(bank(4)[0:NE, :], lambda part, k=k: gate_w[:, part, p, k, :], tokens(xn, k),
                                 start=k == 0, stop=k == FT - 1)
                mm.then_inc(logits, 1)

            def turn_logits(p):
                pe.wait_ge(logits_in, p + 1)
                for g in range(G):
                    mm = pe.transpose(bank(4)[:, g * NE:(g + 1) * NE], w_rows[:, g * P:(g + 1) * P],
                                      constant("ident", NE)[:, 0:NE])
                mm.then_inc(gated, 1)

            def turn_rows(p):
                pe.wait_ge(gate_step, GATE_0[p] + GATE_STEPS[p])
                for g in range(G):
                    mm = pe.transpose(bank(5)[0:NE, g * P:(g + 1) * P], gate_s[:, 5, g, :], constant("ident"))
                mm.then_inc(rows_turned, 1)
                pe.wait_ge(rows_in, p + 1)

            def spread_rows(p, first_spread, experts):
                for e in range(experts):
                    if e >= 2:
                        pe.wait_ge(spread_in, first_spread + e - 1)
                    pe.matmul(bank(5 + e % 2), constant("select", NE)[:, e * P:(e + 1) * P], w_rows[:, :],
                              start=True, stop=True).then_inc(spread, 1)
                pe.wait_ge(spread_in, first_spread + experts)

            def two_tiles(n, slot, act, first_bank, signal, kts=FT, norm=None):
                chunk_ready(n)
                wide(slot, 0, act, bank(first_bank), kts, norm=norm).then_inc(signal, 1)
                wide(slot, kts, act, bank(first_bank + 1), kts).then_inc(chunk_used, 1)

            def down(n, slot, expert, last=False, chunks=1):
                for m in range(FT):
                    c, at = divmod(m, FT // chunks)
                    if at == 0:
                        chunk_ready(n + c)
                        if m == 0:
                            pe.wait_ge(mid_low, 2 * expert + 2)
                    for k in range(2):
                        mm = product(bank(4 + m), tile_of((slot + c) % 2, 2 * at + k),
                                     lambda part, k=k: mid_pair[:, part, k, :], stop=last and k == 1)
                    if at == FT // chunks - 1:
                        mm.then_inc(chunk_used, 1)
                    elif last:
                        mm.then_inc(mixed_out, 1)

            def up_tiles(n, slot, norm=None):
                for m in range(2):
                    chunk_ready(n + m)
                    wide((slot + m) % 2, 0, xn, bank(m), norm=norm if m == 0 else None).then_inc(chunk_used, 1)

            def second_products(p, e, n, slot):
                pe.wait_ge(hid_low, 2 * (NE * p + e) + 2)
                two_tiles(n, slot, hid_pair, 2, second, 2)

            if runs("C"):
                layer_norm(2)
            for p in range(2 if runs("C") else 0):
                cb = CB + C_CHUNKS * p
                if p:
                    pe.wait_ge(second_in, 3 * FT)
                up_tiles(cb, cb % 2, norm=None if p else 2)
                gate_products(p)
                second_products(p, 0, cb + 2, cb % 2)
                turn_logits(p)
                up_tiles(cb + 3, (cb + 1) % 2)
                turn_rows(p)
                spread_rows(p, SPREAD_0[p], GATED)
                for m in range(FT):
                    pe.matmul(bank(4 + m), small_at("c_down_bias", NE)[:, m * P:(m + 1) * P], w_rows[:, :],
                              start=True, stop=False)

                def expert_c(e, n, slot, last=False):
                    down(n, slot, NE * p + e - 1, chunks=2)
                    second_products(p, e, n + 2, slot)
                    if not last:
                        up_tiles(n + 3, 1 - slot)

                with pe.Fori(0, 3) as i:
                    for j in range(2):
                        expert_c(2 * i + j + 1, cb + 5 + 10 * i + 5 * j, (cb + 5 + 5 * j) % 2)
                expert_c(NE - 1, cb + 5 * NE - 5, (cb + 5 * NE - 5) % 2, True)
                down(cb + 5 * NE - 2, cb % 2, NE * p + NE - 1, True, chunks=2)

            if runs("D"):
                layer_norm(3)

                def absorbed_queries(h, buffer):
                    pe.wait_ge(rope_low, QT * h + QT)
                    for k in range(QT):
                        mm = product(bank(7), lambda part, k=k: absorb_pair[:, buffer, part, k * P:(k + 1) * P],
                                     lambda part, k=k: turned_pair[:, buffer, part, k, :],
                                     start=k == 0, stop=k == QT - 1)
                    mm.then_inc(q_lat, 1)

                def query_head(h, slot, buffer, before):
                    n = DB + 2 * h
                    chunk_ready(n)
                    if before:
                        pe.wait_ge(hk_low, h)
                    wide(slot, 0, xn, bank(0), norm=None if before else 3).then_inc(hk_done, 1)
                    chunk_ready(n + 1)
                    if before:
                        pe.wait_ge(q_lat_in, h)
                    for k in range(QT):
                        mm = product(bank(7)[:, k * P:(k + 1) * P],
                                     lambda part, k=k: weight(1 - slot, part, QT + k, XR),
                                     lambda part: weight(slot, part, FT + QT, XR), start=True, stop=True)
                    mm.then_inc(absorbed, 1)
                    pe.wait_ge(hk_low, h + 1)
                    for side in range(2):
                        if before:
                            pe.wait_ge(turn_step, 3 * QT * h - (2 * QT, 1)[side])
                        for k in range(QT):
                            mm = product(bank(1 + QT * side + k),
                                         tile_of(slot, FT + k) if side == 0 else tile_of(1 - slot, k),
                                         lambda part: hk_pair[:, part, :], start=True, stop=True)
                            mm.then_inc(chunk_used if k == QT - 1 else (q_big, q_turned)[side], 1)
                    pe.wait_ge(absorb_low, h + 1)
                    if before:
                        absorbed_queries(h - 1, 1 - buffer)

                slot = DB % 2
                query_head(0, slot, 0, False)
                with pe.Fori(0, (XH - 2) // 2) as i:
                    for j in (1, 2):
                        query_head(2 * i + j, slot, j % 2, True)
                query_head(XH - 1, slot, 1, True)
                pe.wait_ge(q_lat_in, XH)
                absorbed_queries(XH - 1, 1)

                def turn_keys(b, part, k_bank):
                    if part == 0:
                        pe.wait_ge(kv_step, 3 * b + 3)
                    for k in range(4 * part, min(4 * part + 4, KT)):
                        rows = P if k < KT - 1 else LASTK
                        at = (k - 4 * part) * P
                        mm = pe.transpose(bank(k_bank)[:, at:at + rows], kv[0:rows, k, :],
                                          constant("ident", rows)[:, 0:rows])
                    mm.then_inc(keys_t, 1)

                def score_row(i, k, r):
                    unit, buffer, keys = 8 * i + k, k % 2, (k // 4) % 2
                    if r == 0:
                        pe.wait_ge(qu_low, unit + 1)
                        if k % 4 == 0:
                            pe.wait_ge(keys_low, 4 * (2 * i + k // 4) + 4)
                    for c in range(4):
                        pe.wait_ge(exp_done, 6 * unit + 3 * r + (1, 1, 2, 3)[c])
                        product(bank(c)[:, 0:402],
                                lambda part: q_pair[:, buffer, part, r * P:(r + 1) * P],
                                lambda part, c=c: kv_t[:, keys, part, 400 * c:400 * c + 402],
                                start=True, stop=True).then_inc(scored, 1)

                def turn_exp(i, k, q, k_bank):
                    if q == 0:
                        pe.wait_ge(exp_done, 6 * (8 * i + k) + 9)
                    for t in range(2 * q, min(2 * q + 2, KT)):
                        rows = P if t < KT - 1 else LASTK
                        for r in range(2):
                            at = (t % 2) * 256 + r * P
                            mm = pe.transpose(bank(k_bank)[0:rows, at:at + P],
                                              expo[:, k % 2, r, t * P:t * P + rows], constant("ident"))
                    mm.then_inc(exp_t, 1)

                def add_values(i, k, q):
                    unit, buffer = 8 * i + k, (k // 4) % 2
                    if q == 0:
                        if k % 4 == 0:
                            pe.wait_ge(values_split, 2 * i + k // 4 + 1)
                        pe.wait_ge(diagonal, 2 * unit + 2)
                        pe.wait_ge(context_done, unit + 1)
                        pe.matmul(bank(6)[:, 256:512], constant("mean"),
                                  diag[:, k % 2, :, :].rearrange("p r q -> p (r q)"), start=True, stop=True)
                    pe.wait_ge(exp_t_low, 7 * unit + q + 1)
                    for t in range(2 * q, min(2 * q + 2, KT)):
                        rows = P if t < KT - 1 else LASTK
                        cols = slice((t % 2) * 256, (t % 2) * 256 + 256)
                        mm = product(bank(6)[:, 0:256],
                                     lambda part, t=t, rows=rows: kv_pair[0:rows, buffer, part, t, :],
                                     lambda part, rows=rows, cols=cols: expo_t[0:rows, q % 4, part, cols],
                                     start=t == 0, stop=t == KT - 1)
                    if q == 6:
                        mm.then_inc(context_sum, 1)

                def units(i, last):
                    for k in range(8):
                        unit, batch = 8 * i + k, turned_batch(i, k, last)
                        groups = iter(context_groups(k, last))

                        def turn():
                            for _ in range(1 if batch is None else 2):
                                kind, q, k_bank, (before, n) = next(groups)
                                if before == "keys":
                                    pe.wait_ge(keys_low, 4 * batch + n + 1)
                                else:
                                    pe.wait_ge(exp_t_low, 7 * unit + n + 1)
                                if kind == "keys":
                                    turn_keys(batch, q, k_bank)
                                else:
                                    turn_exp(i, k, q, k_bank)

                        def turn_ahead(q):
                            if q == 0:
                                pe.wait_ge(exp_t_low, 7 * unit + 7)
                            elif batch is not None:
                                pe.wait_ge(keys_low, 4 * batch + 5 - q)
                            if k < 7:
                                turn_exp(i, k + 1, q, TURN_BANKS[q])
                            elif not last:
                                turn_exp(i + 1, 0, q, TURN_BANKS[q])

                        if k < 7:
                            score_row(i, k + 1, 1)
                        elif not last:
                            score_row(i + 1, 0, 1)
                        for q in range(4):
                            add_values(i, k, q)
                            turn()
                        if k < 6:
                            score_row(i, k + 2, 0)
                        elif not last:
                            score_row(i + 1, k - 6, 0)
                        for q in range(3):
                            add_values(i, k, 4 + q)
                            turn_ahead(q)

                pe.wait_ge(q_lat_in, XH + 1)
                for part in range(4):
                    if part == 3:
                        pe.wait_ge(keys_low, 1)
                    turn_keys(0, part, TURN_BANKS[part % 3])
                for unit, r in ((0, 0), (0, 1), (1, 0)):
                    score_row(0, unit, r)
                for q in range(3):
                    turn_exp(0, 0, q, TURN_BANKS[q])
                with pe.Fori(0, B // 2 - 1) as i:
                    units(i, False)
                units(B // 2 - 1, True)

                def value_latents(h, slot, buffer):
                    chunk_ready(D3B + h)
                    pe.wait_ge(ctx_low, h + 1)
                    return product(bank(buffer), tile_of(slot, 0), lambda part: ctx_pair[:, buffer, part, :],
                                   start=True, stop=True)

                def latent_outputs(h, n, slot, first_tile, buffer, last=False):
                    chunk_ready(n)
                    pe.wait_ge(lat_low, h + 1)
                    for m in range(FT):
                        mm = product(bank(4 + m), tile_of(slot, first_tile + m),
                                     lambda part: lat_pair[:, buffer, part, :], stop=last)
                        if last and m < FT - 1:
                            mm.then_inc(d_out, 1)
                    mm.then_inc(chunk_used, 1)

                value_latents(0, D3B % 2, 0).then_inc(chunk_used, 1)
                pe.wait_ge(context_done, 4 * B + 1)
                open_sums()

                def latent_head(h, j):
                    slot = (D3B + j) % 2
                    value_latents(h, slot, j % 2).then_inc(lat_done, 1)
                    latent_outputs(h - 1, D3B + h, slot, 1, 1 - j % 2)

                with pe.Fori(0, 7) as i:
                    for j in (1, 2):
                        latent_head(2 * i + j, j)
                latent_head(XH - 1, XH - 1)
                latent_outputs(XH - 1, D3B + XH, (D3B + XH) % 2, 0, (XH - 1) % 2, True)

            if runs("E"):
                layer_norm(4)
                chunk_ready(EB)
                wide(EB % 2, 0, xn, bank(0), norm=4).then_inc(bc_done, 1)
                wide(EB % 2, FT, xn, bank(1)).then_inc(chunk_used, 1)
                dt_w = small_at("dt_w").rearrange("p (k h) -> p k h", h=MH)
                for g in range(G):
                    for k in range(FT):
                        mm = pe.matmul(bank(2)[:, g * MH:(g + 1) * MH], xc[:, k, g * P:(g + 1) * P], dt_w[:, k, :],
                                       start=k == 0, stop=k == FT - 1)
                mm.then_inc(dt_done, 1)
                pe.wait_ge(conv_silu, 2)
                for g in range(G):
                    cols = slice(g * P, (g + 1) * P)
                    mm = pe.matmul(bank(3)[:, cols], bc_t[:, 0, cols], bc_t[:, 1, cols], start=True, stop=True)
                mm.then_inc(g_done, 1)
                pe.wait_ge(dt_step, 1)
                pe.wait_ge(g_masked, 1)

                def mamba_outputs(i):
                    pe.wait_ge(mixed, 4 * i + 4)
                    for m in range(2):
                        pe.wait_ge(xdt_ready, 2 * i + 2)
                        for hh in range(2):
                            for g in range(G):
                                mm = pe.matmul(bank(4 + m)[hh * MP:(hh + 1) * MP, g * P:(g + 1) * P],
                                               xdt[:, g, 2 * m + hh, :], mix[:, g, 2 * m + hh, :],
                                               start=True, stop=True)
                        mm.then_inc(y_done, 1)

                def mamba_tiles(i, buffer, before):
                    n = EB + 1 + 2 * i
                    slot = (EB + 1) % 2
                    pe.wait_ge(xs_copied, 2 * i + 2)
                    two_tiles(n, slot, xn, 0, xs_done)
                    for g in range(G):
                        if g == 2 and before:
                            mamba_outputs(i - 1)
                        pe.wait_ge(decay_ready, 4 * i + g + 1)
                        if g >= 2:
                            pe.wait_ge(decay_exp, 4 * i + g - 1)
                        pe.wait_ge(decay_low, 4 * i + g + 1)
                        for part in range(2):
                            mm = pe.matmul(bank(6 + g % 2), after_r[:, :],
                                           decay_in[:, part, g, :, :].rearrange("p h t -> p (h t)"),
                                           start=part == 0, stop=part == 1)
                        mm.then_inc(decay_sum, 1)
                    if before:
                        pe.wait_ge(gate_silu, 2 * i)
                    two_tiles(n + 1, 1 - slot, xn, 2, gate_done)
                    pe.wait_ge(conv_silu, 2 * i + 4)
                    if before:
                        pe.wait_ge(y_step, 8 * i - 6)
                    for m in range(2):
                        for g in range(G):
                            cols = slice(g * P, (g + 1) * P)
                            mm = pe.transpose(bank(4 + m)[:, cols], xs_t[:, buffer, m, cols], constant("ident"))
                    mm.then_inc(xs_turned, 1)

                for i in range(2):
                    mamba_tiles(i, i, i > 0)
                with pe.Fori(1, IT // 4) as i:
                    for j in range(2):
                        mamba_tiles(2 * i + j, j, True)
                mamba_outputs(IT // 2 - 1)
                pe.wait_ge(y_step, 4 * IT)
                pe.matmul(bank(3), constant("mean"), sq_sum[:, :], start=True, stop=True).then_inc(norm_sum, 1)
                open_sums()

                def output_chunk(c, j, last=False):
                    n = E_OUT + c
                    chunk_ready(n)
                    pe.wait_ge(gh_low, 2 * c + 2)
                    for kk in range(2):
                        for m in range(FT):
                            mm = product(bank(4 + m), tile_of((E_OUT + j) % 2, FT * kk + m),
                                         lambda part, kk=kk: gated_pair[:, 2 * (j % 2) + kk, part, :],
                                         stop=last and kk == 1)
                            if last and kk == 1 and m < FT - 1:
                                mm.then_inc(e_out, 1)
                    mm.then_inc(chunk_used, 1)

                with pe.Fori(0, 3) as i:
                    for j in range(2):
                        output_chunk(2 * i + j, j)
                output_chunk(6, 0)
                output_chunk(7, 1, True)

            if runs("F"):
                layer_norm(5)
                chunk_ready(FB)
                wide(FB % 2, 0, xn, bank(7), norm=5).then_inc(chunk_used, 1)
                gate_products(2)
                two_tiles(FB + 1, (FB + 1) % 2, xn, 0, first)
                turn_logits(2)
                two_tiles(FB + 2, FB % 2, xn, 2, second)
                turn_rows(2)
                pe.matmul(bank(4), constant("select_lora", NE), w_rows[:, :], start=True, stop=True
                          ).then_inc(lora_done, 1)
                spread_rows(2, SPREAD_0[2], NE)
                chunk_ready(FB + 3)
                pe.wait_ge(lora_in, 4)
                for m in range(FT):
                    mm = product(bank(4 + m), tile_of((FB + 3) % 2, m), lambda part: lora_pair[:, part, :],
                                 start=True)
                mm.then_inc(chunk_used, 1)

                def expert_f(e, n, slot):
                    pe.wait_ge(silu_done, 2 * (2 * NE + e))
                    two_tiles(n, slot, xn, 0, first)
                    pe.wait_ge(mid_step, 4 * (2 * NE + e))
                    two_tiles(n + 1, 1 - slot, xn, 2, second)
                    down(n + 2, slot, 2 * NE + e - 1)

                with pe.Fori(0, 3) as i:
                    for j in range(2):
                        expert_f(2 * i + j + 1, FB + 4 + 6 * i + 3 * j, (FB + 3 * j) % 2)
                expert_f(NE - 1, FB + 22, FB % 2)
                down(FB + 25, (FB + 25) % 2, 3 * NE - 1, True)

        @block.scalar
        def _(act):
            def layer_norm(k):
                act.preload_act_table_set("natural_log_exp_and_others")
                for f in range(FT):
                    act.wait_ge(ln_centred, 4 * k + f + 1)
                    act.activation(sq[:, f, :], xc[:, f, :], ACT.Square).then_inc(ln_squared, 1)
                act.wait_ge(ln_var, k + 1)
                act.activation(rstd[:, :], bank(LN_BANKS[k][1]), ACT.Ln, bias=eps[:, 0:1]).then_inc(ln_log, 1)
                act.wait_ge(ln_log, k + 1)
                act.activation(rstd[:, :], rstd[:, :], ACT.Exp, scale=-0.5).then_inc(ln_rstd, 1)
                for f in range(FT):
                    act.wait_ge(ln_normal, 4 * k + f + 1)
                    act.copy(xn[:, 0, f, :], xc[:, f, :]).then_inc(ln_high, 1)

            def queries_in(u, n, rope):
                act.wait_ge(chunk_used, n + 1)
                act.mul((q_raw if rope else q_t)[:, :], bank(0), HD ** -0.5).then_inc(q_in, 1)

            def values_in(stage):
                for g in range(G):
                    act.wait_ge(v_done, G * stage + g + 1) if stage == 0 or g < G - 1 else act.wait_ge(chunk_used, BB + 2)
                    act.copy(v_tok[:, g, :], bank(g)).then_inc(v_in, 1)

            def attention_tile(u, f, ahead):
                def exps(h):
                    act.wait_ge(maxed, HPT * u + h + 1)
                    for g in range(G):
                        act.activation(prob[:, h, g, :], bank(3 + h)[:, g * P:(g + 1) * P], ACT.Exp,
                                       bias=neg_max[:, h, g:g + 1], accum_out=row_sum[:, h, g:g + 1]
                                       ).then_inc(expd, 1)

                def turned_in(h):
                    act.wait_ge(prob_turned, HPT * u + h + 1)
                    act.copy(prob_t[:, h % 2, :, :].rearrange("p g k -> p (g k)"), bank(1 + h % 2)).then_inc(prob_in, 1)

                for h in range(HPT):
                    exps(h)
                if ahead is not None:
                    ahead()
                for h in range(HPT):
                    turned_in(h)
                act.wait_ge(attended, u + 1)
                act.copy(heads_out[:, 0, bass.ds(f, 1), :].rearrange("p a t -> p (a t)"), bank(7)
                         ).then_inc(heads_high, 1)

            act.wait_ge(setup, 7)
            layer_norm(0)
            values_in(0)
            queries_in(0, 1, False)
            for u in range(FT):
                attention_tile(u, u, (lambda: queries_in(u + 1, u + 2, False)) if u < FT - 1 else None)
            if runs("B"):
                layer_norm(1)
                values_in(1)
                queries_in(FT, BB + 2, True)
                with act.Fori(0, FT - 1) as f:
                    attention_tile(FT + f, f, lambda: queries_in(FT + f + 1, BB + 4 + 2 * f, True))
                attention_tile(2 * FT - 1, FT - 1, None)

            def spread_copies(first_spread, count, first_bank, targets):
                for e in range(count):
                    act.wait_ge(spread, first_spread + e + 1)
                    act.copy(targets(e), bank(first_bank(e))).then_inc(spread_in, 1)

            def gate_exps(p, steps):
                act.wait_ge(logits, p + 1)
                act.copy(w_rows[:, :], bank(4)[0:NE, :]).then_inc(logits_in, 1)
                act.wait_ge(gate_step, GATE_0[p] + steps)
                act.activation(gate_s[:, 2, :, :], gate_s[:, 1, :, :], ACT.Exp).then_inc(gate_exp, 1)

            def expert_c(p, e, meanwhile=None):
                expert = NE * p + e
                *up, sw = c_chunks(p, e)
                if not (isinstance(expert, int) and expert == 0):
                    act.wait_ge(mid_step, 4 * expert)
                for m in range(2):
                    act.wait_ge(chunk_used, up[m] + 1)
                    act.activation(hid[:, m, :], bank(m), ACT.Identity,
                                   bias=small_at("c_up_bias")[:, bass.ds(2 * e + m, 1)]).then_inc(hid_in, 1)
                if meanwhile is not None:
                    meanwhile()
                for m in range(2):
                    act.wait_ge(second, expert + 1) if m == 0 else act.wait_ge(chunk_used, sw + 1)
                    act.activation(act_o[:, m, :], bank(2 + m), ACT.Silu,
                                   bias=small_at("c_sw_bias")[:, bass.ds(2 * e + m, 1)]).then_inc(silu_done, 1)

            if runs("C"):
                layer_norm(2)
                for p in range(2):
                    expert_c(p, 0, lambda: gate_exps(p, 3))
                    spread_copies(SPREAD_0[p], GATED, lambda e: 5 + e % 2, lambda e: wide_w[:, e, :])
                    with act.Fori(1, NE) as e:
                        expert_c(p, e)

            if runs("D"):
                layer_norm(3)

                def latent_queries_in(h):
                    act.wait_ge(q_lat, h + 1)
                    act.copy(big[:, :].rearrange("p (b c) -> p b c", b=B)[:, :, bass.ds(h * S, S)],
                             by_batch(bank(7))).then_inc(q_lat_in, 1)

                def query_head(h, buffer, before):
                    act.wait_ge(hk_done, h + 1)
                    act.copy(hk_pair[:, 0, :], bank(0)).then_inc(hk_high, 1)
                    act.wait_ge(absorbed, h + 1)
                    act.copy(absorb_pair[:, buffer, 0, :], bank(7)[:, 0:QT * P]).then_inc(absorb_high, 1)
                    for k in range(QT):
                        if k == QT - 1 and before:
                            latent_queries_in(h - 1)
                        act.wait_ge(turn_step, 3 * QT * h + QT + 2 * k + 2)
                        act.copy(turned_pair[:, buffer, 0, k, :], by_cos[:, k, :]).then_inc(rope_high, 1)

                act.preload_act_table_set("exp_and_others")
                act.sem_inc(q_lat_in, 1)
                query_head(0, 0, False)
                with act.Fori(0, (XH - 2) // 2) as i:
                    for j in (1, 2):
                        query_head(2 * i + j, j % 2, True)
                query_head(XH - 1, 1, True)
                latent_queries_in(XH - 1)

                def keys_in(b, buffer, part, k_bank):
                    act.wait_ge(keys_t, 4 * b + part + 1)
                    at, width = 512 * part, min(512, CTX - 512 * part)
                    act.copy(kv_t[:, buffer, 0, at:at + width], bank(k_bank)[:, 0:width]).then_inc(keys_high, 1)
                    if part == 3:
                        act.copy(kv_t[:, buffer, 0, CTX:CTX + 1], bank(k_bank)[:, width - 1:width]
                                 ).then_inc(keys_high, 1)

                def unit_queries(i, k):
                    act.copy(q_pair[:, k % 2, 0, :], big[:, bass.ds(256 * (8 * i + k), 256)]).then_inc(qu_high, 1)

                def exps(i, k, r):
                    act.wait_ge(max_done, 2 * (8 * i + k) + r + 1)
                    buffer = k % 2
                    act.activation(expo[:, buffer, r, 0:800].rearrange("p (c n) -> p c n", c=2),
                                   psum[:, 0:2, 0:400], ACT.Exp, bias=neg_m[:, r:r + 1],
                                   accum_out=part_sum[:, buffer, r, 0:1]).then_inc(exp_done, 1)
                    for c in (2, 3):
                        at, width = ROW_CHUNKS[c]
                        act.activation(expo[:, buffer, r, at:at + width], bank(c)[:, 0:width], ACT.Exp,
                                       bias=neg_m[:, r:r + 1], accum_out=part_sum[:, buffer, r, c - 1:c]
                                       ).then_inc(exp_done, 1)

                def exp_t_in(i, k, q, k_bank):
                    act.wait_ge(exp_t, 7 * (8 * i + k) + q + 1)
                    rows, width = (P, 512) if q < 6 else (LASTK, 256)
                    act.copy(expo_t[0:rows, q % 4, 0, 0:width], bank(k_bank)[0:rows, 0:width]
                             ).then_inc(exp_t_high, 1)

                def units(i, last):
                    for k in range(8):
                        batch = turned_batch(i, k, last)
                        groups = iter(context_groups(k, last))

                        def turned_in(count):
                            for _ in range(count):
                                kind, q, k_bank, _ = next(groups)
                                if kind == "keys":
                                    keys_in(batch, 1 if k < 4 else 0, q, k_bank)
                                else:
                                    exp_t_in(i, k, q, k_bank)

                        if k < 6:
                            unit_queries(i, k + 2)
                        elif not last:
                            unit_queries(i + 1, k - 6)
                        turned_in(1)
                        if k < 7:
                            exps(i, k + 1, 1)
                        elif not last:
                            exps(i + 1, 0, 1)
                        turned_in(3 if batch is None else 7)
                        after = (i, k + 1) if k < 7 else None if last else (i + 1, 0)
                        if after is not None:
                            exp_t_in(*after, 0, TURN_BANKS[0])
                        if k < 6:
                            exps(i, k + 2, 0)
                        elif not last:
                            exps(i + 1, k - 6, 0)
                        act.wait_ge(context_sum, 8 * i + k + 1)
                        act.copy(out_c[:, :], bank(6)[:, 0:256]).then_inc(context_in, 1)
                        if after is not None:
                            for q in (1, 2):
                                exp_t_in(*after, q, TURN_BANKS[q])

                act.sem_inc(exp_done, 3)
                act.wait_ge(q_lat_in, XH + 1)
                for k in range(2):
                    unit_queries(0, k)
                for part in range(4):
                    keys_in(0, 0, part, TURN_BANKS[part % 3])
                for unit, r in ((0, 0), (0, 1), (1, 0)):
                    exps(0, unit, r)
                for q in range(3):
                    exp_t_in(0, 0, q, TURN_BANKS[q])
                with act.Fori(0, B // 2 - 1) as i:
                    units(i, False)
                units(B // 2 - 1, True)

                def head_context(h, buffer):
                    act.copy(by_batch(ctx_pair[:, buffer, 0, :]),
                             big[:, :].rearrange("p (b c) -> p b c", b=B)[:, :, bass.ds(h * S, S)]
                             ).then_inc(ctx_high, 1)

                def latents_in(h, buffer):
                    if isinstance(h, int) and h == 0:
                        act.wait_ge(chunk_used, D3B + 1)
                    else:
                        act.wait_ge(lat_done, h)
                    act.copy(lat_pair[:, buffer, 0, :], bank(buffer)).then_inc(lat_high, 1)

                act.wait_ge(context_done, 4 * B + 1)
                head_context(0, 0)
                head_context(1, 1)
                latents_in(0, 0)
                head_context(2, 0)
                latents_in(1, 1)
                head_context(3, 1)
                with act.Fori(1, XH // 2 - 1) as i:
                    for j in range(2):
                        latents_in(2 * i + j, j)
                        head_context(2 * i + j + 2, j)
                for j in range(2):
                    latents_in(XH - 2 + j, j)

            if runs("E"):
                layer_norm(4)
                act.activation(exp_a[:, :], small_at("a_log"), ACT.Exp).then_inc(a_exp, 1)
                act.wait_ge(conv_pad, 1)

                def conv_input(m, earlier):
                    if earlier is not None:
                        act.wait_ge(conv_step, earlier)
                    act.copy(conv_in[:, m, :, CONV_K - 1:], by_batch(bank(m))).then_inc(xs_copied, 1)

                act.wait_ge(bc_done, 1)
                conv_input(0, None)
                act.wait_ge(chunk_used, EB + 1)
                conv_input(1, None)
                act.wait_ge(dt_step, 3)
                act.activation(dt_s[:, 3, :], dt_s[:, 2, :], ACT.Exp).then_inc(dt_exp, 1)
                act.wait_ge(dt_exp, 1)
                act.activation(dt_s[:, 4, :], dt_s[:, 3, :], ACT.Ln, bias=1.0).then_inc(dt_exp, 1)
                for m in range(2):
                    act.wait_ge(conv_step, m + 7)
                    act.activation(bc_t[:, m, :], conv_acc[:, m, :], ACT.Silu).then_inc(conv_silu, 1)

                def squares(i):
                    for m in range(2):
                        act.wait_ge(y_step, 8 * i + 3 + m)
                        act.activation(y_sq[:, m, :], y_gated[:, m, :], ACT.Square).then_inc(y_squared, 1)

                def mamba_tiles(i, buffer):
                    n = EB + 1 + 2 * i
                    for m in range(2):
                        act.wait_ge(xs_done, i + 1) if m == 0 else act.wait_ge(chunk_used, n + 1)
                        conv_input(m, 8 * i + m + 7)
                    for g in range(G):
                        act.wait_ge(decay_sum, 4 * i + g + 1)
                        if not (isinstance(i, int) and i == 0):
                            act.wait_ge(mixed, 4 * i + g - 3)
                        act.activation(decay[:, g, :, :].rearrange("p h t -> p (h t)"), bank(6 + g % 2),
                                       ACT.Exp).then_inc(decay_exp, 1)
                    if not (isinstance(i, int) and i < 2):
                        act.wait_ge(y_step, 8 * i - 12)
                    for m in range(2):
                        act.wait_ge(conv_step, 8 * i + m + 15)
                        act.activation(xs_t[:, buffer, m, :], conv_acc[:, m, :], ACT.Silu).then_inc(conv_silu, 1)
                    for m in range(2):
                        act.wait_ge(gate_done, i + 1) if m == 0 else act.wait_ge(chunk_used, n + 2)
                        act.activation(silu_g[:, buffer, m, :], bank(2 + m), ACT.Silu).then_inc(gate_silu, 1)
                    if not (isinstance(i, int) and i == 0):
                        squares(i - 1)

                for i in range(2):
                    mamba_tiles(i, i)
                with act.Fori(1, IT // 4) as i:
                    for j in range(2):
                        mamba_tiles(2 * i + j, j)
                squares(IT // 2 - 1)

                def gated_high(c, j):
                    for kk in range(2):
                        act.copy(gated_pair[:, 2 * (j % 2) + kk, 0, :], big[:, bass.ds(T * (2 * c + kk), T)]
                                 ).then_inc(gh_high, 1)

                act.wait_ge(y_step, 4 * IT)
                gated_high(0, 0)
                gated_high(1, 1)
                act.wait_ge(norm_sum, 1)
                act.activation(rstd[:, :], bank(3), ACT.Ln, bias=eps[:, 0:1], scale=H / INNER).then_inc(norm_log, 1)
                act.wait_ge(norm_log, 1)
                act.activation(rstd[:, :], rstd[:, :], ACT.Exp, scale=-0.5).then_inc(norm_inv, 1)
                with act.Fori(1, 4) as i:
                    for j in range(2):
                        act.wait_ge(chunk_used, E_OUT + 2 * i + j - 1)
                        gated_high(2 * i + j, j)

            if runs("F"):
                layer_norm(5)
                act.wait_ge(chunk_used, FB + 1)
                act.copy(lora_h[:, :], bank(7)).then_inc(lora_in, 1)
                gate_exps(2, 3)

                def expert_f(e):
                    expert = 2 * NE + e
                    act.wait_ge(mid_step, 4 * expert)
                    for m in range(2):
                        act.wait_ge(first, e + 1) if m == 0 else act.wait_ge(chunk_used, f_chunks(e)[0] + 1)
                        act.activation(act_o[:, m, :], bank(m), ACT.Silu).then_inc(silu_done, 1)

                expert_f(0)
                spread_copies(SPREAD_0[2], NE, lambda e: 5 + e % 2, lambda e: wide_w[:, e, :])
                with act.Fori(1, NE) as e:
                    expert_f(e)

        @block.vector
        def _(dve):
            def low(out, value, high):
                return dve.tensor_tensor(out, value, high.bitcast(F32), ALU.subtract)

            def layer_norm(k):
                dve.wait_ge(ln_mean, k + 1)
                for f in range(FT):
                    dve.tensor_tensor(xc[:, f, :], x[:, f, :], bank(LN_BANKS[k][0]), ALU.subtract).then_inc(ln_centred, 1)
                dve.wait_ge(ln_rstd, k + 1)
                for f in range(FT + 1):
                    if f < FT:
                        dve.tensor_tensor(xc[:, f, :], xc[:, f, :], rstd[:, :], ALU.mult).then_inc(ln_normal, 1)
                    if f:
                        dve.wait_ge(ln_high, 4 * k + f)
                        low(xn[:, 1, f - 1, :], xc[:, f - 1, :], xn[:, 0, f - 1, :]).then_inc(ln_low, 1)

            def add_tile(m, k):
                dve.tensor_tensor(x[:, m, :], x[:, m, :], bank(k), ALU.add).then_inc(x_ready, 1)

            def add_projection(stage, n0):
                for c in range(2):
                    dve.wait_ge(out_done, 2 * stage + c + 1)
                    add_tile(2 * c, 2 * c)
                    dve.wait_ge(chunk_used, n0 + c + 1)
                    add_tile(2 * c + 1, 2 * c + 1)

            dve.memset(zero_b[:, :], 0.0).then_inc(setup, 1)
            dve.memset(eps[:, :], 1e-5).then_inc(setup, 1)
            dve.wait_ge(smalls_in, 32)
            dve.tensor_copy(ident_b[:, :], constant("ident")).then_inc(setup, 1)
            for n, name in enumerate(("causal", "batch")):
                dve.tensor_copy(mask_b[:, n, :, :], constant(name).unsqueeze(1).broadcast_to([P, G, P])).then_inc(setup, 1)
            dve.wait_ge(inputs_in, 32)
            dve.tensor_copy(first_pair[:, 0, :], first_raw[:, :]).then_inc(setup, 1)
            dve.wait_ge(setup, 6)
            low(first_pair[:, 1, :], first_raw[:, :], first_pair[:, 0, :]).then_inc(setup, 1)

            for n, name in enumerate(("c_gate", "f_gate")):
                w = small_at(name).rearrange("p (n k e) -> p n k e", k=FT, e=NE)
                high, rest = (gate_w[:, part, 2 * n:2 * n + (2, 1)[n], :, :] for part in range(2))
                dve.tensor_copy(high, w).then_inc(setup, 1)
                dve.wait_ge(setup, 8 + 2 * n)
                low(rest, w, high).then_inc(setup, 1)

            def rope(u, side, raw, arrived, out):
                at = 6 * (u - FT) + 3 * side
                dve.wait_ge(qk_turned, 2 * (u - FT) + side + 1)
                dve.tensor_tensor(by_batch(turned[:, side, :]), by_batch(bank((2, 0)[side])),
                                  over_batches(constant("sin_b")), ALU.mult).then_inc(rope_steps, 1)
                dve.wait_ge(arrived, u + 1)
                dve.tensor_tensor(by_batch(out), by_batch(raw[:, :]), over_batches(constant("cos_b")),
                                  ALU.mult).then_inc(rope_steps, 1)
                dve.wait_ge(rope_steps, at + 2)
                dve.tensor_tensor(out, out, turned[:, side, :], ALU.add).then_inc(rope_steps, 1)

            def queries_and_keys(f):
                dve.wait_ge(chunk_used, BB + 4 + 2 * f)
                dve.tensor_copy(k_raw[:, :], bank(1)).then_inc(k_in, 1)
                rope(FT + f, 0, q_raw, q_in, q_t[:, :])
                rope(FT + f, 1, k_raw, k_in, k_t[:, 0, :])

            def attention_tile(u, f, ahead):
                def row_max(h):
                    dve.wait_ge(scores, HPT * u + h + 1)
                    dve.tensor_reduce(neg_max[:, h, :], bank(3 + h).rearrange("p (g k) -> p g k", g=G), AX_X,
                                      ALU.max, negate=True).then_inc(maxed, 1)

                def normalise(h):
                    dve.wait_ge(expd, G * (HPT * u + h) + G)
                    dve.reciprocal(row_inv[:, h, :], row_sum[:, h, :]).then_inc(row_inverted, 1)
                    dve.wait_ge(row_inverted, HPT * u + h + 1)
                    dve.tensor_tensor(prob[:, h, :, :], prob[:, h, :, :],
                                      row_inv[:, h, :].unsqueeze(2).broadcast_to([P, G, P]), ALU.mult
                                      ).then_inc(normal, 1)

                row_max(0)
                row_max(1)
                row_max(2)
                normalise(0)
                row_max(3)
                normalise(1)
                normalise(2)
                normalise(3)
                if ahead is not None:
                    ahead()
                dve.wait_ge(heads_high, u + 1)
                tile = bass.ds(f, 1)
                dve.tensor_tensor(heads_out[:, 1, tile, :].rearrange("p a t -> p (a t)"), bank(7),
                                  heads_out[:, 0, tile, :].rearrange("p a t -> p (a t)").bitcast(F32),
                                  ALU.subtract).then_inc(heads_low, 1)
                dve.wait_ge(heads_low, u + 1)
                dve.sem_inc(heads_read, 1)

            dve.sem_inc(heads_read, 1)
            layer_norm(0)
            for m in range(FT):
                dve.wait_ge(keys_done, m + 1) if m < FT - 1 else dve.wait_ge(chunk_used, 1)
                dve.tensor_copy(k_t[:, m, :], bank(4 + m)).then_inc(k_in, 1)
            for u in range(FT):
                attention_tile(u, u, None)
            add_projection(0, A_OUT)
            if runs("B"):
                layer_norm(1)
                queries_and_keys(0)
                with dve.Fori(0, FT - 1) as f:
                    attention_tile(FT + f, f, lambda: queries_and_keys(f + 1))
                attention_tile(2 * FT - 1, FT - 1, None)
                add_projection(1, B_OUT)

            class Steps:
                at = 0

                def __call__(self, ins):
                    ins.then_inc(gate_step, 1)
                    self.at += 1
                    dve.wait_ge(gate_step, self.at)

            step = Steps()

            def bcast(ap):
                return ap.broadcast_to([P, G, NE])

            def take_top(values, count, weights_in):
                theirs = values.unsqueeze(2).broadcast_to([P, G, NE, NE])
                own = values.unsqueeze(3).broadcast_to([P, G, NE, NE])
                lower = constant("lower").rearrange("p (e j) -> p e j", e=NE)
                step(dve.tensor_tensor(pairs_s[:, 0, :, :, :], theirs, own, ALU.is_gt))
                step(dve.tensor_tensor(pairs_s[:, 1, :, :, :], theirs, own, ALU.is_equal))
                step(dve.tensor_tensor(pairs_s[:, 1, :, :, :], pairs_s[:, 1, :, :, :],
                                       lower.unsqueeze(1).broadcast_to([P, G, NE, NE]), ALU.mult))
                step(dve.tensor_tensor(pairs_s[:, 0, :, :, :], pairs_s[:, 0, :, :, :], pairs_s[:, 1, :, :, :], ALU.add))
                step(dve.tensor_reduce(gate_s[:, 3, :, :], pairs_s[:, 0, :, :, :], AX_X, ALU.add))
                step(dve.scalar_tensor_tensor(out=gate_s[:, 4, :, :], in0=gate_s[:, 3, :, :], scalar=count - 0.5,
                                              in1=weights_in, op0=ALU.is_lt, op1=ALU.mult))

            def gate_c(p):
                first_b, _ = SMALLS["c_gate_bias"]
                bias = small[:, first_b + NE * p:first_b + NE * (p + 1)]
                dve.wait_ge(gated, p + 1)
                step(dve.tensor_tensor(gate_s[:, 0, :, :], bank(4)[:, 0:G * NE].rearrange("p (g e) -> p g e", e=NE),
                                       bias.unsqueeze(1).broadcast_to([P, G, NE]), ALU.add))
                step(dve.tensor_reduce(gate_col[:, 0, :, :], gate_s[:, 0, :, :], AX_X, ALU.max))
                step(dve.tensor_tensor(gate_s[:, 1, :, :], gate_s[:, 0, :, :], bcast(gate_col[:, 0, :, :]), ALU.subtract))
                dve.wait_ge(gate_exp, p + 1)
                take_top(gate_s[:, 0, :, :], GATED, gate_s[:, 2, :, :])
                step(dve.tensor_reduce(gate_col[:, 1, :, :], gate_s[:, 4, :, :], AX_X, ALU.add))
                step(dve.reciprocal(gate_col[:, 2, :, :], gate_col[:, 1, :, :]))
                step(dve.tensor_tensor(gate_s[:, 5, :, 0:GATED], gate_s[:, 4, :, 0:GATED],
                                       gate_col[:, 2, :, :].broadcast_to([P, G, GATED]), ALU.mult))

            def gate_f():
                dve.wait_ge(gated, 3)
                step(dve.tensor_copy(gate_s[:, 0, :, :], bank(4)[:, 0:G * NE].rearrange("p (g e) -> p g e", e=NE)))
                step(dve.tensor_reduce(gate_col[:, 0, :, :], gate_s[:, 0, :, :], AX_X, ALU.max))
                step(dve.tensor_tensor(gate_s[:, 1, :, :], gate_s[:, 0, :, :], bcast(gate_col[:, 0, :, :]), ALU.subtract))
                dve.wait_ge(gate_exp, 3)
                step(dve.tensor_reduce(gate_col[:, 1, :, :], gate_s[:, 2, :, :], AX_X, ALU.add))
                step(dve.reciprocal(gate_col[:, 2, :, :], gate_col[:, 1, :, :]))
                step(dve.tensor_tensor(gate_s[:, 6, :, :], gate_s[:, 2, :, :], bcast(gate_col[:, 2, :, :]), ALU.mult))
                take_top(gate_s[:, 6, :, :], 2, gate_s[:, 6, :, :])
                step(dve.tensor_reduce(gate_col[:, 1, :, :], gate_s[:, 4, :, :], AX_X, ALU.add))
                step(dve.tensor_scalar(gate_col[:, 2, :, :], gate_col[:, 1, :, :], 1e-9, None, ALU.max))
                step(dve.reciprocal(gate_col[:, 3, :, :], gate_col[:, 2, :, :]))
                step(dve.tensor_tensor(gate_s[:, 5, :, :], gate_s[:, 4, :, :], bcast(gate_col[:, 3, :, :]), ALU.mult))

            def rows_copy(p):
                dve.wait_ge(rows_turned, p + 1)
                dve.tensor_copy(w_rows[:, :], bank(5)[0:NE, :]).then_inc(rows_in, 1)

            def hidden(expert):
                for m in range(2):
                    dve.wait_ge(hid_in, 2 * expert + m + 1)
                    dve.tensor_copy(hid_pair[:, 0, m, :], hid[:, m, :]).then_inc(hid_high, 1)
                for m in range(2):
                    dve.wait_ge(hid_high, 2 * expert + m + 1)
                    low(hid_pair[:, 1, m, :], hid[:, m, :], hid_pair[:, 0, m, :]).then_inc(hid_low, 1)

            def middle(expert, e, other, down_before=None):
                wide_e = wide_w[:, bass.ds(e, 1), :].rearrange("p a t -> p (a t)")
                if not (isinstance(expert, int) and expert == 0):
                    dve.wait_ge(mid_low, 2 * expert)
                for m in range(2):
                    dve.wait_ge(silu_done, 2 * expert + m + 1)
                    dve.tensor_tensor(mid[:, m, :], act_o[:, m, :], other(m), ALU.mult).then_inc(mid_step, 1)
                for m in range(2):
                    dve.wait_ge(mid_step, 4 * expert + m + 1)
                    dve.tensor_tensor(mid[:, m, :], mid[:, m, :], wide_e, ALU.mult).then_inc(mid_step, 1)
                if down_before is not None:
                    dve.wait_ge(chunk_used, down_before + 1)
                for m in range(2):
                    dve.wait_ge(mid_step, 4 * expert + m + 3)
                    dve.tensor_copy(mid_pair[:, 0, m, :], mid[:, m, :]).then_inc(mid_high, 1)
                for m in range(2):
                    dve.wait_ge(mid_high, 2 * expert + m + 1)
                    low(mid_pair[:, 1, m, :], mid[:, m, :], mid_pair[:, 0, m, :]).then_inc(mid_low, 1)

            def sum_ready(p, m, last_chunk):
                if p < 2 and m % 2 or m == FT - 1:
                    dve.wait_ge(chunk_used, last_chunk + (m + 1) // FT)
                else:
                    dve.wait_ge(mixed_out, 2 * p + (m // 2 if p < 2 else m) + 1)

            if runs("C"):
                layer_norm(2)
                dve.memset(gate_s[:, 5, :, GATED:NE], 1.0)
                dve.memset(wide_w[:, GATED:NE, :], 1.0)
                for p in range(2):
                    hidden(NE * p)
                    gate_c(p)
                    rows_copy(p)
                    dve.wait_ge(spread_in, SPREAD_0[p] + GATED)
                    middle(NE * p, 0, lambda m: hid[:, m, :])
                    with dve.Fori(1, NE) as e:
                        hidden(NE * p + e)
                        middle(NE * p + e, e, lambda m: hid[:, m, :])
                    last_chunk = CB + C_CHUNKS * (p + 1) - 1
                    for m in range(FT):
                        sum_ready(p, m, last_chunk)
                        dve.tensor_tensor(sq[:, m, :], xc[:, m, :], bank(4 + m), ALU.add).then_inc(second_in, 1)
                    for m in range(FT):
                        dve.wait_ge(second_in, 3 * FT * p + m + 1)
                        if p == 0:
                            dve.tensor_copy(xn[:, 0, m, :], sq[:, m, :]).then_inc(second_in, 1)
                        else:
                            dve.tensor_tensor(x[:, m, :], x[:, m, :], sq[:, m, :], ALU.add).then_inc(x_ready, 1)
                    for m in range(FT if p == 0 else 0):
                        dve.wait_ge(second_in, FT + m + 1)
                        low(xn[:, 1, m, :], sq[:, m, :], xn[:, 0, m, :]).then_inc(second_in, 1)

            if runs("D"):
                layer_norm(3)
                cos_q = constant("cos_q").rearrange("p (k s) -> p k s", k=QT)
                sin_q = constant("sin_q").rearrange("p (k s) -> p k s", k=QT)

                def query_head(h, buffer):
                    dve.wait_ge(hk_high, h + 1)
                    low(hk_pair[:, 1, :], bank(0), hk_pair[:, 0, :]).then_inc(hk_low, 1)
                    dve.wait_ge(absorb_high, h + 1)
                    low(absorb_pair[:, buffer, 1, :], bank(7)[:, 0:QT * P], absorb_pair[:, buffer, 0, :]
                        ).then_inc(absorb_low, 1)
                    for k in range(QT):
                        dve.wait_ge(q_big, 2 * h + k + 1) if k < 2 else dve.wait_ge(chunk_used, DB + 2 * h + 1)
                        dve.tensor_tensor(by_batch(by_cos[:, k, :]), by_batch(bank(1 + k)),
                                          over_batches(cos_q[:, k, :]), ALU.mult).then_inc(turn_step, 1)
                    for k in range(QT):
                        dve.wait_ge(q_turned, 2 * h + k + 1) if k < 2 else dve.wait_ge(chunk_used, DB + 2 * h + 2)
                        dve.tensor_tensor(by_batch(by_sin[:, k % 2, :]), by_batch(bank(1 + QT + k)),
                                          over_batches(sin_q[:, k, :]), ALU.mult).then_inc(turn_step, 1)
                        dve.wait_ge(turn_step, 3 * QT * h + QT + 2 * k + 1)
                        dve.tensor_tensor(by_cos[:, k, :], by_cos[:, k, :], by_sin[:, k % 2, :], ALU.add
                                          ).then_inc(turn_step, 1)
                    for k in range(QT):
                        dve.wait_ge(rope_high, QT * h + k + 1)
                        low(turned_pair[:, buffer, 1, k, :], by_cos[:, k, :], turned_pair[:, buffer, 0, k, :]
                            ).then_inc(rope_low, 1)

                with dve.Fori(0, XH // 2) as i:
                    for j in range(2):
                        query_head(2 * i + j, j)

                def keys_in(b, buffer, part, k_bank):
                    dve.wait_ge(keys_high, 5 * b + part + (1 if part < 3 else 2))
                    at, width = 512 * part, min(512, CTX - 512 * part)
                    ins = low(kv_t[:, buffer, 1, at:at + width], bank(k_bank)[:, 0:width],
                              kv_t[:, buffer, 0, at:at + width])
                    if part == 3:
                        ins = low(kv_t[:, buffer, 1, CTX:CTX + 1], bank(k_bank)[:, width - 1:width],
                                  kv_t[:, buffer, 0, CTX:CTX + 1])
                    ins.then_inc(keys_low, 1)

                def unit_queries(i, k):
                    unit = 8 * i + k
                    dve.wait_ge(qu_high, unit + 1)
                    low(q_pair[:, k % 2, 1, :], big[:, bass.ds(256 * unit, 256)], q_pair[:, k % 2, 0, :]
                        ).then_inc(qu_low, 1)

                def half_max(i, k, r, half):
                    row = 2 * (8 * i + k) + r
                    dve.wait_ge(scored, 4 * row + 2 * half + 2)
                    dve.tensor_reduce(part_max[:, r, half:half + 1], psum[:, 2 * half:2 * half + 2, 0:402],
                                      mybir.AxisListType.XY, ALU.max).then_inc(max_part, 1)

                def row_max(i, k, r):
                    half_max(i, k, r, 1)
                    dve.wait_ge(max_part, 2 * (2 * (8 * i + k) + r) + 2)
                    dve.tensor_reduce(neg_m[:, r:r + 1], part_max[:, r, :], AX_X, ALU.max, negate=True
                                      ).then_inc(max_done, 1)

                def row_scales(i, k):
                    unit = 8 * i + k
                    dve.wait_ge(exp_done, 6 * unit + 9)
                    dve.tensor_reduce(sums[:, 0, :], part_sum[:, k % 2, :, :], AX_X, ALU.add).then_inc(summed, 1)
                    dve.wait_ge(summed, unit + 1)
                    dve.reciprocal(sums[:, 1, :], sums[:, 0, :]).then_inc(inverted, 1)
                    dve.wait_ge(inverted, unit + 1)
                    for r in range(2):
                        dve.tensor_scalar(diag[:, k % 2, r, :], constant("ident"), sums[:, 1, r:r + 1], float(H),
                                          ALU.mult, ALU.mult).then_inc(diagonal, 1)

                def exp_t_in(i, k, q, k_bank):
                    dve.wait_ge(exp_t_high, 7 * (8 * i + k) + q + 1)
                    rows, width = (P, 512) if q < 6 else (LASTK, 256)
                    low(expo_t[0:rows, q % 4, 1, 0:width], bank(k_bank)[0:rows, 0:width],
                        expo_t[0:rows, q % 4, 0, 0:width]).then_inc(exp_t_low, 1)

                def units(i, last):
                    for k in range(8):
                        unit, batch = 8 * i + k, turned_batch(i, k, last)
                        groups = iter(context_groups(k, last))

                        def turned_in(count):
                            for _ in range(count):
                                kind, q, k_bank, _ = next(groups)
                                if kind == "keys":
                                    keys_in(batch, 1 if k < 4 else 0, q, k_bank)
                                else:
                                    exp_t_in(i, k, q, k_bank)

                        second_row = (i, k + 1) if k < 7 else None if last else (i + 1, 0)
                        first_row = (i, k + 2) if k < 6 else None if last else (i + 1, k - 6)
                        exp_t_in(i, k, 2, TURN_BANKS[2])
                        if second_row is not None:
                            half_max(*second_row, 1, 0)
                            row_max(*second_row, 1)
                        turned_in(1)
                        if first_row is not None:
                            unit_queries(*first_row)
                        turned_in(3 if batch is None else 7)
                        if first_row is not None:
                            half_max(*first_row, 0, 0)
                            row_max(*first_row, 0)
                        if second_row is not None:
                            exp_t_in(*second_row, 0, TURN_BANKS[0])
                            row_scales(*second_row)
                        dve.wait_ge(context_in, unit + 1)
                        dve.tensor_tensor(big[:, bass.ds(256 * unit, 256)], out_c[:, :], bank(6)[:, 256:512],
                                          ALU.mult).then_inc(context_done, 1)
                        if second_row is not None:
                            exp_t_in(*second_row, 1, TURN_BANKS[1])

                dve.sem_inc(context_done, 1)
                for k in range(2):
                    unit_queries(0, k)
                for part in range(4):
                    keys_in(0, 0, part, TURN_BANKS[part % 3])
                for unit, r in ((0, 0), (0, 1), (1, 0)):
                    half_max(0, unit, r, 0)
                    row_max(0, unit, r)
                    if r == 1:
                        row_scales(0, 0)
                for q in range(2):
                    exp_t_in(0, 0, q, TURN_BANKS[q])
                with dve.Fori(0, B // 2 - 1) as i:
                    units(i, False)
                units(B // 2 - 1, True)

                def head_context(h, buffer):
                    dve.wait_ge(ctx_high, h + 1)
                    dve.tensor_tensor(by_batch(ctx_pair[:, buffer, 1, :]),
                                      big[:, :].rearrange("p (b c) -> p b c", b=B)[:, :, bass.ds(h * S, S)],
                                      by_batch(ctx_pair[:, buffer, 0, :]).bitcast(F32), ALU.subtract
                                      ).then_inc(ctx_low, 1)

                def latents_in(h, buffer):
                    dve.wait_ge(lat_high, h + 1)
                    low(lat_pair[:, buffer, 1, :], bank(buffer), lat_pair[:, buffer, 0, :]).then_inc(lat_low, 1)

                head_context(0, 0)
                head_context(1, 1)
                with dve.Fori(0, XH // 2 - 1) as i:
                    for j in range(2):
                        latents_in(2 * i + j, j)
                        head_context(2 * i + j + 2, j)
                for j in range(2):
                    latents_in(XH - 2 + j, j)
                for m in range(FT):
                    dve.wait_ge(d_out, m + 1) if m < FT - 1 else dve.wait_ge(chunk_used, D3B + XH + 1)
                    add_tile(m, 4 + m)

            if runs("E"):
                layer_norm(4)
                upto = constant("upto")
                conv_w, conv_b = small_at("conv_w"), small_at("conv_b")
                dve.memset(sq_sum[:, :], 0.0)
                dve.memset(conv_in[:, :, :, 0:CONV_K - 1], 0.0).then_inc(conv_pad, 1)

                def convolve(v, tile):
                    accs = [by_batch(conv_acc[:, m, :]) for m in range(2)]
                    for m in range(2):
                        dve.wait_ge(xs_copied, 2 * v + m + 1)
                        if not (isinstance(v, int) and v == 0):
                            dve.wait_ge(conv_silu, 2 * v + m - 1)
                        dve.tensor_scalar(accs[m], conv_in[:, m, :, 0:S], conv_w[:, bass.ds(CONV_K * (tile + m), 1)],
                                          conv_b[:, bass.ds(tile + m, 1)], ALU.mult, ALU.add).then_inc(conv_step, 1)
                    for t in range(1, CONV_K):
                        for m in range(2):
                            dve.wait_ge(conv_step, 8 * v + 2 * t + m - 1)
                            dve.scalar_tensor_tensor(out=accs[m], in0=conv_in[:, m, :, t:t + S],
                                                     scalar=conv_w[:, bass.ds(CONV_K * (tile + m) + t, 1)],
                                                     in1=accs[m], op0=ALU.mult, op1=ALU.add).then_inc(conv_step, 1)

                def heads(ap):
                    return ap.rearrange("p (g h) -> p g h", h=MH)

                dt, a = heads(dt_s[:, 0, :]), heads(dt_s[:, 1, :])
                dve.wait_ge(dt_done, 1)
                dve.tensor_tensor(dt, heads(bank(2)[:, 0:G * MH]), small_at("dt_bias").unsqueeze(1).broadcast_to([P, G, MH]),
                                  ALU.add).then_inc(dt_step, 1)
                dve.wait_ge(dt_step, 1)
                dve.tensor_scalar(dt_s[:, 1, :], dt_s[:, 0, :], 0.0, None, ALU.max).then_inc(dt_step, 1)
                dve.scalar_tensor_tensor(out=dt_s[:, 2, :], in0=dt_s[:, 0, :], scalar=-1.0, in1=dt_s[:, 0, :],
                                         op0=ALU.mult, op1=ALU.min).then_inc(dt_step, 1)
                convolve(0, IT)
                dve.wait_ge(dt_exp, 2)
                dve.wait_ge(dt_step, 3)
                dve.tensor_tensor(dt_s[:, 0, :], dt_s[:, 1, :], dt_s[:, 4, :], ALU.add).then_inc(dt_step, 1)
                dve.wait_ge(dt_step, 4)
                dve.wait_ge(a_exp, 1)
                dve.scalar_tensor_tensor(out=a, in0=dt, scalar=-1.0, in1=exp_a[:, :].unsqueeze(1).broadcast_to([P, G, MH]),
                                         op0=ALU.mult, op1=ALU.mult).then_inc(dt_step, 1)
                dve.wait_ge(dt_step, 5)
                dve.tensor_copy(a_pair[:, 0, :], dt_s[:, 1, :]).then_inc(dt_step, 1)
                dve.tensor_copy(after_r[:, :], constant("after"))
                dve.wait_ge(dt_step, 6)
                low(a_pair[:, 1, :], dt_s[:, 1, :], a_pair[:, 0, :]).then_inc(dt_step, 1)
                dve.wait_ge(g_done, 1)
                dve.tensor_tensor(g_mask[:, :, :], bank(3).rearrange("p (g t) -> p g t", g=G),
                                  upto.unsqueeze(1).broadcast_to([P, G, P]), ALU.mult).then_inc(g_masked, 1)

                def outputs_a(i, buffer):
                    for m in range(2):
                        dve.wait_ge(y_done, 2 * i + m + 1)
                        dve.scalar_tensor_tensor(out=y_sum[:, m, :], in0=xs_t[:, buffer, m, :],
                                                 scalar=small_at("skip")[:, bass.ds(2 * i + m, 1)], in1=bank(4 + m),
                                                 op0=ALU.mult, op1=ALU.add).then_inc(y_step, 1)
                    for m in range(2):
                        dve.wait_ge(y_step, 8 * i + m + 1)
                        dve.wait_ge(gate_silu, 2 * i + m + 1)
                        dve.tensor_tensor(y_gated[:, m, :], y_sum[:, m, :], silu_g[:, buffer, m, :], ALU.mult
                                          ).then_inc(y_step, 1)

                def outputs_b(i):
                    for m in range(2):
                        dve.wait_ge(y_step, 8 * i + m + 3)
                        dve.tensor_scalar(big[:, bass.ds(T * (2 * i + m), T)], y_gated[:, m, :],
                                          small_at("norm_w")[:, bass.ds(2 * i + m, 1)], None, ALU.mult
                                          ).then_inc(y_step, 1)
                    for m in range(2):
                        dve.wait_ge(y_squared, 2 * i + m + 1)
                        dve.wait_ge(y_step, 8 * i + m + 6)
                        dve.tensor_tensor(sq_sum[:, :], sq_sum[:, :], y_sq[:, m, :], ALU.add).then_inc(y_step, 1)

                def mamba_tiles(i, buffer):
                    for g in range(G):
                        dve.tensor_tensor(decay_in[:, 0, g, :, :], upto.unsqueeze(1).broadcast_to([P, 4, P]),
                                          heads(a_pair[:, 0, :].bitcast(F32))[:, g, bass.ds(4 * i, 4)].unsqueeze(2)
                                          .broadcast_to([P, 4, P]), ALU.mult
                                          ).then_inc(decay_ready, 1)
                    convolve(i + 1, 2 * i)
                    if not (isinstance(i, int) and i == 0):
                        outputs_a(i - 1, 1 - buffer)
                    for g in range(G):
                        dve.wait_ge(decay_exp, 4 * i + g + 1)
                        dve.tensor_tensor(mix[:, g, :, :], decay[:, g, :, :],
                                          g_mask[:, g, :].unsqueeze(1).broadcast_to([P, 4, P]), ALU.mult
                                          ).then_inc(mixed, 1)
                    dve.wait_ge(xs_turned, i + 1)
                    for m in range(2):
                        dve.tensor_tensor(xdt[:, :, 2 * m:2 * m + 2, :],
                                          bank(4 + m).rearrange("p (g h d) -> p g h d", g=G, h=2),
                                          dt[:, :, bass.ds(4 * i + 2 * m, 2)].unsqueeze(3).broadcast_to([P, G, 2, MP]),
                                          ALU.mult).then_inc(xdt_ready, 1)
                    if not (isinstance(i, int) and i == 0):
                        outputs_b(i - 1)

                for i in range(2):
                    mamba_tiles(i, i)
                with dve.Fori(1, IT // 4) as i:
                    for j in range(2):
                        mamba_tiles(2 * i + j, j)
                outputs_a(IT // 2 - 1, 1)
                outputs_b(IT // 2 - 1)

                def gated_low(c, j):
                    for kk in range(2):
                        dve.wait_ge(gh_high, 2 * c + kk + 1)
                        buffer = 2 * (j % 2) + kk
                        low(gated_pair[:, buffer, 1, :], big[:, bass.ds(T * (2 * c + kk), T)],
                            gated_pair[:, buffer, 0, :]).then_inc(gh_low, 1)

                with dve.Fori(0, 4) as i:
                    for j in range(2):
                        gated_low(2 * i + j, j)
                dve.wait_ge(norm_inv, 1)
                for m in range(FT):
                    dve.wait_ge(e_out, m + 1) if m < FT - 1 else dve.wait_ge(chunk_used, E_OUT + 8)
                    if m >= 2:
                        dve.wait_ge(x_ready, 4 * 4 + m - 1)
                    dve.tensor_tensor(y_sum[:, m % 2, :], bank(4 + m), rstd[:, :], ALU.mult).then_inc(e_scaled, 1)
                    dve.wait_ge(e_scaled, m + 1)
                    dve.tensor_tensor(x[:, m, :], x[:, m, :], y_sum[:, m % 2, :], ALU.add).then_inc(x_ready, 1)

            if runs("F"):
                layer_norm(5)
                gate_f()
                rows_copy(2)
                dve.wait_ge(lora_in, 1)
                dve.wait_ge(lora_done, 1)
                dve.tensor_tensor(lora_w[:, :], lora_h[:, :], bank(4), ALU.mult).then_inc(lora_in, 1)
                dve.wait_ge(lora_in, 2)
                dve.tensor_copy(lora_pair[:, 0, :], lora_w[:, :]).then_inc(lora_in, 1)
                dve.wait_ge(lora_in, 3)
                low(lora_pair[:, 1, :], lora_w[:, :], lora_pair[:, 0, :]).then_inc(lora_in, 1)

                def expert_f(e):
                    if not isinstance(e, int):
                        dve.wait_ge(second, 2 * NE + e + 1)
                    dve.wait_ge(chunk_used, f_chunks(e)[1] + 1)
                    middle(2 * NE + e, e, lambda m: bank(2 + m),
                           None if isinstance(e, int) else f_chunks(e)[1] + 1)

                dve.wait_ge(spread_in, SPREAD_0[2] + NE)
                expert_f(0)
                with dve.Fori(1, NE) as e:
                    expert_f(e)
                for m in range(FT):
                    sum_ready(2, m, FB + 25)
                    add_tile(m, 4 + m)


STAGES = ("A", "B", "C", "D", "E", "F")
LAST_STAGE = "F"


def kernel(**inputs):
    import concourse.bacc as bacc
    from concourse.bass_utils import run_bass_kernel_spmd

    nc = bacc.Bacc("TRN2", target_bir_lowering=False, num_devices=1)
    arrays = lay_out({name: np.asarray(a) for name, a in inputs.items()})
    order = ("x", "ctx_first", "ctx", "weights", "small", "constants", "rope_k")
    args = [nc.dram_tensor(f"in_{name}", arrays[name].shape, F32, kind="ExternalInput").ap() for name in order]
    out = nc.dram_tensor("out", (P, FT, T), F32, kind="ExternalOutput").ap()
    perceiver_stack(nc, *args, out)
    r = run_bass_kernel_spmd(nc, [{f"in_{name}": arrays[name] for name in order}], core_ids=[0])
    return np.ascontiguousarray(r.results[0]["out"].transpose(2, 1, 0).reshape(B, S, H))
```
